# Optimizing a Trainium2 kernel written in Bass

```python
import numpy as np
import jax
import jax.numpy as jnp

def _softmax(x, axis=-1):
    return jax.nn.softmax(x, axis=axis)

def _gelu(x):
    return jax.nn.gelu(x, approximate=True)

def _silu(x):
    return jax.nn.silu(x)

def _sigmoid(x):
    return jax.nn.sigmoid(x)

def _layernorm(x, axis=-1, eps=1e-05):
    m = jnp.mean(x, axis=axis, keepdims=True)
    v = jnp.var(x, axis=axis, keepdims=True)
    return (x - m) / jnp.sqrt(v + eps)

def _scatter_add(tgt, idx, src, axis=0):
    return tgt.at[idx].add(src)

def _segment_sum(src, seg, n):
    return jax.ops.segment_sum(src, seg, n)
kernel_name = 'mk_flamingo_gated_d1_seqx_r4_f23f47'

def setup_inputs(seed: int=0):
    np.random.seed(seed)
    _w = jnp.asarray

    def _rec_inputs():
        import jax
        import jax.numpy as jnp
        _rk = jax.random.key(seed)
        x = -0.0002928 + 1 * jax.random.normal(jax.random.fold_in(_rk, 1), (32, 112, 256), jnp.float32)
        _lenS = 112 - jax.random.randint(jax.random.fold_in(_rk, 7), (32,), 0, max(1, 112 // 4) + 1, jnp.int32)
        _lenS2 = 375 - jax.random.randint(jax.random.fold_in(_rk, 8), (32,), 0, max(1, 375 // 4) + 1, jnp.int32)
        _ctx_1024P = jax.random.normal(jax.random.fold_in(_rk, 11), (32, 16, 256), jnp.float32)
        _ctx_1024c = jax.random.dirichlet(jax.random.fold_in(_rk, 511), 0.3 * jnp.ones((16,), jnp.float32), (32, 375))
        _ctx_1024t = jnp.einsum('bsk,bkd->bsd', _ctx_1024c, _ctx_1024P)
        _ctx_1024t = _ctx_1024t * jax.lax.rsqrt(jnp.mean(jnp.square(_ctx_1024t)) + 1e-12) * 0.953939
        ctx_1024 = -1.39393e-06 + 0.999914 * (_ctx_1024t + 0.3 * jax.random.normal(jax.random.fold_in(_rk, 611), (32, 375, 256), jnp.float32))
        _g = jax.random.normal(jax.random.fold_in(_rk, 9001), (2, 1), jnp.float32)
        _g = jnp.sign(_g) * jnp.maximum(jnp.abs(_g), 1.0) + (_g == 0) * 1.0
        g_xattn = _g[0]
        g_ffn = _g[1]
        return (x, ctx_1024, g_xattn, g_ffn)
    x, ctx_1024, g_xattn, g_ffn = _rec_inputs()

    def _L0_xattn_setup():
        import jax, jax.numpy as jnp
        import numpy as np
        EMBED_DIM = 256
        NUM_HEADS = 16
        HEAD_DIM = EMBED_DIM // NUM_HEADS
        WINDOW = 128
        B, S_Q, S_K = (2, 512, 512)

        def apply_rope(x):
            Dh = x.shape[-1]
            half = Dh // 2
            pos = jnp.arange(x.shape[2], dtype=jnp.float32)
            inv_freq = 1.0 / 10000.0 ** (jnp.arange(0, half, dtype=jnp.float32) / half)
            ang = pos[:, None] * inv_freq[None, :]
            cos = jnp.cos(ang)[None, None, :, :].astype(x.dtype)
            sin = jnp.sin(ang)[None, None, :, :].astype(x.dtype)
            x1, x2 = (x[..., :half], x[..., half:])
            return jnp.concatenate([x1 * cos - x2 * sin, x1 * sin + x2 * cos], axis=-1)
        key = jax.random.key(seed)
        ks = jax.random.split(key, 11)
        scale = 1.0 / np.sqrt(EMBED_DIM)
        inp = {'query': jax.random.normal(ks[0], (B, S_Q, EMBED_DIM), jnp.float32), 'key': jax.random.normal(ks[1], (B, S_K, EMBED_DIM), jnp.float32), 'value': jax.random.normal(ks[2], (B, S_K, EMBED_DIM), jnp.float32), 'Wq': jax.random.normal(ks[3], (EMBED_DIM, EMBED_DIM), jnp.float32) * scale, 'bq': jnp.zeros((EMBED_DIM,), jnp.float32), 'Wk': jax.random.normal(ks[4], (EMBED_DIM, EMBED_DIM), jnp.float32) * scale, 'bk': jnp.zeros((EMBED_DIM,), jnp.float32), 'Wv': jax.random.normal(ks[5], (EMBED_DIM, EMBED_DIM), jnp.float32) * scale, 'bv': jnp.zeros((EMBED_DIM,), jnp.float32), 'Wo': jax.random.normal(ks[6], (EMBED_DIM, EMBED_DIM), jnp.float32) * scale, 'bo': jnp.zeros((EMBED_DIM,), jnp.float32)}
        return inp
    _L0_xattn_all = _L0_xattn_setup()
    _L0_xattn_in = {k: v for k, v in _L0_xattn_all.items() if k in ('Wq', 'bq', 'Wk', 'bk', 'Wv', 'bv', 'Wo', 'bo')}
    del _L0_xattn_all

    def _L0_ffn_setup():
        import jax, jax.numpy as jnp
        import numpy as np
        E, G, TOPK = (32, 16, 2)
        HID, INTER, A_INTER = (256, 512, 128)
        CAP_FACTOR = 1.25
        SCALE = 0.05

        def _stats(x):
            mean = x.mean(-1, keepdims=True)
            std = jnp.std(x, axis=-1, keepdims=True, ddof=1)
            mn = x.min(-1, keepdims=True)
            mx = x.max(-1, keepdims=True)
            l2 = jnp.linalg.norm(x, axis=-1, keepdims=True)
            sp = (jnp.abs(x) < 1e-06).astype(x.dtype).mean(-1, keepdims=True)
            return jnp.concatenate([mean, std, mn, mx, l2, sp], -1)
        key = jax.random.key(seed)
        ks = jax.random.split(key, 8)
        B, N = (4, 256)
        s = lambda k, shape, sc: jax.random.normal(k, shape, jnp.float32) * sc
        return {'x': jax.random.normal(ks[0], (B, N, HID), jnp.float32), 'r1_w': s(ks[1], (HID // 2, HID + 6), 0.02), 'r1_b': jnp.zeros((HID // 2,), jnp.float32), 'r2_w': s(ks[2], (E, HID // 2), 0.02), 'w_up': s(ks[3], (E, 2 * INTER, HID), 0.02), 'w_down': s(ks[4], (E, HID, INTER), 0.02), 'a_up': s(ks[5], (G, 2 * A_INTER, HID), 0.02), 'a_down': s(ks[6], (G, HID, A_INTER), 0.02)}
    _L0_ffn_all = _L0_ffn_setup()
    _L0_ffn_in = {k: v for k, v in _L0_ffn_all.items() if k in ('r1_w', 'r1_b', 'r2_w', 'w_up', 'w_down', 'a_up', 'a_down')}
    del _L0_ffn_all
    return {'x': x, 'ctx_1024': ctx_1024, 'g_xattn': g_xattn, 'g_ffn': g_ffn, 'L0_xattn_Wq': _L0_xattn_in['Wq'], 'L0_xattn_bq': _L0_xattn_in['bq'], 'L0_xattn_Wk': _L0_xattn_in['Wk'], 'L0_xattn_bk': _L0_xattn_in['bk'], 'L0_xattn_Wv': _L0_xattn_in['Wv'], 'L0_xattn_bv': _L0_xattn_in['bv'], 'L0_xattn_Wo': _L0_xattn_in['Wo'], 'L0_xattn_bo': _L0_xattn_in['bo'], 'L0_ffn_r1_w': _L0_ffn_in['r1_w'], 'L0_ffn_r1_b': _L0_ffn_in['r1_b'], 'L0_ffn_r2_w': _L0_ffn_in['r2_w'], 'L0_ffn_w_up': _L0_ffn_in['w_up'], 'L0_ffn_w_down': _L0_ffn_in['w_down'], 'L0_ffn_a_up': _L0_ffn_in['a_up'], 'L0_ffn_a_down': _L0_ffn_in['a_down']}

def reference(x, ctx_1024, g_xattn, g_ffn, L0_xattn_Wq, L0_xattn_bq, L0_xattn_Wk, L0_xattn_bk, L0_xattn_Wv, L0_xattn_bv, L0_xattn_Wo, L0_xattn_bo, L0_ffn_r1_w, L0_ffn_r1_b, L0_ffn_r2_w, L0_ffn_w_up, L0_ffn_w_down, L0_ffn_a_up, L0_ffn_a_down):
    import jax
    import jax.numpy as jnp

    def _L0_xattn_ref(query, key, value, Wq, bq, Wk, bk, Wv, bv, Wo, bo):
        import jax, jax.numpy as jnp
        import numpy as np
        EMBED_DIM = 256
        NUM_HEADS = 16
        HEAD_DIM = EMBED_DIM // NUM_HEADS
        WINDOW = 128
        B, S_Q, S_K = (2, 512, 512)

        def apply_rope(x):
            Dh = x.shape[-1]
            half = Dh // 2
            pos = jnp.arange(x.shape[2], dtype=jnp.float32)
            inv_freq = 1.0 / 10000.0 ** (jnp.arange(0, half, dtype=jnp.float32) / half)
            ang = pos[:, None] * inv_freq[None, :]
            cos = jnp.cos(ang)[None, None, :, :].astype(x.dtype)
            sin = jnp.sin(ang)[None, None, :, :].astype(x.dtype)
            x1, x2 = (x[..., :half], x[..., half:])
            return jnp.concatenate([x1 * cos - x2 * sin, x1 * sin + x2 * cos], axis=-1)
        Bq, Sq, D = query.shape
        Sk = key.shape[1]
        H, Dh = (NUM_HEADS, HEAD_DIM)

        def proj(x, W, b):
            return (x @ W.T + b).reshape(x.shape[0], x.shape[1], H, Dh).transpose(0, 2, 1, 3)
        q = apply_rope(proj(query, Wq, bq))
        k = apply_rope(proj(key, Wk, bk))
        v = proj(value, Wv, bv)
        q = q * Dh ** (-0.5)
        scores = jnp.einsum('bhqd,bhkd->bhqk', q, k)
        q_idx = jnp.arange(Sq)[:, None]
        kv_idx = jnp.arange(Sk)[None, :]
        rel = kv_idx - q_idx
        mask = (rel > 0) | (rel < -WINDOW)
        mask4 = mask[None, None, :, :]
        neg = jnp.finfo(scores.dtype).min
        scores = jnp.where(mask4, neg, scores)
        probs = jax.nn.softmax(scores, axis=-1)
        all_masked = jnp.all(mask4, axis=-1, keepdims=True)
        probs = jnp.where(all_masked, jnp.zeros((), probs.dtype), probs)
        out = jnp.einsum('bhqk,bhkd->bhqd', probs, v)
        out = out.transpose(0, 2, 1, 3).reshape(Bq, Sq, D)
        return out @ Wo.T + bo

    def _L0_ffn_ref(x, r1_w, r1_b, r2_w, w_up, w_down, a_up, a_down):
        import jax, jax.numpy as jnp
        import numpy as np
        E, G, TOPK = (32, 16, 2)
        HID, INTER, A_INTER = (256, 512, 128)
        CAP_FACTOR = 1.25
        SCALE = 0.05

        def _stats(x):
            mean = x.mean(-1, keepdims=True)
            std = jnp.std(x, axis=-1, keepdims=True, ddof=1)
            mn = x.min(-1, keepdims=True)
            mx = x.max(-1, keepdims=True)
            l2 = jnp.linalg.norm(x, axis=-1, keepdims=True)
            sp = (jnp.abs(x) < 1e-06).astype(x.dtype).mean(-1, keepdims=True)
            return jnp.concatenate([mean, std, mn, mx, l2, sp], -1)
        B, N, C = x.shape
        xf = x.reshape(-1, C)
        T = xf.shape[0]
        cap = int(CAP_FACTOR * T / E)
        ri = jnp.concatenate([xf, _stats(xf)], -1)
        h = jax.nn.gelu(ri @ r1_w.T + r1_b, approximate=False)
        probs = jax.nn.softmax(h @ r2_w.T, -1)
        topp, topi = jax.lax.top_k(probs, TOPK)
        wnorm = topp / topp.sum(-1, keepdims=True)
        eids = jnp.arange(E)
        hit = topi[..., None] == eids
        routed = hit.any(1)
        Wc = jnp.where(hit, wnorm[..., None], 0.0).sum(1)
        score = jnp.where(routed, probs, -jnp.inf)
        idx = jnp.argsort(-score, axis=0)[:cap].T
        valid = jnp.take_along_axis(routed.T, idx, 1)
        w = jnp.take_along_axis(Wc.T, idx, 1) * valid
        xe = xf[idx]
        up = jnp.einsum('eci,eji->ecj', xe, w_up)
        gate, upv = jnp.split(up, 2, axis=-1)
        hact = jax.nn.silu(gate) * upv
        ye = jnp.einsum('ecj,eoj->eco', hact, w_down)
        out = jnp.zeros((T, C), xf.dtype).at[idx.reshape(-1)].add((w[..., None] * ye).reshape(-1, C))
        Wmask = jnp.zeros((T, E), xf.dtype).at[idx, eids[:, None]].add(w)
        gw = SCALE * Wmask.reshape(T, G, E // G).sum(-1)
        aup = jnp.einsum('tc,gjc->tgj', xf, a_up)
        ag, av = jnp.split(aup, 2, axis=-1)
        ah = jax.nn.silu(ag) * av
        ay = jnp.einsum('tgj,goj->tgo', ah, a_down)
        out = out + jnp.einsum('tg,tgo->to', gw, ay)
        return out.reshape(B, N, C)
    x = x + jnp.tanh(g_xattn[0]) * _L0_xattn_ref(_layernorm(x, axis=-1), ctx_1024, ctx_1024, L0_xattn_Wq, L0_xattn_bq, L0_xattn_Wk, L0_xattn_bk, L0_xattn_Wv, L0_xattn_bv, L0_xattn_Wo, L0_xattn_bo)
    x = x + jnp.tanh(g_ffn[0]) * _L0_ffn_ref(_layernorm(x, axis=-1), L0_ffn_r1_w, L0_ffn_r1_b, L0_ffn_r2_w, L0_ffn_w_up, L0_ffn_w_down, L0_ffn_a_up, L0_ffn_a_down)
    return x

_drawn_inputs = setup_inputs


def setup_inputs(seed=0):
    import zlib

    import numpy as np

    out = dict(_drawn_inputs(seed))
    spreads = {'L0_xattn_bq': (0.0, 0.451),
     'L0_xattn_bk': (0.0, 0.8),
     'L0_xattn_bv': (0.0, 0.1),
     'L0_xattn_bo': (0.0, 0.1),
     'L0_ffn_r1_b': (0.0, 0.8)}
    factors = {'L0_ffn_r1_w': 6.894,
     'L0_ffn_r2_w': 6.897,
     'L0_ffn_w_up': 6.885,
     'L0_ffn_w_down': 6.885,
     'L0_ffn_a_up': 8.0,
     'L0_ffn_a_down': 8.0}
    for name, (base, spread) in spreads.items():
        noise = np.random.default_rng([zlib.crc32(name.encode()), seed]).standard_normal(out[name].shape)
        drawn = base * np.exp(spread * noise) if base else spread * noise
        out[name] = jnp.asarray(drawn.astype(out[name].dtype))
    for name, factor in factors.items():
        out[name] = (out[name] * factor).astype(out[name].dtype)
    return out
```

```python
from contextlib import ExitStack

import numpy as np
import concourse.bass as bass
from concourse import mybir

F32 = mybir.dt.float32
BF16 = mybir.dt.bfloat16
I32 = mybir.dt.int32
ALU = mybir.AluOpType
ACT = mybir.ActivationFunctionType
X = mybir.AxisListType.X

NB, T, C = 32, 112, 256
NH, DH = 16, 16
WINDOW = 128
assert T <= WINDOW
GB = 4
NG = NB // GB
NT = GB * T
HU = 4
NU = NH // HU
GU = GB * NU
VE = DH + 1
NE, NGRP, INTER, AINTER = 32, 16, 512, 128
HID = 128
NST = 6
TOKENS = NB * T
CAP = int(1.25 * TOKENS / NE)
HC = CAP // 2
ROW = C + NE + 1
BIG = float(1 << 20)
NCH, CHB = 4, NB // 4
ROUNDS, DIGITS = 15, 3
KE = INTER // 128
KD = KE + 1
WE_COLS = 2 * 2 * INTER + KE * C
WA_COLS = 2 * 2 * AINTER + C
SCALE = 0.05

TAB = {}
_at = 0
for _name, _n in (("ident", 128), ("cos", T), ("sin", T), ("causal", T), ("lower", T), ("rev", NE),
                  ("slot0", NE), ("parity", 2), ("chunk", 128)):
    TAB[_name] = slice(_at, _at + _n)
    _at += _n
TAB_COLS = _at


def table():
    t = np.zeros((128, TAB_COLS), np.float32)
    t[:, TAB["ident"]] = np.eye(128)
    half = DH // 2
    freq = (1.0 / 10000.0 ** (np.arange(half, dtype=np.float32) / half)).astype(np.float32)
    ang = np.arange(T, dtype=np.float32)[None, :] * freq[:, None]
    row = np.arange(128)
    t[:, TAB["cos"]] = np.cos(ang)[row % half]
    t[:, TAB["sin"]] = np.sin(ang)[row % half] * np.where(row % DH < half, -1.0, 1.0)[:, None]
    q = np.arange(T)
    t[:T, TAB["causal"]] = np.where(q[None, :] > q[:, None], -1e30, 0.0)
    t[:T, TAB["lower"]] = q[:, None] < q[None, :]
    t[:, TAB["rev"]] = NE - np.arange(NE)
    t[:, TAB["slot0"]] = CAP * np.arange(NE) + BIG
    t[:, TAB["parity"]] = (row[:, None] // DH) % 2 == np.arange(2)[None, :]
    t[:, TAB["chunk"]] = (row[:, None] % NE) == (row[None, :] % NE)
    return t


def digits():
    d = np.zeros((128, ROUNDS, DIGITS), np.int32)
    for r in range(ROUNDS):
        d[:, r] = [j << (2 * (ROUNDS - 1 - r)) for j in range(1, DIGITS + 1)]
    return d


def wait(eng, sem, value):
    if not (isinstance(value, int) and value <= 0):
        eng.wait_ge(sem, value)


class Plain:

    def __init__(self, sem):
        self.sem = sem

    def __call__(self, eng):
        eng.sem_inc(self.sem, 1)


class Chain:

    def __init__(self, eng, sem):
        self.eng, self.sem, self.base, self.n = eng, sem, 0, 0

    def __call__(self, ins, then=None):
        self.n += 1
        ins.then_inc(self.sem, 1)
        self.eng.wait_ge(self.sem, self.base + self.n)
        if then:
            then(self.eng)

    def enter(self, trip, per_trip):
        self.outer = self.base + self.n
        self.base, self.n, self.per_trip = self.outer + trip * per_trip, 0, per_trip

    def leave(self, trips):
        assert self.n == self.per_trip, (self.sem, self.n, self.per_trip)
        self.base, self.n = self.outer + trips * self.per_trip, 0


FRONT = [(4, "K", 0), (5, "X", 0), (6, "K", 1), (6, "X", 1), (7, "X", 2), (8, "X", 3),
         (10, "Q", 0), (12, "Q", 1), (9, "V", 0), (11, "V", 1), (14, "V", 2), (16, "V", 3)]
ROUTE = [(7, "T", 0), (8, "H", 0), (10, "T", 1), (12, "H", 1), (14, "T", 2), (15, "H", 2),
         (17, "T", 3), (18, "H", 3)]
OUT = [(NU * b + 7, "A", b) for b in range(GB)] + [(NU * b + 8, "O", b) for b in range(GB)]
STEPS = 21
ATT_STEPS = tuple(NU * b + 7 for b in range(GB))
ROTATE = (6, 8, 11, 13)
KEYS = (9, 11)


def items(front, route, out=True):
    all_ = (FRONT if front else []) + (ROUTE if route else []) + (OUT if out else [])
    return [(s, w, j, n % 2, n // 2) for n, (s, w, j) in enumerate(sorted(all_, key=lambda x: x[0]))]


def m_base(g):
    f, r, o = len(FRONT) // 2, len(ROUTE) // 2, len(OUT) // 2
    if isinstance(g, int):
        return max(0, min(g + 1, NG)) * f + max(0, g - 1) * r + max(0, g) * o
    return (f + r + o) * g + (f - r)


BS, BT, BO, BM = (0, 1, 2), (3, 4), 5, (6, 7)
POOL_LINKS, DVE_LINKS = 22, 112


def signal(eng, ins, sem, value):
    ins.then_inc(sem, 1)
    eng.wait_ge(sem, value)


def build(nc, d):
    ctx = ExitStack()
    with ctx:
        program(nc, d, ctx)


def program(nc, d, ctx):
    def sb(name, shape, dt=F32):
        return ctx.enter_context(nc.sbuf_tensor(name, shape, dt))

    def sem(name):
        return ctx.enter_context(nc.semaphore(name))

    tab = sb("tab", [128, TAB_COLS])
    ident = tab[:, TAB["ident"]]
    xf_all = sb("xf_all", [T, NB, ROW])
    hpre = sb("hpre", [HID, TOKENS])
    we = [[sb(f"we{s}{j}", [128, WE_COLS]) for j in range(2)] for s in range(2)]
    wa = [sb(f"wa{s}", [128, WA_COLS]) for s in range(2)]
    gates = sb("gates", [128, 4])
    r2t = sb("r2t", [HID, NE])
    banks = [ctx.enter_context(nc.psum_tensor(f"bank{i}", [128, 512], F32)) for i in range(8)]

    ARENA = 25440
    arena = sb("arena", [128, ARENA])
    used = [0]

    def take(parts, shape, dt=F32):
        n = int(np.prod(shape))
        words = n if dt != BF16 else (n + 1) // 2
        a = arena[:, used[0]:used[0] + words]
        used[0] += words
        assert used[0] <= ARENA, used[0]
        a = a if dt == F32 else a.bitcast(dt)
        names = "abcd"[:len(shape)]
        if len(shape) > 1:
            a = a.rearrange(f"p ({' '.join(names)}) -> p {' '.join(names)}", **dict(zip(names, shape)))
        return a[0:parts]

    wq, wk, wv, wo = (take(128, [2, C]) for _ in range(4))
    bqk = take(128, [4])
    bvb, gbo = take(T, [C]), take(T, [C])
    r1t, r1s = take(128, [2, HID]), take(NST, [HID])
    r1b = take(128, [1])
    identb, causalb = take(T, [T], BF16), take(T, [T], BF16)
    ctxt = [take(128, [2, NT]) for _ in range(2)]
    xin = [take(T, [GB, C]) for _ in range(2)]
    half_pow = take(T, [8])
    mv1, mv2, mv3 = (take(T, [GB, 2]) for _ in range(3))
    rs1, rs2, tmp4 = (take(T, [GB]) for _ in range(3))
    bns = take(T, [6])
    xn = take(T, [GB, C])
    xnt = take(128, [2, NT])
    proj = [take(128, [NT]) for _ in range(2)]
    pcos = [take(128, [NT]) for _ in range(2)]
    prot = [take(128, [NT]) for _ in range(2)]
    kraw = [take(128, [NT]) for _ in range(2)]
    qt = [take(128, [2, NT]) for _ in range(2)]
    kz = [take(128, [2, 2, NT]) for _ in range(2)]
    vx = [take(T, [GB, NH, VE]) for _ in range(2)]
    mx = [take(T, [HU]) for _ in range(3)]
    nmx = [take(T, [HU]) for _ in range(3)]
    pr = [take(T, [HU, T]) for _ in range(3)]
    prt = [take(T, [HU, T]) for _ in range(2)]
    rden = take(T, [NH])
    att = take(T, [C])
    attt = take(128, [2, T])
    x1 = take(T, [GB, C])
    xf = take(T, [GB, C])
    st = take(T, [GB, NST])
    xft, stt = take(128, [2, T]), take(NST, [T])
    spj = take(T, [C])


    used[0] = 0
    prb, w0, w1, h1, h2 = (take(T, [NB, NE]) for _ in range(5))
    sc = take(T, [CHB, NCH, NE])
    sc_flat = sc.rearrange("p j c e -> p (j c e)")
    sc_turned = sc.rearrange("p j c e -> p c j e")
    col = [take(T, [NB]) for _ in range(8)]
    se = take(128, [CHB * T])
    sej = take(128, [CHB * T])
    vb = take(128, [1 + DIGITS])
    cand = take(128, [DIGITS])
    cnt = take(128, [DIGITS])
    dig = take(128, [ROUNDS, DIGITS], I32)
    thd, thr, cgt = take(NE, [NE]), take(T, [NE]), take(T, [NE])
    ge = take(T, [2, NB, NE], BF16)
    inc = [take(T, [2, NB + 1, NE], BF16) for _ in range(2)]
    lowb, onesb = take(T, [T], BF16), take(T, [T], BF16)
    ones = take(128, [T])
    dest = take(T, [2, NB], I32)


    used[0] = 0
    xr = [take(HC, [2, ROW]) for _ in range(4)]
    xet = [take(128, [2, CAP]) for _ in range(2)]
    th = [take(128, [CAP]) for _ in range(2)]
    gs = [take(128, [CAP]) for _ in range(2)]
    hh = [take(128, [KD, CAP]) for _ in range(2)]
    yt = [take(128, [2, CAP]) for _ in range(2)]
    yr = [take(HC, [2, C]) for _ in range(2)]
    fill = hpre[0:HC, 0:2 * ROW].rearrange("p (s c) -> p s c", s=2)
    zero = hpre[0:HC, 2 * ROW:2 * ROW + 2 * C].rearrange("p (s c) -> p s c", s=2)

    s_tab, s_const, s_filled, s_gl = sem("tables_in"), sem("weights_in"), sem("filling_made"), sem("gates_in")
    s_fo = sem("filling_out")
    s_setup, s_gate = sem("vector_setup"), sem("gates_ready")
    s_xin = [sem("x_in0"), sem("x_in1")]
    s_ctx = [sem("ctx_in0"), sem("ctx_in1")]
    s_mv1, s_rs1, s_xn, s_xnt = sem("mean1"), sem("rstd1"), sem("xn_ready"), sem("xnt_ready")
    s_xb = sem("bias_added")
    s_m = [sem("m1_written"), sem("m2_written")]
    s_mf = [sem("m1_read"), sem("m2_read")]
    s_proj, s_rot, s_rope, s_kz, s_v = (sem(n) for n in ("proj_ready", "rotated", "roped", "kz_ready", "v_ready"))
    s_s, s_mx, s_exp, s_ptr = sem("scores_ready"), sem("max_ready"), sem("exp_ready"), sem("probs_turned")
    s_pte = [sem("prt_even"), sem("prt_odd")]
    s_pv, s_att, s_attt, s_x1 = (sem(n) for n in ("pv_done", "att_ready", "attt_ready", "x1_ready"))
    s_ln2, s_rs2, s_mv3, s_st, s_xout, s_xfc = (sem(n) for n in (
        "ln2_stats", "rstd2", "xf_stats", "stats_ready", "x1_stored", "xf_kept"))
    s_xft = sem("xft_ready")
    s_dve, s_act, s_pool = sem("vector_chain"), sem("scalar_chain"), sem("pool_chain")

    x_rows = d["x"].rearrange("(n p) c -> p n c", p=T)
    o_rows = d["out"][0:TOKENS, :].rearrange("(n p) c -> p n c", p=T)
    block = ctx.enter_context(nc.Block())

    plain = Plain(sem("waits_carried"))
    GV = {}
    for s, per in ((s_mv1, 1), (s_rs1, 1), (s_xn, 1), (s_xb, 1), (s_xnt, 4), (s_proj, 4), (s_rot, 4),
                   (s_rope, 4), (s_kz, 2), (s_v, 4), (s_s, GU), (s_mx, GU), (s_exp, GU), (s_ptr, GU),
                   (s_pte[0], GU // 2), (s_pte[1], GU // 2), (s_pv, GU), (s_att, GB),
                   (s_attt, GB), (s_x1, GB), (s_ln2, 1), (s_rs2, 1), (s_mv3, 1), (s_st, 1),
                   (s_xft, 4), (s_xout, 16), (s_xfc, 16)):
        GV[s] = per * NG
    for b in range(2):
        GV[s_m[b]] = GV[s_mf[b]] = NG * (len(FRONT) + len(ROUTE) + len(OUT)) // 2

    def attention_done(eng):
        for s, v in GV.items():
            eng.wait_ge(s, v)

    def groups(eng_fori, body, chain=None, per_trip=0):
        body(0, 0, True, False)
        with eng_fori(0, (NG - 2) // 2) as i:
            if chain:
                chain.enter(i, per_trip)
            body(2 * i + 1, 1, True, True)
            body(2 * i + 2, 0, True, True)
            if chain:
                chain.leave((NG - 2) // 2)
        body(NG - 1, 1, False, True)

    w_sem = [sem("experts_in0"), sem("experts_in1")]
    s_pair = sem("pair_done")
    s_xs, s_xr = sem("rows_dispatched"), [sem(f"xr_in{i}") for i in range(4)]
    s_added = sem("rows_added")

    def load_pair(p, slot):
        for j in range(2):
            nc.sync.dma_start(we[slot][j][:], d["w_experts"][2 * p + j]).then_inc(w_sem[slot], 16)
        nc.sync.dma_start(wa[slot][:], d["w_adapters"][p]).then_inc(w_sem[slot], 16)

    s_h, s_lg, s_sub, s_e = sem("gelu_ready"), sem("logits_ready"), sem("logits_shifted"), sem("exp_of_logits")
    s_dig, s_ones, s_scr, s_set = sem("digits_in"), sem("ones_ready"), sem("scores_by_token"), sem("scores_turned")
    s_cnt, s_tot, s_thd, s_thr = sem("chunk_counts"), sem("totals"), sem("thresholds"), sem("thresholds_spread")
    s_ge, s_inc, s_slot, s_dest = sem("compared"), sem("prefix_ready"), sem("slots_counted"), sem("destinations")
    HG = TOKENS // GB // 2

    def routing_scalar(act):
        attention_done(act)
        for g in range(NG):
            nc.scalar.activation(hpre[:, g * HG:(g + 1) * HG], hpre[:, g * HG:(g + 1) * HG], ACT.Gelu).then_inc(s_h, 1)
        act.wait_ge(s_sub, 1)
        nc.scalar.activation(w0, w0, ACT.Exp).then_inc(s_e, 1)
        act.wait_ge(s_set, 1)
        nc.scalar.copy(se[:, 0:GB * T], banks[2][:, 0:GB * T])
        nc.scalar.copy(se[:, GB * T:], banks[3][:, 0:GB * T]).then_inc(s_set, 1)

    def routing_tensor(pe):
        attention_done(pe)
        for b in range(NB):
            pe.wait_ge(s_h, b // GB + 1)
            last = nc.tensor.matmul(banks[b // 16][0:T, (b % 16) * NE:(b % 16 + 1) * NE],
                                    hpre[:, b * T:(b + 1) * T], r2t[:], start=True, stop=True)
        last.then_inc(s_lg, 1)
        pe.wait_ge(s_scr, 1)
        for j in range(CHB):
            last = nc.tensor.transpose(banks[2 + j // GB][:, (j % GB) * T:(j % GB + 1) * T],
                                       sc_flat[:, j * 128:(j + 1) * 128], ident[0:T, 0:T])
        last.then_inc(s_set, 1)
        with nc.tensor.Fori(0, ROUNDS) as r:
            pe.wait_ge(s_cnt, r + 1)
            nc.tensor.matmul(banks[4][:, 0:DIGITS], tab[:, TAB["chunk"]], cnt, start=True, stop=True).then_inc(s_tot, 1)
        pe.wait_ge(s_thd, 1)
        nc.tensor.matmul(banks[5][0:T, 0:NE], ones[0:NE], thd, start=True, stop=True).then_inc(s_thr, 1)
        pe.wait_ge(s_ge, 1)
        pe.wait_ge(s_inc, 1)
        for w in range(2):
            for q in range(2):
                out = banks[2 * w + q][0:T, :]
                nc.tensor.matmul(out, lowb, ge[:, w, q * 16:(q + 1) * 16, :], start=True, stop=False)
                nc.tensor.matmul(out, onesb, inc[1][:, w, q * 16:(q + 1) * 16, :], start=False, stop=True)
        nc.tensor.matmul(banks[6][0:T, 0:NE], onesb, inc[1][:, 0, NB, :], start=True, stop=True).then_inc(s_slot, 1)

    def routing_vector(dve, link):
        attention_done(dve)
        over_b = lambda a: a.unsqueeze(1).to_broadcast([T, NB, NE])
        over_e = lambda a: a.unsqueeze(2).to_broadcast([T, a.shape[1], NE])
        rev = over_b(tab[0:T, TAB["rev"]])
        nc.vector.memset(ones, 1.0).then_inc(s_ones, 1)
        nc.vector.memset(onesb, 1.0).then_inc(s_ones, 1)
        nc.vector.tensor_copy(lowb, tab[0:T, TAB["lower"]]).then_inc(s_ones, 1)
        nc.vector.memset(vb[:, 0:1], 0.0)
        for i in range(2):
            link(nc.vector.memset(inc[i][:, :, 0, :], 0.0))
        dve.wait_ge(s_lg, 1)
        for q in range(2):
            lg = banks[q][0:T, :].rearrange("p (b e) -> p b e", e=NE)
            link(nc.vector.tensor_reduce(col[0][:, q * 16:(q + 1) * 16], lg, X, ALU.max))
            link(nc.vector.tensor_tensor(w0[:, q * 16:(q + 1) * 16, :], lg, over_e(col[0][:, q * 16:(q + 1) * 16]),
                                         ALU.subtract))
        dve.sem_inc(s_sub, 1)
        dve.wait_ge(s_e, 1)
        link(nc.vector.tensor_reduce(col[1], w0, X, ALU.add))
        link(nc.vector.reciprocal(col[2], col[1]))
        link(nc.vector.tensor_tensor(prb, w0, over_e(col[2]), ALU.mult))

        def choose(values, top, hit):
            link(nc.vector.tensor_reduce(top, values, X, ALU.max))
            link(nc.vector.tensor_tensor(w1, values, over_e(top), ALU.is_equal))
            link(nc.vector.tensor_tensor(w1, w1, rev, ALU.mult))
            link(nc.vector.tensor_reduce(col[3], w1, X, ALU.max))
            link(nc.vector.tensor_tensor(hit, w1, over_e(col[3]), ALU.is_equal))

        choose(prb, col[4], h1)
        link(nc.vector.scalar_tensor_tensor(w0, h1, -2.0, prb, ALU.mult, ALU.add))
        choose(w0, col[5], h2)
        link(nc.vector.tensor_tensor(w1, h1, h2, ALU.add))
        link(nc.vector.tensor_tensor(w0, prb, w1, ALU.mult))
        link(nc.vector.tensor_scalar(w1, w1, -1.0, None, ALU.add))
        link(nc.vector.tensor_tensor(sc_turned, w0, w1, ALU.add))
        dve.sem_inc(s_scr, 1)
        link(nc.vector.tensor_tensor(col[6], col[4], col[5], ALU.add))
        link(nc.vector.reciprocal(col[7], col[6]))
        link(nc.vector.tensor_scalar(col[7], col[7], gates[0:T, 2:3], None, ALU.mult))
        link(nc.vector.tensor_tensor(col[4], col[4], col[7], ALU.mult))
        link(nc.vector.tensor_tensor(col[5], col[5], col[7], ALU.mult))
        link(nc.vector.tensor_tensor(w0, h1, over_e(col[4]), ALU.mult))
        link(nc.vector.tensor_tensor(w1, h2, over_e(col[5]), ALU.mult))
        link(nc.vector.tensor_tensor(xf_all[:, :, C:C + NE], w0, w1, ALU.add))
        dve.wait_ge(s_dig, 16)
        dve.wait_ge(s_set, 2)
        per = DIGITS + 3
        with nc.vector.Fori(0, ROUNDS) as r:
            link.enter(r, per)
            link(nc.vector.tensor_tensor(cand.bitcast(I32), dig[:, r, :],
                                         vb[:, 0:1].bitcast(I32).to_broadcast([128, DIGITS]), ALU.bitwise_or))
            for j in range(DIGITS):
                link(nc.vector.tensor_scalar(sej, se, cand[:, j:j + 1], None, ALU.is_ge, ALU.add,
                                             accum_out=cnt[:, j:j + 1]))
            dve.sem_inc(s_cnt, 1)
            dve.wait_ge(s_tot, r + 1)
            link(nc.vector.scalar_tensor_tensor(vb[:, 1:1 + DIGITS], banks[4][:, 0:DIGITS], float(CAP), cand,
                                                ALU.is_ge, ALU.mult))
            link(nc.vector.tensor_reduce(vb[:, 0:1], vb, X, ALU.max))
            link.leave(ROUNDS)
        link(nc.vector.tensor_scalar(thd, ident[0:NE, 0:NE], vb[0:NE, 0:1], None, ALU.mult))
        dve.sem_inc(s_thd, 1)
        dve.wait_ge(s_thr, 1)
        link(nc.vector.tensor_copy(thr, banks[5][0:T, 0:NE]))
        tb = thr.unsqueeze(1).unsqueeze(1).to_broadcast([T, NCH, CHB, NE])
        for w, op in ((0, ALU.is_gt), (1, ALU.is_equal)):
            for c in range(NCH):
                rows = slice(c * CHB, (c + 1) * CHB)
                link(nc.vector.tensor_tensor(ge[:, w, rows, :], sc[:, :, c, :],
                                             thr.unsqueeze(1).to_broadcast([T, CHB, NE]), op))
        dve.sem_inc(s_ge, 1)
        src, step = ge, 1
        for n in range(5):
            dst = inc[(n + 1) % 2]
            s_ = src[:, :, 1:, :] if n else ge
            link(nc.vector.tensor_copy(dst[:, :, 1:1 + step, :], s_[:, :, 0:step, :]))
            for w in range(2):
                link(nc.vector.tensor_tensor(dst[:, w, 1 + step:, :], s_[:, w, step:, :],
                                             s_[:, w, 0:NB - step, :], ALU.add))
            src, step = dst, 2 * step
        dve.sem_inc(s_inc, 1)
        dve.wait_ge(s_slot, 1)
        link(nc.vector.tensor_copy(cgt, banks[6][0:T, 0:NE]))
        for q in range(2):
            rows = slice(q * 16, (q + 1) * 16)
            pg = banks[q][0:T, :].rearrange("p (b e) -> p b e", e=NE)
            pq = banks[2 + q][0:T, :].rearrange("p (b e) -> p b e", e=NE)
            link(nc.vector.tensor_tensor(w0[:, rows, :], ge[:, 0, rows, :], pg, ALU.mult))
            link(nc.vector.tensor_tensor(w1[:, rows, :], cgt.unsqueeze(1).to_broadcast([T, 16, NE]), pq, ALU.add))
        link(nc.vector.tensor_tensor(w1, w1, ge[:, 1], ALU.mult))
        link(nc.vector.tensor_tensor(w0, w0, w1, ALU.add))
        link(nc.vector.tensor_tensor(w1, ge[:, 0], ge[:, 1], ALU.add))
        link(nc.vector.scalar_tensor_tensor(w1, w1, -BIG, w0, ALU.mult, ALU.add))
        link(nc.vector.tensor_scalar(w0, w0, float(CAP), BIG, ALU.is_ge, ALU.mult))
        link(nc.vector.tensor_tensor(w0, w0, w1, ALU.add))
        link(nc.vector.tensor_tensor(w0, w0, over_b(tab[0:T, TAB["slot0"]]), ALU.add))
        for k, hit in enumerate((h1, h2)):
            link(nc.vector.tensor_tensor(w1, w0, hit, ALU.mult))
            link(nc.vector.tensor_reduce(col[0], w1, X, ALU.add))
            link(nc.vector.tensor_copy(dest[:, k, :], col[0]))
        dve.sem_inc(s_dest, 1)

    s_xet, s_xrt, s_up, s_th, s_hh, s_yt, s_yts, s_yw, s_yr = (sem(n) for n in (
        "xet_ready", "rows_turned", "up_done", "tanh_ready", "hidden_ready", "down_done", "yt_ready",
        "y_turned", "y_ready"))
    s_gs = sem("gated")
    LAST = NE - 4

    def experts_sync(sp):
        def load_rows(e, slot):
            nc.sync.dma_start(xr[slot], d["slots"][e]).then_inc(s_xr[slot], 16)

        sp.wait_ge(s_xs, 16 * 2 * NB)
        for e in range(4):
            load_rows(e, e)
        with nc.sync.Fori(0, NE // 4 - 1) as i:
            for s in range(2):
                sp.wait_ge(s_pair, 2 * i + s + 1)
                load_pair(2 * i + s + 2, s)
                sp.wait_ge(s_added, 32 * (4 * i + 2 * s + 2))
                for j in range(2):
                    load_rows(4 * i + 4 + 2 * s + j, 2 * s + j)

    def experts_pool(pool, link):
        attention_done(pool)
        pool.wait_ge(s_dest, 1)
        pool.wait_ge(s_fo, 16 * (NE + 1))
        slots = d["slots_flat"]
        for b in range(NB):
            for k in range(2):
                nc.gpsimd.indirect_dma_start(slots, bass.IndirectOffsetOnAxis(ap=dest[:, k, b:b + 1], axis=0),
                                             xf_all[:, b, :], None, bounds_check=NE * CAP - 1,
                                             oob_is_err=False).then_inc(s_xs, 16)

        def expert(e, j):
            pool.wait_ge(s_yr, e + 1)
            wait(pool, s_added, 32 * e)
            plain(pool)
            for h in range(2):
                nc.gpsimd.indirect_dma_start(d["out"], bass.IndirectOffsetOnAxis(
                    ap=xr[j][:, h, ROW - 1:ROW].bitcast(I32), axis=0), yr[j % 2][:, h, :], None,
                    compute_op=ALU.add).then_inc(s_added, 16)

        for j in range(4):
            expert(j, j)
        with nc.gpsimd.Fori(1, NE // 4) as i:
            for j in range(4):
                expert(4 * i + j, j)
        pool.wait_ge(s_added, 32 * NE)

    def experts_scalar(act):
        def expert(e, j):
            act.wait_ge(s_xrt, e + 1)
            wait(act, s_up, KD * (e - 1))
            nc.scalar.copy(xet[j % 2].rearrange("p c t -> p (c t)"), banks[4][:, 0:2 * CAP]).then_inc(s_xet, 1)
            for k in range(KD):
                n, m = KD * e + k, KD * j + k
                act.wait_ge(s_up, n + 1)
                wait(act, s_gs, n - 1)
                nc.scalar.activation(th[m % 2], banks[m % 4][:, 0:CAP], ACT.Tanh, scale=0.5).then_inc(s_th, 1)
            act.wait_ge(s_yt, e + 1)
            wait(act, s_yw, e - 1)
            nc.scalar.copy(yt[j % 2][:, 0, :], banks[5][:, 0:CAP])
            nc.scalar.copy(yt[j % 2][:, 1, :], banks[6][:, 0:CAP]).then_inc(s_yts, 1)

        for j in range(4):
            expert(j, j)
        with nc.scalar.Fori(1, NE // 4) as i:
            for j in range(4):
                expert(4 * i + j, j)

    def experts_vector(dve, link):
        def turned(e, j):
            dve.wait_ge(s_yw, e + 1)
            wait(dve, s_added, 32 * (e - 1))
            for h in range(2):
                last = nc.vector.tensor_scalar(yr[j % 2][:, h, :], banks[7][0:HC, h * C:(h + 1) * C],
                                               xr[j][:, h, bass.ds(C + e, 1)], None, ALU.mult)
            last.then_inc(s_yr, 1)

        def expert(e, j):
            for k in range(KD):
                n, m = KD * e + k, KD * j + k
                dve.wait_ge(s_th, n + 1)
                signal(dve, nc.vector.scalar_tensor_tensor(gs[m % 2], th[m % 2], 1.0, banks[m % 4][:, 0:CAP],
                                                           ALU.add, ALU.mult), s_gs, n + 1)
                if k == 0:
                    wait(dve, s_yt, e - 1)
                if k < KE:
                    nc.vector.tensor_tensor(hh[j % 2][:, k, :], gs[m % 2], banks[m % 4][:, CAP:2 * CAP],
                                            ALU.mult).then_inc(s_hh, 1)
                else:
                    nc.vector.scalar_tensor_tensor(hh[j % 2][:, k, :], gs[m % 2], SCALE,
                                                   banks[m % 4][:, CAP:2 * CAP], ALU.mult,
                                                   ALU.mult).then_inc(s_hh, 1)
            turned(e, j)

        for j in range(4):
            expert(j, j)
        with nc.vector.Fori(1, NE // 4) as i:
            for j in range(4):
                expert(4 * i + j, j)

    def experts_tensor(pe):
        def turn_rows(e, j, loads):
            pe.wait_ge(s_xr[j], 16 * loads)
            wait(pe, s_xet, e)
            for c in range(2):
                for h in range(2):
                    last = nc.tensor.transpose(banks[4][:, c * CAP + h * HC:c * CAP + (h + 1) * HC],
                                               xr[j][:, h, c * 128:(c + 1) * 128], ident[0:HC, 0:HC])
            last.then_inc(s_xrt, 1)

        def up(e, j, k):
            n, m = KD * e + k, KD * j + k
            wait(pe, s_hh, n - 3)
            w, width, at = (we[j // 2][j % 2], INTER, k * 128) if k < KE else (wa[j // 2], AINTER, 0)
            for part in range(2):
                for c in range(2):
                    col0 = c * 2 * width + part * width + at
                    last = nc.tensor.matmul(banks[m % 4][:, part * CAP:(part + 1) * CAP], w[:, col0:col0 + 128],
                                            xet[j % 2][:, c, :], start=(c == 0), stop=(c == 1))
            last.then_inc(s_up, 1)

        def down(e, j, k):
            pe.wait_ge(s_hh, KD * e + k + 1)
            if k == 0:
                wait(pe, s_yts, e)
            w, col0 = (we[j // 2][j % 2], 4 * INTER + k * C) if k < KE else (wa[j // 2], 4 * AINTER)
            for o in range(2):
                last = nc.tensor.matmul(banks[5 + o][:, 0:CAP], w[:, col0 + o * 128:col0 + (o + 1) * 128],
                                        hh[j % 2][:, k, :], start=(k == 0), stop=(k == KD - 1))
            if k == KD - 1:
                last.then_inc(s_yt, 1)

        def turn_back(e, j):
            pe.wait_ge(s_yts, e + 1)
            wait(pe, s_yr, e)
            for h in range(2):
                for o in range(2):
                    last = nc.tensor.transpose(banks[7][0:HC, h * C + o * 128:h * C + (o + 1) * 128],
                                               yt[j % 2][:, o, h * HC:(h + 1) * HC], ident)
            last.then_inc(s_yw, 1)

        def four(i, loads, first, last_four):
            for j in range(4):
                e = 4 * i + j
                if j % 2 == 0:
                    pe.wait_ge(w_sem[j // 2], 48 * loads)
                pe.wait_ge(s_xet, e + 1)
                for k in range(KD):
                    up(e, j, k)
                    if k >= 2:
                        down(e, j, k - 2)
                if j < 3:
                    turn_rows(e + 1, j + 1, loads)
                elif not last_four:
                    turn_rows(e + 1, 0, loads + 1)
                down(e, j, KD - 2)
                down(e, j, KD - 1)
                if j % 2 == 1:
                    pe.wait_ge(s_yt, e + 1)
                    pe.sem_inc(s_pair, 1)
                turn_back(e, j)

        turn_rows(0, 0, 1)
        four(0, 1, True, False)
        with nc.tensor.Fori(1, NE // 4 - 1) as i:
            four(i, i + 1, False, False)
        four(NE // 4 - 1, NE // 4, False, True)

    @block.sync
    def _(sp):
        nc.sync.dma_start(xin[0], x_rows[:, 0:GB, :]).then_inc(s_xin[0], 16)
        nc.sync.dma_start(tab[:], d["table"]).then_inc(s_tab, 16)
        nc.sync.dma_start(ctxt[0], d["ctx"][0]).then_inc(s_ctx[0], 16)
        for dst, name in ((wq, "wq"), (wk, "wk"), (wv, "wv"), (wo, "wo"), (bqk, "bqk"), (r1t, "r1t"),
                          (r1s, "r1s"), (r1b, "r1b")):
            nc.sync.dma_start(dst, d[name]).then_inc(s_const, 16)
        nc.sync.dma_start(bvb, d["bv"].partition_broadcast(T)).then_inc(s_const, 16)
        nc.sync.dma_start(gbo, d["bo"].partition_broadcast(T)).then_inc(s_const, 16)
        nc.sync.dma_start(r2t[:], d["r2t"]).then_inc(s_const, 16)
        nc.sync.dma_start(gates[:, 0:2], d["gates"].partition_broadcast(128)).then_inc(s_gl, 16)
        sp.wait_ge(s_filled, 2)
        with nc.sync.Fori(0, NE) as e:
            nc.sync.dma_start(d["slots"][e], fill).then_inc(s_fo, 16)
        nc.sync.dma_start(d["out"][TOKENS:TOKENS + CAP, :].rearrange("(s p) c -> p s c", p=HC),
                          zero).then_inc(s_fo, 16)
        load_pair(0, 0)
        load_pair(1, 1)

        def group(g, par, front, route):
            if front:
                wait(sp, s_x1, GB * g)
                wait(sp, s_v, 4 * g)
                wait(sp, s_proj, 4 * g)
                nc.sync.dma_start(xin[1 - par], x_rows[:, bass.ds(GB * (g + 1), GB), :]).then_inc(s_xin[1 - par], 16)
                nc.sync.dma_start(ctxt[1 - par], d["ctx"][g + 1]).then_inc(s_ctx[1 - par], 16)
            if route:
                wait(sp, s_mv3, g)
                nc.sync.dma_start(xf_all[:, bass.ds(GB * (g - 1), GB), 0:C], xf).then_inc(s_xfc, 16)
            wait(sp, s_x1, GB * (g + 1))
            nc.sync.dma_start(o_rows[:, bass.ds(GB * g, GB), :], x1).then_inc(s_xout, 16)

        groups(nc.sync.Fori, group)
        sp.wait_ge(s_mv3, NG)
        nc.sync.dma_start(xf_all[:, GB * (NG - 1):NB, 0:C], xf).then_inc(s_xfc, 16)
        attention_done(sp)
        nc.sync.dma_start(dig, d["digits"]).then_inc(s_dig, 16)
        experts_sync(sp)

    @block.gpsimd
    def _(pool):
        link = Chain(pool, s_pool)
        link(nc.gpsimd.memset(hpre[0:HC, 0:2 * ROW + 2 * C], 0.0))
        nc.gpsimd.iota(fill[:, :, ROW - 1].bitcast(I32), pattern=[[HC, 2]], base=TOKENS,
                       channel_multiplier=1).then_inc(s_filled, 1)
        nc.gpsimd.iota(xf_all[:, :, ROW - 1].bitcast(I32), pattern=[[T, NB]], base=0,
                       channel_multiplier=1).then_inc(s_filled, 1)
        nc.gpsimd.memset(half_pow[:, 0:4], -0.5)
        link(nc.gpsimd.memset(half_pow[:, 4:8], 0.5))

        def ln1_rstd(n):
            wait(pool, s_mv1, n + 1)
            plain(pool)
            link(nc.gpsimd.tensor_scalar(tmp4, mv1[:, :, 1], 1e-5, None, ALU.add))
            signal(pool, nc.gpsimd.tensor_tensor(rs1, tmp4, half_pow[:, 0:4], ALU.pow), s_rs1, n + 1)

        def add_bias(n, par):
            wait(pool, s_xn, n + 1)
            pool.wait_ge(s_gate, 2)
            nc.gpsimd.tensor_tensor(xin[par], xin[par], gbo.unsqueeze(1).to_broadcast([T, GB, C]),
                                    ALU.add).then_inc(s_xb, 1)

        def rope(n, par, z):
            wait(pool, s_rot, 4 * n + z + 1)
            link(nc.gpsimd.tensor_tensor(prot[z % 2].rearrange("p (b t) -> p b t", b=GB),
                                         prot[z % 2].rearrange("p (b t) -> p b t", b=GB),
                                         tab[:, TAB["sin"]].unsqueeze(1).to_broadcast([128, GB, T]), ALU.mult))
            if z < 2:
                wait(pool, s_kz, 2 * n + z - 1)
                dst = kraw[z]
            else:
                wait(pool, s_s, GU * (n - 1))
                dst = qt[par][:, z - 2, :]
            nc.gpsimd.tensor_tensor(dst, pcos[z % 2], prot[z % 2], ALU.add).then_inc(s_rope, 1)

        def ln2_rstd(r):
            wait(pool, s_ln2, r + 1)
            plain(pool)
            link(nc.gpsimd.tensor_scalar(tmp4, mv2[:, :, 1], 1e-5, None, ALU.add))
            signal(pool, nc.gpsimd.tensor_tensor(rs2, tmp4, half_pow[:, 0:4], ALU.pow), s_rs2, r + 1)

        def router_stats(r):
            wait(pool, s_mv3, r + 1)
            plain(pool)
            link(nc.gpsimd.tensor_scalar(tmp4, mv3[:, :, 1], float(C) / (C - 1), None, ALU.mult))
            link(nc.gpsimd.tensor_tensor(st[:, :, 1], tmp4, half_pow[:, 4:8], ALU.pow))
            link(nc.gpsimd.tensor_tensor(tmp4, mv3[:, :, 0], mv3[:, :, 0], ALU.mult))
            link(nc.gpsimd.tensor_tensor(tmp4, tmp4, mv3[:, :, 1], ALU.add), plain)
            link(nc.gpsimd.tensor_scalar(tmp4, tmp4, float(C), None, ALU.mult))
            signal(pool, nc.gpsimd.tensor_tensor(st[:, :, 4], tmp4, half_pow[:, 4:8], ALU.pow), s_st, r + 1)

        def group(g, par, front, route):
            if route:
                ln2_rstd(g - 1)
            if front:
                ln1_rstd(g + 1)
            if route:
                router_stats(g - 1)
            if front:
                add_bias(g + 1, 1 - par)
                for z in range(4):
                    rope(g + 1, 1 - par, z)

        ln1_rstd(0)
        pool.wait_ge(s_tab, 16)
        add_bias(0, 0)
        for z in range(4):
            rope(0, 0, z)
        groups(nc.gpsimd.Fori, group, link, POOL_LINKS)
        ln2_rstd(NG - 1)
        router_stats(NG - 1)
        experts_pool(pool, link)

    @block.scalar
    def _(act):
        act.wait_ge(s_gl, 16)
        nc.scalar.activation(gates[:, 0:2], gates[:, 0:2], ACT.Tanh).then_inc(s_gate, 1)
        act.wait_ge(s_const, 16 * 11)
        act.wait_ge(s_tab, 16)

        def read(bank, g, k):
            wait(act, s_m[bank], m_base(g) + k + 1)

        def item(g, n, par, what, j, bank, k):
            src = banks[BM[bank]]
            read(bank, g, k)
            if what == "X":
                if j == 0:
                    wait(act, s_proj, 4 * n)
                nc.scalar.copy(xnt[:, :, j * T:(j + 1) * T],
                               src[:, 0:2 * T].rearrange("p (c t) -> p c t", c=2)).then_inc(s_xnt, 1)
                act.wait_ge(s_xnt, 4 * n + j + 1)
                act.sem_inc(s_mf[bank], 1)
            elif what in "KQ":
                z = j + (2 if what == "Q" else 0)
                wait(act, s_rot, 4 * n + z - 1)
                nc.scalar.activation(proj[z % 2], src[:, 0:NT], ACT.Identity,
                                     bias=bqk[:, z:z + 1]).then_inc(s_proj, 1)
                act.wait_ge(s_proj, 4 * n + z + 1)
                act.sem_inc(s_mf[bank], 1)
            elif what == "T":
                r = g - 1
                nc.scalar.copy(xft, src[:, 0:2 * T].rearrange("p (c t) -> p c t", c=2))
                nc.scalar.copy(stt, src[0:NST, 2 * T:3 * T]).then_inc(s_xft, 1)
                act.wait_ge(s_xft, 4 * r + j + 1)
                act.sem_inc(s_mf[bank], 1)
            elif what == "A":
                wait(act, s_x1, GB * g + j)
                nc.scalar.copy(attt, src[:, 0:2 * T].rearrange("p (c t) -> p c t", c=2)).then_inc(s_attt, 1)
                act.wait_ge(s_attt, GB * g + j + 1)
                act.sem_inc(s_mf[bank], 1)
            elif what == "H":
                r = g - 1
                if j == 0:
                    act.wait_ge(s_fo, 16 * (NE + 1))
                nc.scalar.activation(hpre[:, bass.ds((GB * r + j) * T, T)], src[:, 0:T], ACT.Identity,
                                     bias=r1b[:, 0:1]).then_inc(s_mf[bank], 1)

        def keys(n, par, z):
            wait(act, s_rope, 4 * n + z + 1)
            wait(act, s_s, GU * (n - 1))
            nc.scalar.mul(kz[par][:, z, 0, :], kraw[z], tab[:, TAB["parity"]][:, 0:1])
            nc.scalar.mul(kz[par][:, z, 1, :], kraw[z], tab[:, TAB["parity"]][:, 1:2]).then_inc(s_kz, 1)

        def group(g, par, front, route):
            todo = [x for x in items(front, route) if x[1] not in "VO"]
            for s in range(STEPS):
                if s < GU:
                    wait(act, s_mx, GU * g + s + 1)
                    wait(act, s_ptr, GU * g + s - 2 if s >= 3 else GU * g)
                    for j in range(HU):
                        last = nc.scalar.activation(pr[s % 3][:, j, :], banks[BS[s % 3]][0:T, j * T:(j + 1) * T],
                                                    ACT.Exp, bias=nmx[s % 3][:, j:j + 1], scale=DH ** -0.5)
                    last.then_inc(s_exp, 1)
                u = s - 2
                if 0 <= u < GU and u % 2 == 1:
                    wait(act, s_ptr, GU * g + u + 1)
                    wait(act, s_pv, GU * g + u - 1)
                    nc.scalar.copy(prt[1].rearrange("p a b -> p (a b)"),
                                   banks[BT[1]][0:T, 0:HU * T]).then_inc(s_pte[1], 1)
                for st_, what, j, bank, k in todo:
                    if st_ == s:
                        item(g, g + 1, 1 - par, what, j, bank, k)
                if front and s in KEYS:
                    keys(g + 1, 1 - par, KEYS.index(s))

        for _, what, j, bank, k in items(True, False, False):
            if what != "V":
                item(-1, 0, 0, what, j, bank, k)
            if what == "Q":
                keys(0, 0, j)
        groups(nc.scalar.Fori, group)
        for _, what, j, bank, k in items(False, True, False):
            item(NG, NG + 1, 0, what, j, bank, k)
        routing_scalar(act)
        experts_scalar(act)

    @block.vector
    def _(dve):
        link = Chain(dve, s_dve)
        for par in range(2):
            nc.vector.memset(vx[par], 1.0).then_inc(s_setup, 1)
        dve.wait_ge(s_tab, 16)
        nc.vector.tensor_copy(identb, tab[0:T, TAB["ident"]][:, 0:T]).then_inc(s_setup, 1)
        nc.vector.tensor_copy(causalb, tab[0:T, TAB["causal"]]).then_inc(s_setup, 1)
        dve.wait_ge(s_setup, 4)
        dve.wait_ge(s_gate, 1)
        dve.wait_ge(s_const, 16 * 11)
        nc.vector.tensor_scalar(gates[:, 2:3], gates[:, 1:2], 0.5, None, ALU.mult).then_inc(s_setup, 1)
        nc.vector.tensor_scalar(gbo, gbo, gates[0:T, 0:1], None, ALU.mult).then_inc(s_gate, 1)

        def ln1_stats(n, par, loads):
            wait(dve, s_xin[par], 16 * loads)
            wait(dve, s_xn, n)
            for b in range(GB):
                link(nc.vector.bn_stats(bns, xin[par][:, b, :]), plain)
                link(nc.vector.bn_aggr(mv1[:, b, :], bns))
            dve.sem_inc(s_mv1, 1)

        def ln1_apply(n, par):
            wait(dve, s_rs1, n + 1)
            wait(dve, s_xnt, 4 * n)
            for b in range(GB):
                last = nc.vector.tensor_scalar(xn[:, b, :], xin[par][:, b, :], mv1[:, b, 0:1], rs1[:, b:b + 1],
                                               ALU.subtract, ALU.mult)
            signal(dve, last, s_xn, n + 1)

        def rotate(n, z):
            wait(dve, s_proj, 4 * n + z + 1)
            wait(dve, s_rope, 4 * n + z - 1)
            nc.vector.tensor_tensor(pcos[z % 2].rearrange("p (b t) -> p b t", b=GB),
                                    proj[z % 2].rearrange("p (b t) -> p b t", b=GB),
                                    tab[:, TAB["cos"]].unsqueeze(1).to_broadcast([128, GB, T]), ALU.mult)
            nc.vector.stream_shuffle(prot[z % 2], proj[z % 2],
                                     mask=[i + DH // 2 if i % DH < DH // 2 else i - DH // 2
                                           for i in range(32)]).then_inc(s_rot, 1)

        def values(g, n, par, j, bank, k):
            wait(dve, s_m[bank], m_base(g) + k + 1)
            wait(dve, s_pv, GU * (n - 1))
            nc.vector.tensor_tensor(vx[par][:, j, :, 0:DH],
                                    banks[BM[bank]][0:T, 0:C].rearrange("p (h d) -> p h d", h=NH),
                                    bvb.rearrange("p (h d) -> p h d", h=NH), ALU.add).then_inc(s_v, 1)
            dve.wait_ge(s_v, 4 * n + j + 1)
            dve.sem_inc(s_mf[bank], 1)

        def residual(g, par, b, bank, k):
            wait(dve, s_m[bank], m_base(g) + k + 1)
            wait(dve, s_xb, g + 1)
            if b == 0:
                wait(dve, s_xout, 16 * g)
            signal(dve, nc.vector.scalar_tensor_tensor(x1[:, b, :], banks[BM[bank]][0:T, 0:C], gates[0:T, 0:1],
                                                       xin[par][:, b, :], ALU.mult, ALU.add),
                   s_x1, GB * g + b + 1)
            dve.sem_inc(s_mf[bank], 1)
            link(nc.vector.bn_stats(bns, x1[:, b, :]), plain)
            link(nc.vector.bn_aggr(mv2[:, b, :], bns))
            if b == GB - 1:
                dve.sem_inc(s_ln2, 1)

        def ln2_apply(r):
            wait(dve, s_rs2, r + 1)
            for b in range(GB):
                link(nc.vector.tensor_scalar(xf[:, b, :], x1[:, b, :], mv2[:, b, 0:1], rs2[:, b:b + 1],
                                             ALU.subtract, ALU.mult))

        def xf_stats(r):
            for b in range(GB):
                link(nc.vector.bn_stats(bns, xf[:, b, :]), plain)
                link(nc.vector.bn_aggr(mv3[:, b, :], bns))
            nc.vector.tensor_copy(st[:, :, 0], mv3[:, :, 0])
            nc.vector.tensor_reduce(st[:, :, 2], xf, X, ALU.min)
            nc.vector.tensor_reduce(st[:, :, 3], xf, X, ALU.max)
            for b in range(GB):
                link(nc.vector.tensor_scalar(spj, xf[:, b, :], 1e-6, None, ALU.is_lt))
                link(nc.vector.scalar_tensor_tensor(spj, xf[:, b, :], -1e-6, spj, ALU.is_gt, ALU.mult,
                                                    accum_out=st[:, b, 5:6]))
            nc.vector.tensor_scalar(st[:, :, 5], st[:, :, 5], 1.0 / C, None, ALU.mult).then_inc(s_mv3, 1)

        def group(g, par, front, route, loads):
            todo = [x for x in items(front, route) if x[1] in "VO"]
            for s in range(STEPS):
                if s < GU:
                    wait(dve, s_s, GU * g + s + 1)
                    link(nc.vector.tensor_reduce(mx[s % 3], banks[BS[s % 3]][0:T, 0:HU * T].rearrange(
                        "p (h k) -> p h k", h=HU), X, ALU.max))
                    nc.vector.tensor_scalar(nmx[s % 3], mx[s % 3], -(DH ** -0.5), None, ALU.mult).then_inc(s_mx, 1)
                u = s - 2
                if 0 <= u < GU and u % 2 == 0:
                    wait(dve, s_ptr, GU * g + u + 1)
                    wait(dve, s_pv, GU * g + u - 1 if u >= 2 else GU * g)
                    nc.vector.tensor_copy(prt[0].rearrange("p a b -> p (a b)"),
                                          banks[BT[0]][0:T, 0:HU * T]).then_inc(s_pte[0], 1)
                if s in ATT_STEPS:
                    b = ATT_STEPS.index(s)
                    wait(dve, s_pv, GU * g + NU * (b + 1))
                    ov = banks[BO][0:T, 0:NH * VE].rearrange("p (h e) -> p h e", h=NH)
                    link(nc.vector.reciprocal(rden, ov[:, :, DH]))
                    nc.vector.tensor_tensor(att.rearrange("p (h e) -> p h e", h=NH), ov[:, :, 0:DH],
                                            rden.unsqueeze(2).to_broadcast([T, NH, DH]), ALU.mult).then_inc(s_att, 1)
                if front and s == 2:
                    ln1_stats(g + 1, 1 - par, loads)
                if route and s == 1:
                    ln2_apply(g - 1)
                if front and s == 4:
                    ln1_apply(g + 1, 1 - par)
                if route and s == 3:
                    xf_stats(g - 1)
                for st_, what, j, bank, k in todo:
                    if st_ == s and what == "V":
                        values(g, g + 1, 1 - par, j, bank, k)
                    elif st_ == s:
                        residual(g, par, j, bank, k)
                if route and s == STEPS - 1:
                    wait(dve, s_xfc, 16 * g)
                if front and s in ROTATE:
                    rotate(g + 1, ROTATE.index(s))

        ln1_stats(0, 0, 1)
        ln1_apply(0, 0)
        for _, w, j, bank, k in items(True, False, False):
            if w == "V":
                values(-1, 0, 0, j, bank, k)
            elif w in "KQ":
                rotate(0, j + (2 if w == "Q" else 0))
        group(0, 0, True, False, 1)
        with nc.vector.Fori(0, (NG - 2) // 2) as i:
            link.enter(i, DVE_LINKS)
            group(2 * i + 1, 1, True, True, i + 2)
            group(2 * i + 2, 0, True, True, i + 2)
            link.leave((NG - 2) // 2)
        group(NG - 1, 1, False, True, 0)
        ln2_apply(NG - 1)
        xf_stats(NG - 1)
        routing_vector(dve, link)
        experts_vector(dve, link)

    @block.tensor
    def _(pe):
        def item(g, n, par, loads, what, j, bank, k):
            out = banks[BM[bank]]
            wait(pe, s_mf[bank], m_base(g) + k)
            if what == "X":
                wait(pe, s_xn, n + 1)
                for c in range(2):
                    last = nc.tensor.transpose(out[:, c * T:(c + 1) * T], xn[:, j, c * 128:(c + 1) * 128],
                                               ident[0:T, 0:T])
            elif what in "KQ":
                if what == "K":
                    pe.wait_ge(s_ctx[par], 16 * loads)
                else:
                    wait(pe, s_xnt, 4 * (n + 1))
                w, src = (wk, ctxt[par]) if what == "K" else (wq, xnt)
                for c in range(2):
                    last = nc.tensor.matmul(out[:, 0:NT], w[:, c, j * 128:(j + 1) * 128], src[:, c, :],
                                            start=(c == 0), stop=(c == 1))
            elif what == "A":
                wait(pe, s_att, GB * g + j + 1)
                for c in range(2):
                    last = nc.tensor.transpose(out[:, c * T:(c + 1) * T], att[:, c * 128:(c + 1) * 128],
                                               ident[0:T, 0:T])
            elif what == "O":
                wait(pe, s_attt, GB * g + j + 1)
                for c in range(2):
                    last = nc.tensor.matmul(out[0:T, 0:C], attt[:, c, :], wo[:, c, :],
                                            start=(c == 0), stop=(c == 1))
            elif what == "V":
                pe.wait_ge(s_ctx[par], 16 * loads)
                for c in range(2):
                    last = nc.tensor.matmul(out[0:T, 0:C], ctxt[par][:, c, j * T:(j + 1) * T], wv[:, c, :],
                                            start=(c == 0), stop=(c == 1))
            elif what == "T":
                wait(pe, s_st, g)
                for c in range(2):
                    nc.tensor.transpose(out[:, c * T:(c + 1) * T], xf[:, j, c * 128:(c + 1) * 128], ident[0:T, 0:T])
                last = nc.tensor.transpose(out[0:NST, 2 * T:3 * T], st[:, j, :], ident[0:T, 0:T])
            elif what == "H":
                wait(pe, s_xft, 4 * (g - 1) + j + 1)
                for c in range(2):
                    nc.tensor.matmul(out[:, 0:T], r1t[:, c, :], xft[:, c, :], start=(c == 0), stop=False)
                last = nc.tensor.matmul(out[:, 0:T], r1s, stt, start=False, stop=True)
            last.then_inc(s_m[bank], 1)

        def scores(g, par, s):
            b, k = s // NU, s % NU
            out = banks[BS[s % 3]]
            if s == 0:
                wait(pe, s_kz, 2 * (g + 1))
                wait(pe, s_rope, 4 * (g + 1))
            wait(pe, s_exp, GU * g + s - 2 if s >= 3 else GU * g)
            nc.tensor.matmul(out[0:T, 0:HU * T], identb, causalb.unsqueeze(1).to_broadcast([T, HU, T]),
                             start=True, stop=False)
            rows = slice(32 * k, 32 * k + 32)
            for t in range(2):
                last = nc.tensor.matmul(out[0:T, t * 2 * T:(t + 1) * 2 * T], qt[par][rows, t, b * T:(b + 1) * T],
                                        kz[par][rows, t, :, b * T:(b + 1) * T], start=False, stop=(t == 1))
            last.then_inc(s_s, 1)

        def turn(g, u):
            wait(pe, s_exp, GU * g + u + 1)
            if u % 2 == 0:
                wait(pe, s_pte[0], GU // 2 * g + u // 2)
            else:
                wait(pe, s_pte[1], GU // 2 * g + u // 2)
            for j in range(HU):
                last = nc.tensor.transpose(banks[BT[u % 2]][0:T, j * T:(j + 1) * T], pr[u % 3][:, j, :],
                                           ident[0:T, 0:T])
            last.then_inc(s_ptr, 1)

        def weigh(g, par, u):
            b, k = u // NU, u % NU
            if u == 0:
                wait(pe, s_v, 4 * (g + 1))
            if k == 0:
                wait(pe, s_att, GB * g + b)
            wait(pe, s_pte[u % 2], GU // 2 * g + u // 2 + 1)
            for j in range(HU):
                h = 8 * (j // 2) + 2 * k + j % 2
                last = nc.tensor.matmul(banks[BO][0:T, h * VE:(h + 1) * VE], prt[u % 2][:, j, :],
                                        vx[par][:, b, h, :], start=True, stop=True)
            last.then_inc(s_pv, 1)

        def group(g, par, front, route, loads):
            todo = items(front, route)
            for s in range(STEPS):
                if s < GU:
                    scores(g, par, s)
                if 0 <= s - 2 < GU:
                    turn(g, s - 2)
                if 0 <= s - 3 < GU:
                    weigh(g, par, s - 3)
                for st_, what, j, bank, k in todo:
                    if st_ == s:
                        item(g, g + 1, 1 - par, loads, what, j, bank, k)

        pe.wait_ge(s_tab, 16)
        pe.wait_ge(s_const, 16 * 11)
        pe.wait_ge(s_setup, 4)
        for _, what, j, bank, k in items(True, False, False):
            item(-1, 0, 0, 1, what, j, bank, k)
        group(0, 0, True, False, 1)
        with nc.tensor.Fori(0, (NG - 2) // 2) as i:
            group(2 * i + 1, 1, True, True, i + 2)
            group(2 * i + 2, 0, True, True, i + 2)
        group(NG - 1, 1, False, True, 0)
        for _, what, j, bank, k in items(False, True, False):
            item(NG, NG + 1, 0, 0, what, j, bank, k)
        routing_tensor(pe)
        experts_tensor(pe)


def kernel(**inputs):
    import concourse.bacc as bacc
    from concourse.bass_utils import run_bass_kernel_spmd

    a = {n: np.asarray(v) for n, v in inputs.items()}
    halves = lambda w: np.ascontiguousarray(w.T.reshape(2, 128, -1).transpose(1, 0, 2))
    up = a["L0_ffn_w_up"].transpose(0, 2, 1).reshape(NE, 2, 128, 2 * INTER).transpose(0, 2, 1, 3).reshape(NE, 128, -1)
    down = a["L0_ffn_w_down"].transpose(0, 2, 1).reshape(NE, KE, 128, C).transpose(0, 2, 1, 3).reshape(NE, 128, -1)
    aup = a["L0_ffn_a_up"].transpose(0, 2, 1).reshape(NGRP, 2, 128, 2 * AINTER).transpose(0, 2, 1, 3)
    adown = a["L0_ffn_a_down"].transpose(0, 2, 1)
    r1 = a["L0_ffn_r1_w"]
    ctx_t = a["ctx_1024"][:, :T].transpose(2, 0, 1).reshape(2, 128, NG, NT).transpose(2, 1, 0, 3)
    arrays = {
        "x": a["x"].reshape(TOKENS, C),
        "ctx": ctx_t,
        "table": table(),
        "digits": digits(),
        "wq": halves(a["L0_xattn_Wq"]), "wk": halves(a["L0_xattn_Wk"]),
        "wv": halves(a["L0_xattn_Wv"]), "wo": halves(a["L0_xattn_Wo"]),
        "bqk": np.concatenate([a["L0_xattn_bk"].reshape(2, 128), a["L0_xattn_bq"].reshape(2, 128)]).T,
        "bv": a["L0_xattn_bv"], "bo": a["L0_xattn_bo"],
        "gates": np.concatenate([a["g_xattn"], a["g_ffn"]]),
        "r1t": halves(r1[:, :C]), "r1s": r1[:, C:].T, "r1b": a["L0_ffn_r1_b"].reshape(HID, 1),
        "r2t": a["L0_ffn_r2_w"].T,
        "w_experts": np.concatenate([up, down], axis=2),
        "w_adapters": np.concatenate([aup.reshape(NGRP, 128, -1), adown], axis=2),
    }
    arrays = {f"{n}_in": np.ascontiguousarray(v) for n, v in arrays.items()}
    nc = bacc.Bacc("TRN2", target_bir_lowering=False, num_devices=1)
    d = {n[:-3]: nc.dram_tensor(n, v.shape, mybir.dt.from_np(v.dtype), kind="ExternalInput").ap()
         for n, v in arrays.items()}
    d["out"] = nc.dram_tensor("rows_out", (TOKENS + CAP, C), F32, kind="ExternalOutput").ap()
    slots = nc.dram_tensor("slots", (NE * CAP, ROW), F32).ap()
    d["slots_flat"] = slots
    d["slots"] = slots.rearrange("(e s p) c -> e p s c", e=NE, s=2)
    build(nc, d)
    r = run_bass_kernel_spmd(nc, [arrays], core_ids=[0])
    return r.results[0]["rows_out"][:TOKENS].reshape(NB, T, C)
```

```python
from contextlib import ExitStack

import numpy as np
import concourse.bass as bass
from concourse import mybir

F32 = mybir.dt.float32
BF16 = mybir.dt.bfloat16
I32 = mybir.dt.int32
ALU = mybir.AluOpType
ACT = mybir.ActivationFunctionType
X = mybir.AxisListType.X

NB, T, C = 32, 112, 256
NH, DH = 16, 16
WINDOW = 128
assert T <= WINDOW
GB = 4
NG = NB // GB
NT = GB * T
HU = 4
NU = NH // HU
GU = GB * NU
VE = DH + 1
NE, NGRP, INTER, AINTER = 32, 16, 512, 128
HID = 128
NST = 6
TOKENS = NB * T
CAP = int(1.25 * TOKENS / NE)
HC = CAP // 2
ROW = C + NE + 1
BIG = float(1 << 20)
NCH, CHB = 4, NB // 4
ROUNDS, DIGITS = 15, 3
KE = INTER // 128
KD = KE + 1
WE_COLS = 2 * 2 * INTER + KE * C
WA_COLS = 2 * 2 * AINTER + C
SCALE = 0.05

TAB = {}
_at = 0
for _name, _n in (("ident", 128), ("cos", T), ("sin", T), ("causal", T), ("lower", T), ("rev", NE),
                  ("slot0", NE), ("parity", 2), ("chunk", 128)):
    TAB[_name] = slice(_at, _at + _n)
    _at += _n
TAB_COLS = _at


def table():
    t = np.zeros((128, TAB_COLS), np.float32)
    t[:, TAB["ident"]] = np.eye(128)
    half = DH // 2
    freq = (1.0 / 10000.0 ** (np.arange(half, dtype=np.float32) / half)).astype(np.float32)
    ang = np.arange(T, dtype=np.float32)[None, :] * freq[:, None]
    row = np.arange(128)
    t[:, TAB["cos"]] = np.cos(ang)[row % half]
    t[:, TAB["sin"]] = np.sin(ang)[row % half] * np.where(row % DH < half, -1.0, 1.0)[:, None]
    q = np.arange(T)
    t[:T, TAB["causal"]] = np.where(q[None, :] > q[:, None], -1e30, 0.0)
    t[:T, TAB["lower"]] = q[:, None] < q[None, :]
    t[:, TAB["rev"]] = NE - np.arange(NE)
    t[:, TAB["slot0"]] = CAP * np.arange(NE) + BIG
    t[:, TAB["parity"]] = (row[:, None] // DH) % 2 == np.arange(2)[None, :]
    t[:, TAB["chunk"]] = (row[:, None] % NE) == (row[None, :] % NE)
    return t


def digits():
    d = np.zeros((128, ROUNDS, DIGITS), np.int32)
    for r in range(ROUNDS):
        d[:, r] = [j << (2 * (ROUNDS - 1 - r)) for j in range(1, DIGITS + 1)]
    return d


def wait(eng, sem, value):
    if not (isinstance(value, int) and value <= 0):
        eng.wait_ge(sem, value)


class Plain:

    def __init__(self, sem):
        self.sem = sem

    def __call__(self, eng):
        eng.sem_inc(self.sem, 1)


class Chain:

    def __init__(self, eng, sem):
        self.eng, self.sem, self.base, self.n = eng, sem, 0, 0

    def __call__(self, ins, then=None):
        self.n += 1
        ins.then_inc(self.sem, 1)
        self.eng.wait_ge(self.sem, self.base + self.n)
        if then:
            then(self.eng)

    def enter(self, trip, per_trip):
        self.outer = self.base + self.n
        self.base, self.n, self.per_trip = self.outer + trip * per_trip, 0, per_trip

    def leave(self, trips):
        assert self.n == self.per_trip, (self.sem, self.n, self.per_trip)
        self.base, self.n = self.outer + trips * self.per_trip, 0


FRONT = [(0, "K", 0), (2, "K", 1), (3, "V", 0), (6, "V", 1), (10, "X", 0), (11, "X", 1), (12, "Q", 0), (13, "Q", 1)]
OUT = sorted([(NU * b + 8, "A", b) for b in range(GB)] + [(NU * b + 9, "O", b) for b in range(GB)])
ROUTE = [(GU + 8, "T", 0), (GU + 9, "T", 1), (GU + 14, "S", 0), (GU + 15, "H", 0)]
KINDS = (FRONT, OUT, ROUTE)
FIRST = (0, 0, 1)
STEPS = GU
TURN, WEIGH, ATT = 2, 3, 3
ROTATE = (1, 3, 13, 14)
LN1_STATS, LN1_APPLY = 8, 9
LN2_APPLY, XF_STATS = 6, {7: "mean", 10: "zeros0", 11: "min", 12: "zeros1", 13: "max"}


def at_step(s, body, own, prev):
    front = body
    found = []
    for kind, items in enumerate(KINDS):
        for n, (when, what, j) in enumerate(items):
            if kind == 0:
                hit, back = front and when == s, -1
            else:
                hit, back = (own and when == s, 0) if when < STEPS else (prev and when - STEPS == s, 1)
            if hit:
                found.append((kind, back, what, j, n))
    return found


def unit_at(s, lag, own, prev):
    u = s - lag
    return [(0, u)] if u >= 0 and own and u < GU else [(1, u + GU)] if u < 0 and prev else []


BS, BT, BO, BM = (0, 1), (2, 3), 4, (5, 6, 7)
POOL_LINKS, DVE_LINKS = 22, 88


def signal(eng, ins, sem, value):
    ins.then_inc(sem, 1)
    eng.wait_ge(sem, value)


def build(nc, d):
    ctx = ExitStack()
    with ctx:
        program(nc, d, ctx)


def program(nc, d, ctx):
    def sb(name, shape, dt=F32):
        return ctx.enter_context(nc.sbuf_tensor(name, shape, dt))

    def sem(name):
        return ctx.enter_context(nc.semaphore(name))

    tab = sb("tab", [128, TAB_COLS])
    ident = tab[:, TAB["ident"]]
    xf_all = sb("xf_all", [T, NB, ROW])
    hpre = sb("hpre", [HID, TOKENS])
    we = [[sb(f"we{s}{j}", [128, WE_COLS]) for j in range(2)] for s in range(2)]
    wa = [sb(f"wa{s}", [128, WA_COLS]) for s in range(2)]
    gates = sb("gates", [128, 4])
    r2t = sb("r2t", [HID, NE])
    banks = [ctx.enter_context(nc.psum_tensor(f"bank{i}", [128, 512], F32)) for i in range(8)]

    ARENA = 25440
    arena = sb("arena", [128, ARENA])
    used = [0]

    def take(parts, shape, dt=F32):
        n = int(np.prod(shape))
        words = n if dt != BF16 else (n + 1) // 2
        a = arena[:, used[0]:used[0] + words]
        used[0] += words
        assert used[0] <= ARENA, used[0]
        a = a if dt == F32 else a.bitcast(dt)
        names = "abcd"[:len(shape)]
        if len(shape) > 1:
            a = a.rearrange(f"p ({' '.join(names)}) -> p {' '.join(names)}", **dict(zip(names, shape)))
        return a[0:parts]

    wq, wk, wv, wo = (take(128, [2, C]) for _ in range(4))
    bqk = take(128, [4])
    bvb, gbo = take(T, [C]), take(T, [C])
    r1t, r1s = take(128, [2, HID]), take(NST, [HID])
    r1b = take(128, [1])
    identb, causalb = take(T, [T], BF16), take(T, [T], BF16)
    ctxt = [take(128, [2, NT]) for _ in range(2)]
    xin = [take(T, [GB, C]) for _ in range(2)]
    half_pow = take(T, [8])
    mv1, mv2, mv3 = (take(T, [GB, 2]) for _ in range(3))
    rs1, rs2, tmp4 = (take(T, [GB]) for _ in range(3))
    bns = take(T, [GB, 6])
    xn = take(T, [GB, C])
    xnt = take(128, [2, NT])
    proj = [take(128, [NT]) for _ in range(2)]
    prot = [take(128, [NT]) for _ in range(2)]
    qt = [take(128, [2, NT]) for _ in range(2)]
    kt = [take(128, [2, NT]) for _ in range(2)]
    kz = [take(128, [2, 8, T]) for _ in range(2)]
    vx = [take(T, [GB, NH, VE]) for _ in range(2)]
    mx = [take(T, [HU]) for _ in range(2)]
    nmx = [take(T, [HU]) for _ in range(2)]
    pr = [take(T, [HU, T]) for _ in range(2)]
    prt = [take(T, [HU, T]) for _ in range(2)]
    rden = take(T, [NH])
    att = take(T, [C])
    attt = take(128, [2, T])
    x1 = take(T, [GB, C])
    xf = take(T, [GB, C])
    st = take(T, [GB, NST])
    xft = we[1][0][:, 0:2 * NT].rearrange("p (c t) -> p c t", c=2)
    stt = we[1][0][0:NST, 2 * NT:3 * NT]
    spj = [we[1][0][0:T, 3 * NT + i * C:3 * NT + (i + 1) * C] for i in range(2)]


    used[0] = 0
    prb, w0, w1, h1, h2 = (take(T, [NB, NE]) for _ in range(5))
    sc = take(T, [CHB, NCH, NE])
    sc_flat = sc.rearrange("p j c e -> p (j c e)")
    sc_turned = sc.rearrange("p j c e -> p c j e")
    col = [take(T, [NB]) for _ in range(8)]
    se = take(128, [CHB * T])
    sej = take(128, [CHB * T])
    vb = take(128, [1 + DIGITS])
    cand = take(128, [DIGITS])
    cnt = take(128, [DIGITS])
    dig = take(128, [ROUNDS, DIGITS], I32)
    thd, thr, cgt = take(NE, [NE]), take(T, [NE]), take(T, [NE])
    ge = take(T, [2, NB, NE], BF16)
    inc = [take(T, [2, NB + 1, NE], BF16) for _ in range(2)]
    lowb, onesb = take(T, [T], BF16), take(T, [T], BF16)
    ones = take(128, [T])
    dest = take(T, [2, NB], I32)


    used[0] = 0
    xr = [take(HC, [2, ROW]) for _ in range(4)]
    xet = [take(128, [2, CAP]) for _ in range(2)]
    th = [take(128, [CAP]) for _ in range(2)]
    gs = [take(128, [CAP]) for _ in range(2)]
    hh = [take(128, [KD, CAP]) for _ in range(2)]
    yt = [take(128, [2, CAP]) for _ in range(2)]
    yr = [take(HC, [2, C]) for _ in range(2)]
    fill = hpre[0:HC, 0:2 * ROW].rearrange("p (s c) -> p s c", s=2)
    zero = hpre[0:HC, 2 * ROW:2 * ROW + 2 * C].rearrange("p (s c) -> p s c", s=2)

    s_tab, s_const, s_filled, s_gl = sem("tables_in"), sem("weights_in"), sem("filling_made"), sem("gates_in")
    s_fo = sem("filling_out")
    s_setup, s_gate = sem("vector_setup"), sem("gates_ready")
    s_xin = [sem("x_in0"), sem("x_in1")]
    s_ctx = [sem("ctx_in0"), sem("ctx_in1")]
    s_mv1, s_rs1, s_xn, s_xnt = sem("mean1"), sem("rstd1"), sem("xn_ready"), sem("xnt_ready")
    s_xb = sem("bias_added")
    s_m = [sem("front_written"), sem("out_written"), sem("route_written")]
    s_mf = [sem("front_read"), sem("out_read"), sem("route_read")]
    s_proj, s_rot, s_rope, s_kz, s_v = (sem(n) for n in ("proj_ready", "rotated", "roped", "kz_ready", "v_ready"))
    s_s, s_mx, s_exp, s_ptr = sem("scores_ready"), sem("max_ready"), sem("exp_ready"), sem("probs_turned")
    s_pte = [sem("prt_even"), sem("prt_odd")]
    s_pv, s_att, s_attt, s_x1 = (sem(n) for n in ("pv_done", "att_ready", "attt_ready", "x1_ready"))
    s_ln2, s_rs2, s_mv3, s_st, s_xout, s_xfc = (sem(n) for n in (
        "ln2_stats", "rstd2", "xf_stats", "stats_ready", "x1_stored", "xf_kept"))
    s_xft, s_ln2a = sem("xft_ready"), sem("xf_ready")
    s_zeros = sem("zeros_ready")
    s_dve, s_act, s_pool = sem("vector_chain"), sem("scalar_chain"), sem("pool_chain")

    x_rows = d["x"].rearrange("(n p) c -> p n c", p=T)
    o_rows = d["out"][0:TOKENS, :].rearrange("(n p) c -> p n c", p=T)
    block = ctx.enter_context(nc.Block())

    plain = Plain(sem("waits_carried"))
    GV = {}
    for s, per in ((s_mv1, 1), (s_rs1, 1), (s_xn, 1), (s_xb, 1), (s_xnt, 2), (s_proj, 4), (s_rot, 4),
                   (s_rope, 4), (s_kz, 4 * GB), (s_v, 2), (s_s, GU), (s_mx, GU), (s_exp, GU), (s_ptr, GU),
                   (s_pte[0], GU // 2), (s_pte[1], GU // 2), (s_pv, GU), (s_att, GB),
                   (s_attt, GB), (s_x1, GB), (s_ln2, 1), (s_ln2a, 1), (s_rs2, 1), (s_mv3, 1), (s_st, 1),
                   (s_xft, 3), (s_xout, 16), (s_xfc, 16)):
        GV[s] = per * NG
    GV[s_xfc] += 1
    for kind in range(3):
        GV[s_m[kind]] = NG * len(KINDS[kind])
        GV[s_mf[kind]] = FIRST[kind] + NG * len(KINDS[kind])

    def attention_done(eng):
        for s, v in GV.items():
            eng.wait_ge(s, v)

    def groups(eng_fori, body, chain=None, per_trip=0):
        body(-1, 1, True, False, False)
        body(0, 0, True, True, False)
        with eng_fori(0, (NG - 2) // 2) as i:
            if chain:
                chain.enter(i, per_trip)
            body(2 * i + 1, 1, True, True, True, i + 2)
            body(2 * i + 2, 0, True, True, True, i + 2)
            if chain:
                chain.leave((NG - 2) // 2)
        body(NG - 1, 1, False, True, True)
        body(NG, 0, False, False, True)

    w_sem = [sem("experts_in0"), sem("experts_in1")]
    s_pair = sem("pair_done")
    s_xs, s_xr = sem("rows_dispatched"), [sem(f"xr_in{i}") for i in range(4)]
    s_added = sem("rows_added")

    def load_pair(p, slot):
        for j in range(2):
            nc.sync.dma_start(we[slot][j][:], d["w_experts"][2 * p + j]).then_inc(w_sem[slot], 16)
        nc.sync.dma_start(wa[slot][:], d["w_adapters"][p]).then_inc(w_sem[slot], 16)

    s_h, s_lg, s_sub, s_e = sem("gelu_ready"), sem("logits_ready"), sem("logits_shifted"), sem("exp_of_logits")
    s_dig, s_ones, s_scr, s_set = sem("digits_in"), sem("ones_ready"), sem("scores_by_token"), sem("scores_turned")
    s_cnt, s_tot, s_thd, s_thr = sem("chunk_counts"), sem("totals"), sem("thresholds"), sem("thresholds_spread")
    s_ge, s_inc, s_slot, s_dest = sem("compared"), sem("prefix_ready"), sem("slots_counted"), sem("destinations")
    HG = TOKENS // GB // 2

    def routing_scalar(act):
        attention_done(act)
        for g in range(NG):
            nc.scalar.activation(hpre[:, g * HG:(g + 1) * HG], hpre[:, g * HG:(g + 1) * HG], ACT.Gelu).then_inc(s_h, 1)
        act.wait_ge(s_sub, 1)
        nc.scalar.activation(w0, w0, ACT.Exp).then_inc(s_e, 1)
        act.wait_ge(s_set, 1)
        nc.scalar.copy(se[:, 0:GB * T], banks[2][:, 0:GB * T])
        nc.scalar.copy(se[:, GB * T:], banks[3][:, 0:GB * T]).then_inc(s_set, 1)

    def routing_tensor(pe):
        attention_done(pe)
        for b in range(NB):
            pe.wait_ge(s_h, b // GB + 1)
            last = nc.tensor.matmul(banks[b // 16][0:T, (b % 16) * NE:(b % 16 + 1) * NE],
                                    hpre[:, b * T:(b + 1) * T], r2t[:], start=True, stop=True)
        last.then_inc(s_lg, 1)
        pe.wait_ge(s_scr, 1)
        for j in range(CHB):
            last = nc.tensor.transpose(banks[2 + j // GB][:, (j % GB) * T:(j % GB + 1) * T],
                                       sc_flat[:, j * 128:(j + 1) * 128], ident[0:T, 0:T])
        last.then_inc(s_set, 1)
        with nc.tensor.Fori(0, ROUNDS) as r:
            pe.wait_ge(s_cnt, r + 1)
            nc.tensor.matmul(banks[4][:, 0:DIGITS], tab[:, TAB["chunk"]], cnt, start=True, stop=True).then_inc(s_tot, 1)
        pe.wait_ge(s_thd, 1)
        nc.tensor.matmul(banks[5][0:T, 0:NE], ones[0:NE], thd, start=True, stop=True).then_inc(s_thr, 1)
        pe.wait_ge(s_ge, 1)
        pe.wait_ge(s_inc, 1)
        for w in range(2):
            for q in range(2):
                out = banks[2 * w + q][0:T, :]
                nc.tensor.matmul(out, lowb, ge[:, w, q * 16:(q + 1) * 16, :], start=True, stop=False)
                nc.tensor.matmul(out, onesb, inc[1][:, w, q * 16:(q + 1) * 16, :], start=False, stop=True)
        nc.tensor.matmul(banks[6][0:T, 0:NE], onesb, inc[1][:, 0, NB, :], start=True, stop=True).then_inc(s_slot, 1)

    def routing_vector(dve, link):
        attention_done(dve)
        over_b = lambda a: a.unsqueeze(1).to_broadcast([T, NB, NE])
        over_e = lambda a: a.unsqueeze(2).to_broadcast([T, a.shape[1], NE])
        rev = over_b(tab[0:T, TAB["rev"]])
        nc.vector.memset(ones, 1.0).then_inc(s_ones, 1)
        nc.vector.memset(onesb, 1.0).then_inc(s_ones, 1)
        nc.vector.tensor_copy(lowb, tab[0:T, TAB["lower"]]).then_inc(s_ones, 1)
        nc.vector.memset(vb[:, 0:1], 0.0)
        for i in range(2):
            link(nc.vector.memset(inc[i][:, :, 0, :], 0.0))
        dve.wait_ge(s_lg, 1)
        for q in range(2):
            lg = banks[q][0:T, :].rearrange("p (b e) -> p b e", e=NE)
            link(nc.vector.tensor_reduce(col[0][:, q * 16:(q + 1) * 16], lg, X, ALU.max))
            link(nc.vector.tensor_tensor(w0[:, q * 16:(q + 1) * 16, :], lg, over_e(col[0][:, q * 16:(q + 1) * 16]),
                                         ALU.subtract))
        dve.sem_inc(s_sub, 1)
        dve.wait_ge(s_e, 1)
        link(nc.vector.tensor_reduce(col[1], w0, X, ALU.add))
        link(nc.vector.reciprocal(col[2], col[1]))
        link(nc.vector.tensor_tensor(prb, w0, over_e(col[2]), ALU.mult))

        def choose(values, top, hit):
            link(nc.vector.tensor_reduce(top, values, X, ALU.max))
            link(nc.vector.tensor_tensor(w1, values, over_e(top), ALU.is_equal))
            link(nc.vector.tensor_tensor(w1, w1, rev, ALU.mult))
            link(nc.vector.tensor_reduce(col[3], w1, X, ALU.max))
            link(nc.vector.tensor_tensor(hit, w1, over_e(col[3]), ALU.is_equal))

        choose(prb, col[4], h1)
        link(nc.vector.scalar_tensor_tensor(w0, h1, -2.0, prb, ALU.mult, ALU.add))
        choose(w0, col[5], h2)
        link(nc.vector.tensor_tensor(w1, h1, h2, ALU.add))
        link(nc.vector.tensor_tensor(w0, prb, w1, ALU.mult))
        link(nc.vector.tensor_scalar(w1, w1, -1.0, None, ALU.add))
        link(nc.vector.tensor_tensor(sc_turned, w0, w1, ALU.add))
        dve.sem_inc(s_scr, 1)
        link(nc.vector.tensor_tensor(col[6], col[4], col[5], ALU.add))
        link(nc.vector.reciprocal(col[7], col[6]))
        link(nc.vector.tensor_scalar(col[7], col[7], gates[0:T, 2:3], None, ALU.mult))
        link(nc.vector.tensor_tensor(col[4], col[4], col[7], ALU.mult))
        link(nc.vector.tensor_tensor(col[5], col[5], col[7], ALU.mult))
        link(nc.vector.tensor_tensor(w0, h1, over_e(col[4]), ALU.mult))
        link(nc.vector.tensor_tensor(w1, h2, over_e(col[5]), ALU.mult))
        link(nc.vector.tensor_tensor(xf_all[:, :, C:C + NE], w0, w1, ALU.add))
        dve.wait_ge(s_dig, 16)
        dve.wait_ge(s_set, 2)
        per = DIGITS + 3
        with nc.vector.Fori(0, ROUNDS) as r:
            link.enter(r, per)
            link(nc.vector.tensor_tensor(cand.bitcast(I32), dig[:, r, :],
                                         vb[:, 0:1].bitcast(I32).to_broadcast([128, DIGITS]), ALU.bitwise_or))
            for j in range(DIGITS):
                link(nc.vector.tensor_scalar(sej, se, cand[:, j:j + 1], None, ALU.is_ge, ALU.add,
                                             accum_out=cnt[:, j:j + 1]))
            dve.sem_inc(s_cnt, 1)
            dve.wait_ge(s_tot, r + 1)
            link(nc.vector.scalar_tensor_tensor(vb[:, 1:1 + DIGITS], banks[4][:, 0:DIGITS], float(CAP), cand,
                                                ALU.is_ge, ALU.mult))
            link(nc.vector.tensor_reduce(vb[:, 0:1], vb, X, ALU.max))
            link.leave(ROUNDS)
        link(nc.vector.tensor_scalar(thd, ident[0:NE, 0:NE], vb[0:NE, 0:1], None, ALU.mult))
        dve.sem_inc(s_thd, 1)
        dve.wait_ge(s_thr, 1)
        link(nc.vector.tensor_copy(thr, banks[5][0:T, 0:NE]))
        tb = thr.unsqueeze(1).unsqueeze(1).to_broadcast([T, NCH, CHB, NE])
        for w, op in ((0, ALU.is_gt), (1, ALU.is_equal)):
            for c in range(NCH):
                rows = slice(c * CHB, (c + 1) * CHB)
                link(nc.vector.tensor_tensor(ge[:, w, rows, :], sc[:, :, c, :],
                                             thr.unsqueeze(1).to_broadcast([T, CHB, NE]), op))
        dve.sem_inc(s_ge, 1)
        src, step = ge, 1
        for n in range(5):
            dst = inc[(n + 1) % 2]
            s_ = src[:, :, 1:, :] if n else ge
            link(nc.vector.tensor_copy(dst[:, :, 1:1 + step, :], s_[:, :, 0:step, :]))
            for w in range(2):
                link(nc.vector.tensor_tensor(dst[:, w, 1 + step:, :], s_[:, w, step:, :],
                                             s_[:, w, 0:NB - step, :], ALU.add))
            src, step = dst, 2 * step
        dve.sem_inc(s_inc, 1)
        dve.wait_ge(s_slot, 1)
        link(nc.vector.tensor_copy(cgt, banks[6][0:T, 0:NE]))
        for q in range(2):
            rows = slice(q * 16, (q + 1) * 16)
            pg = banks[q][0:T, :].rearrange("p (b e) -> p b e", e=NE)
            pq = banks[2 + q][0:T, :].rearrange("p (b e) -> p b e", e=NE)
            link(nc.vector.tensor_tensor(w0[:, rows, :], ge[:, 0, rows, :], pg, ALU.mult))
            link(nc.vector.tensor_tensor(w1[:, rows, :], cgt.unsqueeze(1).to_broadcast([T, 16, NE]), pq, ALU.add))
        link(nc.vector.tensor_tensor(w1, w1, ge[:, 1], ALU.mult))
        link(nc.vector.tensor_tensor(w0, w0, w1, ALU.add))
        link(nc.vector.tensor_tensor(w1, ge[:, 0], ge[:, 1], ALU.add))
        link(nc.vector.scalar_tensor_tensor(w1, w1, -BIG, w0, ALU.mult, ALU.add))
        link(nc.vector.tensor_scalar(w0, w0, float(CAP), BIG, ALU.is_ge, ALU.mult))
        link(nc.vector.tensor_tensor(w0, w0, w1, ALU.add))
        link(nc.vector.tensor_tensor(w0, w0, over_b(tab[0:T, TAB["slot0"]]), ALU.add))
        for k, hit in enumerate((h1, h2)):
            link(nc.vector.tensor_tensor(w1, w0, hit, ALU.mult))
            link(nc.vector.tensor_reduce(col[0], w1, X, ALU.add))
            link(nc.vector.tensor_copy(dest[:, k, :], col[0]))
        dve.sem_inc(s_dest, 1)

    s_xet, s_xrt, s_up, s_th, s_hh, s_yt, s_yts, s_yw, s_yr = (sem(n) for n in (
        "xet_ready", "rows_turned", "up_done", "tanh_ready", "hidden_ready", "down_done", "yt_ready",
        "y_turned", "y_ready"))
    s_gs = sem("gated")
    LAST = NE - 4

    def experts_sync(sp):
        def load_rows(e, slot):
            nc.sync.dma_start(xr[slot], d["slots"][e]).then_inc(s_xr[slot], 16)

        sp.wait_ge(s_xs, 16 * 2 * NB)
        for e in range(4):
            load_rows(e, e)
        with nc.sync.Fori(0, NE // 4 - 1) as i:
            for s in range(2):
                sp.wait_ge(s_pair, 2 * i + s + 1)
                load_pair(2 * i + s + 2, s)
                sp.wait_ge(s_added, 32 * (4 * i + 2 * s + 2))
                for j in range(2):
                    load_rows(4 * i + 4 + 2 * s + j, 2 * s + j)

    def experts_pool(pool, link):
        attention_done(pool)
        pool.wait_ge(s_dest, 1)
        pool.wait_ge(s_fo, 16 * (NE + 1))
        slots = d["slots_flat"]
        for b in range(NB):
            for k in range(2):
                nc.gpsimd.indirect_dma_start(slots, bass.IndirectOffsetOnAxis(ap=dest[:, k, b:b + 1], axis=0),
                                             xf_all[:, b, :], None, bounds_check=NE * CAP - 1,
                                             oob_is_err=False).then_inc(s_xs, 16)

        def expert(e, j):
            pool.wait_ge(s_yr, e + 1)
            wait(pool, s_added, 32 * e)
            plain(pool)
            for h in range(2):
                nc.gpsimd.indirect_dma_start(d["out"], bass.IndirectOffsetOnAxis(
                    ap=xr[j][:, h, ROW - 1:ROW].bitcast(I32), axis=0), yr[j % 2][:, h, :], None,
                    compute_op=ALU.add).then_inc(s_added, 16)

        for j in range(4):
            expert(j, j)
        with nc.gpsimd.Fori(1, NE // 4) as i:
            for j in range(4):
                expert(4 * i + j, j)
        pool.wait_ge(s_added, 32 * NE)

    def experts_scalar(act):
        def expert(e, j):
            act.wait_ge(s_xrt, e + 1)
            wait(act, s_up, KD * (e - 1))
            nc.scalar.copy(xet[j % 2].rearrange("p c t -> p (c t)"), banks[4][:, 0:2 * CAP]).then_inc(s_xet, 1)
            for k in range(KD):
                n, m = KD * e + k, KD * j + k
                act.wait_ge(s_up, n + 1)
                wait(act, s_gs, n - 1)
                nc.scalar.activation(th[m % 2], banks[m % 4][:, 0:CAP], ACT.Tanh, scale=0.5).then_inc(s_th, 1)
            act.wait_ge(s_yt, e + 1)
            wait(act, s_yw, e - 1)
            nc.scalar.copy(yt[j % 2][:, 0, :], banks[5][:, 0:CAP])
            nc.scalar.copy(yt[j % 2][:, 1, :], banks[6][:, 0:CAP]).then_inc(s_yts, 1)

        for j in range(4):
            expert(j, j)
        with nc.scalar.Fori(1, NE // 4) as i:
            for j in range(4):
                expert(4 * i + j, j)

    def experts_vector(dve, link):
        def turned(e, j):
            dve.wait_ge(s_yw, e + 1)
            wait(dve, s_added, 32 * (e - 1))
            for h in range(2):
                last = nc.vector.tensor_scalar(yr[j % 2][:, h, :], banks[7][0:HC, h * C:(h + 1) * C],
                                               xr[j][:, h, bass.ds(C + e, 1)], None, ALU.mult)
            last.then_inc(s_yr, 1)

        def expert(e, j):
            for k in range(KD):
                n, m = KD * e + k, KD * j + k
                dve.wait_ge(s_th, n + 1)
                signal(dve, nc.vector.scalar_tensor_tensor(gs[m % 2], th[m % 2], 1.0, banks[m % 4][:, 0:CAP],
                                                           ALU.add, ALU.mult), s_gs, n + 1)
                if k == 0:
                    wait(dve, s_yt, e - 1)
                if k < KE:
                    nc.vector.tensor_tensor(hh[j % 2][:, k, :], gs[m % 2], banks[m % 4][:, CAP:2 * CAP],
                                            ALU.mult).then_inc(s_hh, 1)
                else:
                    nc.vector.scalar_tensor_tensor(hh[j % 2][:, k, :], gs[m % 2], SCALE,
                                                   banks[m % 4][:, CAP:2 * CAP], ALU.mult,
                                                   ALU.mult).then_inc(s_hh, 1)
            turned(e, j)

        for j in range(4):
            expert(j, j)
        with nc.vector.Fori(1, NE // 4) as i:
            for j in range(4):
                expert(4 * i + j, j)

    def experts_tensor(pe):
        def turn_rows(e, j, loads):
            pe.wait_ge(s_xr[j], 16 * loads)
            wait(pe, s_xet, e)
            for c in range(2):
                for h in range(2):
                    last = nc.tensor.transpose(banks[4][:, c * CAP + h * HC:c * CAP + (h + 1) * HC],
                                               xr[j][:, h, c * 128:(c + 1) * 128], ident[0:HC, 0:HC])
            last.then_inc(s_xrt, 1)

        def up(e, j, k):
            n, m = KD * e + k, KD * j + k
            wait(pe, s_hh, n - 3)
            w, width, at = (we[j // 2][j % 2], INTER, k * 128) if k < KE else (wa[j // 2], AINTER, 0)
            for part in range(2):
                for c in range(2):
                    col0 = c * 2 * width + part * width + at
                    last = nc.tensor.matmul(banks[m % 4][:, part * CAP:(part + 1) * CAP], w[:, col0:col0 + 128],
                                            xet[j % 2][:, c, :], start=(c == 0), stop=(c == 1))
            last.then_inc(s_up, 1)

        def down(e, j, k):
            pe.wait_ge(s_hh, KD * e + k + 1)
            if k == 0:
                wait(pe, s_yts, e)
            w, col0 = (we[j // 2][j % 2], 4 * INTER + k * C) if k < KE else (wa[j // 2], 4 * AINTER)
            for o in range(2):
                last = nc.tensor.matmul(banks[5 + o][:, 0:CAP], w[:, col0 + o * 128:col0 + (o + 1) * 128],
                                        hh[j % 2][:, k, :], start=(k == 0), stop=(k == KD - 1))
            if k == KD - 1:
                last.then_inc(s_yt, 1)

        def turn_back(e, j):
            pe.wait_ge(s_yts, e + 1)
            wait(pe, s_yr, e)
            for h in range(2):
                for o in range(2):
                    last = nc.tensor.transpose(banks[7][0:HC, h * C + o * 128:h * C + (o + 1) * 128],
                                               yt[j % 2][:, o, h * HC:(h + 1) * HC], ident)
            last.then_inc(s_yw, 1)

        def four(i, loads, first, last_four):
            for j in range(4):
                e = 4 * i + j
                if j % 2 == 0:
                    pe.wait_ge(w_sem[j // 2], 48 * loads)
                pe.wait_ge(s_xet, e + 1)
                for k in range(KD):
                    up(e, j, k)
                    if k >= 2:
                        down(e, j, k - 2)
                if j < 3:
                    turn_rows(e + 1, j + 1, loads)
                elif not last_four:
                    turn_rows(e + 1, 0, loads + 1)
                down(e, j, KD - 2)
                down(e, j, KD - 1)
                if j % 2 == 1:
                    pe.wait_ge(s_yt, e + 1)
                    pe.sem_inc(s_pair, 1)
                turn_back(e, j)

        turn_rows(0, 0, 1)
        four(0, 1, True, False)
        with nc.tensor.Fori(1, NE // 4 - 1) as i:
            four(i, i + 1, False, False)
        four(NE // 4 - 1, NE // 4, False, True)

    @block.sync
    def _(sp):
        nc.sync.dma_start(xin[0], x_rows[:, 0:GB, :]).then_inc(s_xin[0], 16)
        nc.sync.dma_start(tab[:], d["table"]).then_inc(s_tab, 16)
        nc.sync.dma_start(ctxt[0], d["ctx"][0]).then_inc(s_ctx[0], 16)
        for dst, name in ((wq, "wq"), (wk, "wk"), (wv, "wv"), (wo, "wo"), (bqk, "bqk"), (r1t, "r1t"),
                          (r1s, "r1s"), (r1b, "r1b")):
            nc.sync.dma_start(dst, d[name]).then_inc(s_const, 16)
        nc.sync.dma_start(bvb, d["bv"].partition_broadcast(T)).then_inc(s_const, 16)
        nc.sync.dma_start(gbo, d["bo"].partition_broadcast(T)).then_inc(s_const, 16)
        nc.sync.dma_start(r2t[:], d["r2t"]).then_inc(s_const, 16)
        nc.sync.dma_start(gates[:, 0:2], d["gates"].partition_broadcast(128)).then_inc(s_gl, 16)
        sp.wait_ge(s_filled, 2)
        with nc.sync.Fori(0, NE) as e:
            nc.sync.dma_start(d["slots"][e], fill).then_inc(s_fo, 16)
        nc.sync.dma_start(d["out"][TOKENS:TOKENS + CAP, :].rearrange("(s p) c -> p s c", p=HC),
                          zero).then_inc(s_fo, 16)
        load_pair(0, 0)

        def group(g, par, front, own, prev, _=1):
            if front and own:
                wait(sp, s_v, 2 * g)
                plain(sp)
                wait(sp, s_proj, 4 * g)
                plain(sp)
                nc.sync.dma_start(ctxt[1 - par], d["ctx"][g + 1]).then_inc(s_ctx[1 - par], 16)
            if prev:
                wait(sp, s_x1, GB * g)
                plain(sp)
                nc.sync.dma_start(o_rows[:, bass.ds(GB * (g - 1), GB), :], x1).then_inc(s_xout, 16)
            if front and own:
                wait(sp, s_x1, GB * g)
                plain(sp)
                nc.sync.dma_start(xin[1 - par], x_rows[:, bass.ds(GB * (g + 1), GB), :]).then_inc(s_xin[1 - par], 16)
            if prev:
                wait(sp, s_ln2a, g)
                plain(sp)
                nc.sync.dma_start(xf_all[:, bass.ds(GB * (g - 1), GB), 0:C], xf).then_inc(s_xfc, 16)

        sp.sem_inc(s_xfc, 1)
        groups(nc.sync.Fori, group)
        attention_done(sp)
        load_pair(1, 1)
        nc.sync.dma_start(dig, d["digits"]).then_inc(s_dig, 16)
        experts_sync(sp)

    @block.gpsimd
    def _(pool):
        link = Chain(pool, s_pool)
        link(nc.gpsimd.memset(hpre[0:HC, 0:2 * ROW + 2 * C], 0.0))
        nc.gpsimd.iota(fill[:, :, ROW - 1].bitcast(I32), pattern=[[HC, 2]], base=TOKENS,
                       channel_multiplier=1).then_inc(s_filled, 1)
        nc.gpsimd.iota(xf_all[:, :, ROW - 1].bitcast(I32), pattern=[[T, NB]], base=0,
                       channel_multiplier=1).then_inc(s_filled, 1)
        nc.gpsimd.memset(half_pow[:, 0:4], -0.5)
        link(nc.gpsimd.memset(half_pow[:, 4:8], 0.5))

        def ln1_rstd(n):
            wait(pool, s_mv1, n + 1)
            plain(pool)
            link(nc.gpsimd.tensor_scalar(tmp4, mv1[:, :, 1], 1e-5, None, ALU.add))
            signal(pool, nc.gpsimd.tensor_tensor(rs1, tmp4, half_pow[:, 0:4], ALU.pow), s_rs1, n + 1)

        def add_bias(n, par):
            wait(pool, s_xn, n + 1)
            pool.wait_ge(s_gate, 2)
            signal(pool, nc.gpsimd.tensor_tensor(xin[par], xin[par], gbo.unsqueeze(1).to_broadcast([T, GB, C]),
                                                 ALU.add), s_xb, n + 1)

        def rope(n, par, z):
            wait(pool, s_rot, 4 * n + z + 1)
            link(nc.gpsimd.tensor_tensor(prot[z % 2].rearrange("p (b t) -> p b t", b=GB),
                                         prot[z % 2].rearrange("p (b t) -> p b t", b=GB),
                                         tab[:, TAB["sin"]].unsqueeze(1).to_broadcast([128, GB, T]), ALU.mult))
            if z < 2:
                wait(pool, s_kz, 4 * GB * (n - 1))
                dst = kt[par][:, z, :]
            else:
                wait(pool, s_s, GU * (n - 1))
                dst = qt[par][:, z - 2, :]
            signal(pool, nc.gpsimd.tensor_tensor(dst, proj[z % 2], prot[z % 2], ALU.add), s_rope, 4 * n + z + 1)

        def spread(n, par, b):
            if b == 0:
                wait(pool, s_rope, 4 * n + 2)
            wait(pool, s_s, GU * n + NU * (b - 1))
            for r in range(4):
                rows = slice(32 * r, 32 * r + 32)
                signal(pool, nc.gpsimd.tensor_tensor(
                    kz[b % 2][rows, :, 2 * r:2 * r + 2, :],
                    kt[par][rows, :, b * T:(b + 1) * T].unsqueeze(2).to_broadcast([32, 2, 2, T]),
                    tab[rows, TAB["parity"]].unsqueeze(1).unsqueeze(3).to_broadcast([32, 2, 2, T]),
                    ALU.mult), s_kz, 4 * (GB * n + b) + r + 1)

        def ln2_rstd(r):
            wait(pool, s_ln2, r + 1)
            plain(pool)
            link(nc.gpsimd.tensor_scalar(tmp4, mv2[:, :, 1], 1e-5, None, ALU.add))
            signal(pool, nc.gpsimd.tensor_tensor(rs2, tmp4, half_pow[:, 0:4], ALU.pow), s_rs2, r + 1)

        def router_stats(r):
            wait(pool, s_mv3, r + 1)
            plain(pool)
            link(nc.gpsimd.tensor_scalar(tmp4, mv3[:, :, 1], float(C) / (C - 1), None, ALU.mult))
            link(nc.gpsimd.tensor_tensor(st[:, :, 1], tmp4, half_pow[:, 4:8], ALU.pow))
            link(nc.gpsimd.tensor_tensor(tmp4, mv3[:, :, 0], mv3[:, :, 0], ALU.mult))
            link(nc.gpsimd.tensor_tensor(tmp4, tmp4, mv3[:, :, 1], ALU.add), plain)
            link(nc.gpsimd.tensor_scalar(tmp4, tmp4, float(C), None, ALU.mult))
            signal(pool, nc.gpsimd.tensor_tensor(st[:, :, 4], tmp4, half_pow[:, 4:8], ALU.pow), s_st, r + 1)

        def group(g, par, front, own, prev, _=1):
            if own:
                spread(g, par, 1)
            if front:
                rope(g + 1, 1 - par, 0)
            if own:
                spread(g, par, 2)
            if front:
                rope(g + 1, 1 - par, 1)
            if prev:
                ln2_rstd(g - 1)
            if front:
                ln1_rstd(g + 1)
            if own:
                spread(g, par, 3)
            if front:
                add_bias(g + 1, 1 - par)
            if prev:
                router_stats(g - 1)
            if front:
                spread(g + 1, 1 - par, 0)
                rope(g + 1, 1 - par, 2)
                rope(g + 1, 1 - par, 3)

        for i in range(2):
            nc.gpsimd.memset(kz[i], 0.0).then_inc(s_zeros, 1)
        pool.wait_ge(s_zeros, 2)
        pool.wait_ge(s_tab, 16)
        groups(nc.gpsimd.Fori, group, link, POOL_LINKS)
        experts_pool(pool, link)

    @block.scalar
    def _(act):
        act.wait_ge(s_gl, 16)
        nc.scalar.activation(gates[:, 0:2], gates[:, 0:2], ACT.Tanh).then_inc(s_gate, 1)
        act.wait_ge(s_const, 16 * 11)
        act.wait_ge(s_tab, 16)

        def item(q, par, kind, what, j, n):
            src = banks[BM[kind]]
            wait(act, s_m[kind], len(KINDS[kind]) * q + n + 1)
            if what == "X":
                if j == 0:
                    wait(act, s_proj, 4 * q)
                nc.scalar.copy(xnt[:, :, 2 * j * T:2 * (j + 1) * T],
                               src[:, 0:4 * T].rearrange("p (c t) -> p c t", c=2)).then_inc(s_xnt, 1)
                act.wait_ge(s_xnt, 2 * q + j + 1)
                act.sem_inc(s_mf[kind], 1)
            elif what in "KQ":
                z = j + (2 if what == "Q" else 0)
                wait(act, s_rope, 4 * q + z - 1)
                nc.scalar.activation(proj[z % 2], src[:, 0:NT], ACT.Identity,
                                     bias=bqk[:, z:z + 1]).then_inc(s_proj, 1)
                act.wait_ge(s_proj, 4 * q + z + 1)
                act.sem_inc(s_mf[kind], 1)
            elif what == "T":
                nc.scalar.copy(xft[:, :, 2 * j * T:2 * (j + 1) * T],
                               src[:, 0:4 * T].rearrange("p (c t) -> p c t", c=2)).then_inc(s_xft, 1)
                act.wait_ge(s_xft, 3 * q + j + 1)
                act.sem_inc(s_mf[kind], 1)
            elif what == "S":
                nc.scalar.copy(stt, src[0:NST, 0:NT]).then_inc(s_xft, 1)
                act.wait_ge(s_xft, 3 * q + 3)
                act.sem_inc(s_mf[kind], 1)
            elif what == "A":
                wait(act, s_x1, GB * q + j)
                nc.scalar.copy(attt, src[:, 0:2 * T].rearrange("p (c t) -> p c t", c=2)).then_inc(s_attt, 1)
                act.wait_ge(s_attt, GB * q + j + 1)
                act.sem_inc(s_mf[kind], 1)
            elif what == "H":
                act.wait_ge(s_fo, 16 * (NE + 1))
                nc.scalar.activation(hpre[:, bass.ds(q * NT, NT)], src[:, 0:NT], ACT.Identity,
                                     bias=r1b[:, 0:1]).then_inc(s_mf[kind], 1)

        def group(g, par, front, own, prev, _=1):
            for s in range(STEPS):
                for back, u in unit_at(s, TURN, own, prev):
                    if u % 2 == 1:
                        wait(act, s_ptr, GU * (g - back) + u + 1)
                        wait(act, s_pv, GU * (g - back) + u - 1)
                        nc.scalar.copy(prt[1].rearrange("p a b -> p (a b)"),
                                       banks[BT[1]][0:T, 0:HU * T]).then_inc(s_pte[1], 1)
                if own:
                    wait(act, s_mx, GU * g + s + 1)
                    wait(act, s_ptr, GU * g + s - 1)
                    for j in range(HU):
                        last = nc.scalar.activation(pr[s % 2][:, j, :], banks[BS[s % 2]][0:T, j * T:(j + 1) * T],
                                                    ACT.Exp, bias=nmx[s % 2][:, j:j + 1], scale=DH ** -0.5)
                    last.then_inc(s_exp, 1)
                for kind, back, what, j, n in at_step(s, front, own, prev):
                    if what not in "VO":
                        item(g - back, (par + back) % 2, kind, what, j, n)

        groups(nc.scalar.Fori, group)
        routing_scalar(act)
        experts_scalar(act)

    @block.vector
    def _(dve):
        link = Chain(dve, s_dve)
        for par in range(2):
            nc.vector.memset(vx[par], 1.0).then_inc(s_setup, 1)
        dve.wait_ge(s_tab, 16)
        nc.vector.tensor_copy(identb, tab[0:T, TAB["ident"]][:, 0:T]).then_inc(s_setup, 1)
        nc.vector.tensor_copy(causalb, tab[0:T, TAB["causal"]]).then_inc(s_setup, 1)
        dve.wait_ge(s_setup, 4)
        dve.wait_ge(s_gate, 1)
        dve.wait_ge(s_const, 16 * 11)
        nc.vector.tensor_scalar(gates[:, 2:3], gates[:, 1:2], 0.5, None, ALU.mult).then_inc(s_setup, 1)
        nc.vector.tensor_scalar(gbo, gbo, gates[0:T, 0:1], None, ALU.mult).then_inc(s_gate, 1)

        def ln1_stats(n, par, loads):
            wait(dve, s_xin[par], 16 * loads)
            wait(dve, s_xn, n)
            for b in range(GB):
                last = nc.vector.bn_stats(bns[:, b, :], xin[par][:, b, :])
            link(last, plain)
            for b in range(GB):
                last = nc.vector.bn_aggr(mv1[:, b, :], bns[:, b, :])
            link(last)
            dve.sem_inc(s_mv1, 1)

        def ln1_apply(n, par):
            wait(dve, s_rs1, n + 1)
            wait(dve, s_xnt, 2 * n)
            for b in range(GB):
                last = nc.vector.tensor_scalar(xn[:, b, :], xin[par][:, b, :], mv1[:, b, 0:1], rs1[:, b:b + 1],
                                               ALU.subtract, ALU.mult)
            signal(dve, last, s_xn, n + 1)

        def rotate(n, z):
            wait(dve, s_proj, 4 * n + z + 1)
            wait(dve, s_rope, 4 * n + z - 1)
            plain(dve)
            link(nc.vector.stream_shuffle(prot[z % 2], proj[z % 2],
                                          mask=[i + DH // 2 if i % DH < DH // 2 else i - DH // 2
                                                for i in range(32)]))
            by_sequence = proj[z % 2].rearrange("p (b t) -> p b t", b=GB)
            nc.vector.tensor_tensor(by_sequence, by_sequence,
                                    tab[:, TAB["cos"]].unsqueeze(1).to_broadcast([128, GB, T]),
                                    ALU.mult).then_inc(s_rot, 1)

        def values(q, par, j, kind, n):
            wait(dve, s_m[kind], len(KINDS[kind]) * q + n + 1)
            wait(dve, s_pv, GU * (q - 1))
            nc.vector.tensor_tensor(
                vx[par][:, 2 * j:2 * j + 2, :, 0:DH],
                banks[BM[kind]][0:T, 0:2 * C].rearrange("p (b h d) -> p b h d", b=2, h=NH),
                bvb.rearrange("p (h d) -> p h d", h=NH).unsqueeze(1).to_broadcast([T, 2, NH, DH]),
                ALU.add).then_inc(s_v, 1)
            dve.wait_ge(s_v, 2 * q + j + 1)
            dve.sem_inc(s_mf[kind], 1)

        def residual(q, par, b, kind, n):
            wait(dve, s_m[kind], len(KINDS[kind]) * q + n + 1)
            wait(dve, s_xb, q + 1)
            if b == 0:
                wait(dve, s_xout, 16 * q)
            signal(dve, nc.vector.scalar_tensor_tensor(x1[:, b, :], banks[BM[kind]][0:T, 0:C], gates[0:T, 0:1],
                                                       xin[par][:, b, :], ALU.mult, ALU.add),
                   s_x1, GB * q + b + 1)
            dve.sem_inc(s_mf[kind], 1)
            link(nc.vector.bn_stats(bns[:, b, :], x1[:, b, :]), plain)
            link(nc.vector.bn_aggr(mv2[:, b, :], bns[:, b, :]))
            if b == GB - 1:
                dve.sem_inc(s_ln2, 1)

        def ln2_apply(r):
            wait(dve, s_rs2, r + 1)
            wait(dve, s_xfc, 1 + 16 * r)
            for b in range(GB):
                last = nc.vector.tensor_scalar(xf[:, b, :], x1[:, b, :], mv2[:, b, 0:1], rs2[:, b:b + 1],
                                               ALU.subtract, ALU.mult)
            signal(dve, last, s_ln2a, r + 1)

        def xf_stats(r, part):
            if part == "mean":
                for b in range(GB):
                    last = nc.vector.bn_stats(bns[:, b, :], xf[:, b, :])
                link(last, plain)
                for b in range(GB):
                    last = nc.vector.bn_aggr(mv3[:, b, :], bns[:, b, :])
                link(last)
                link(nc.vector.tensor_copy(st[:, :, 0], mv3[:, :, 0]))
            elif part == "min":
                link(nc.vector.tensor_reduce(st[:, :, 2], xf, X, ALU.min))
            elif part == "max":
                link(nc.vector.tensor_reduce(st[:, :, 3], xf, X, ALU.max))
                dve.sem_inc(s_mv3, 1)
            else:
                two = (0, 1) if part == "zeros0" else (2, 3)
                for b in two:
                    last = nc.vector.tensor_scalar(spj[b % 2], xf[:, b, :], 1e-6, None, ALU.is_lt)
                link(last)
                for b in two:
                    last = nc.vector.scalar_tensor_tensor(spj[b % 2], xf[:, b, :], -1e-6, spj[b % 2], ALU.is_gt,
                                                          ALU.mult, accum_out=st[:, b, 5:6])
                link(last)
                if part == "zeros1":
                    link(nc.vector.tensor_scalar(st[:, :, 5], st[:, :, 5], 1.0 / C, None, ALU.mult))

        def group(g, par, front, own, prev, loads=1):
            for s in range(STEPS):
                for back, u in unit_at(s, WEIGH + ATT + 1, own, prev):
                    if u % NU == 0:
                        wait(dve, s_pv, GU * (g - back) + u + NU)
                        ov = banks[BO][0:T, 0:NH * VE].rearrange("p (h e) -> p h e", h=NH)
                        link(nc.vector.reciprocal(rden, ov[:, :, DH]))
                        nc.vector.tensor_tensor(att.rearrange("p (h e) -> p h e", h=NH), ov[:, :, 0:DH],
                                                rden.unsqueeze(2).to_broadcast([T, NH, DH]),
                                                ALU.mult).then_inc(s_att, 1)
                for back, u in unit_at(s, TURN, own, prev):
                    if u % 2 == 0:
                        wait(dve, s_ptr, GU * (g - back) + u + 1)
                        wait(dve, s_pv, GU * (g - back) + u - 1)
                        nc.vector.tensor_copy(prt[0].rearrange("p a b -> p (a b)"),
                                              banks[BT[0]][0:T, 0:HU * T]).then_inc(s_pte[0], 1)
                if own:
                    wait(dve, s_s, GU * g + s + 1)
                    link(nc.vector.tensor_reduce(mx[s % 2], banks[BS[s % 2]][0:T, 0:HU * T].rearrange(
                        "p (h k) -> p h k", h=HU), X, ALU.max))
                    nc.vector.tensor_scalar(nmx[s % 2], mx[s % 2], -(DH ** -0.5), None, ALU.mult).then_inc(s_mx, 1)
                if front and s == LN1_STATS:
                    ln1_stats(g + 1, 1 - par, loads)
                if prev and s == LN2_APPLY:
                    ln2_apply(g - 1)
                if front and s == LN1_APPLY:
                    ln1_apply(g + 1, 1 - par)
                if prev and s in XF_STATS:
                    xf_stats(g - 1, XF_STATS[s])
                for kind, back, what, j, n in at_step(s, front, own, prev):
                    if what == "V":
                        values(g - back, (par + back) % 2, j, kind, n)
                    elif what == "O":
                        residual(g - back, (par + back) % 2, j, kind, n)
                if front and s in ROTATE:
                    rotate(g + 1, ROTATE.index(s))

        groups(nc.vector.Fori, group, link, DVE_LINKS)
        routing_vector(dve, link)
        experts_vector(dve, link)

    @block.tensor
    def _(pe):
        def item(q, par, loads, kind, what, j, n):
            out = banks[BM[kind]]
            wait(pe, s_mf[kind], FIRST[kind] + len(KINDS[kind]) * q + n)
            if what in "XT":
                rows = xn if what == "X" else xf
                if what == "X":
                    wait(pe, s_xn, q + 1)
                else:
                    wait(pe, s_ln2a, q + 1)
                for c in range(2):
                    for h in range(2):
                        last = nc.tensor.transpose(out[:, (2 * c + h) * T:(2 * c + h + 1) * T],
                                                   rows[:, 2 * j + h, c * 128:(c + 1) * 128], ident[0:T, 0:T])
            elif what in "KQ":
                if what == "K":
                    pe.wait_ge(s_ctx[par], 16 * loads)
                else:
                    wait(pe, s_xnt, 2 * (q + 1))
                w, src = (wk, ctxt[par]) if what == "K" else (wq, xnt)
                for c in range(2):
                    last = nc.tensor.matmul(out[:, 0:NT], w[:, c, j * 128:(j + 1) * 128], src[:, c, :],
                                            start=(c == 0), stop=(c == 1))
            elif what == "A":
                wait(pe, s_att, GB * q + j + 1)
                for c in range(2):
                    last = nc.tensor.transpose(out[:, c * T:(c + 1) * T], att[:, c * 128:(c + 1) * 128],
                                               ident[0:T, 0:T])
            elif what == "O":
                wait(pe, s_attt, GB * q + j + 1)
                for c in range(2):
                    last = nc.tensor.matmul(out[0:T, 0:C], attt[:, c, :], wo[:, c, :],
                                            start=(c == 0), stop=(c == 1))
            elif what == "V":
                pe.wait_ge(s_ctx[par], 16 * loads)
                for h in range(2):
                    for c in range(2):
                        last = nc.tensor.matmul(out[0:T, h * C:(h + 1) * C],
                                                ctxt[par][:, c, (2 * j + h) * T:(2 * j + h + 1) * T], wv[:, c, :],
                                                start=(c == 0), stop=(c == 1))
            elif what == "S":
                wait(pe, s_st, q + 1)
                for b in range(GB):
                    last = nc.tensor.transpose(out[0:NST, b * T:(b + 1) * T], st[:, b, :], ident[0:T, 0:T])
            elif what == "H":
                wait(pe, s_xft, 3 * (q + 1))
                for c in range(2):
                    nc.tensor.matmul(out[:, 0:NT], r1t[:, c, :], xft[:, c, :], start=(c == 0), stop=False)
                last = nc.tensor.matmul(out[:, 0:NT], r1s, stt, start=False, stop=True)
            last.then_inc(s_m[kind], 1)

        def scores(g, par, s):
            b, k = s // NU, s % NU
            out = banks[BS[s % 2]][0:T, 0:HU * T]
            if s == 0:
                wait(pe, s_rope, 4 * (g + 1))
            if k == 0:
                wait(pe, s_kz, 4 * (GB * g + b + 1))
            nc.tensor.matmul(out, identb, causalb.unsqueeze(1).to_broadcast([T, HU, T]), start=True, stop=False)
            t, h = divmod(HU * k, 8)
            nc.tensor.matmul(out, qt[par][:, t, b * T:(b + 1) * T], kz[b % 2][:, t, h:h + HU, :],
                             start=False, stop=True).then_inc(s_s, 1)

        def turn(q, u):
            wait(pe, s_exp, GU * q + u + 1)
            wait(pe, s_pte[u % 2], GU // 2 * q + u // 2)
            for j in range(HU):
                last = nc.tensor.transpose(banks[BT[u % 2]][0:T, j * T:(j + 1) * T], pr[u % 2][:, j, :],
                                           ident[0:T, 0:T])
            last.then_inc(s_ptr, 1)

        def weigh(q, par, u):
            b, k = u // NU, u % NU
            if u == 0:
                wait(pe, s_v, 2 * (q + 1))
            if k == 0:
                wait(pe, s_att, GB * q + b)
            wait(pe, s_pte[u % 2], GU // 2 * q + u // 2 + 1)
            for j in range(HU):
                h = HU * k + j
                last = nc.tensor.matmul(banks[BO][0:T, h * VE:(h + 1) * VE], prt[u % 2][:, j, :],
                                        vx[par][:, b, h, :], start=True, stop=True)
            last.then_inc(s_pv, 1)

        def group(g, par, front, own, prev, loads=1):
            for s in range(STEPS):
                for back, u in unit_at(s, TURN, own, prev):
                    turn(g - back, u)
                if own:
                    scores(g, par, s)
                for kind, back, what, j, n in at_step(s, front, own, prev):
                    item(g - back, (par + back) % 2, loads, kind, what, j, n)
                for back, u in unit_at(s, WEIGH, own, prev):
                    weigh(g - back, (par + back) % 2, u)

        pe.wait_ge(s_tab, 16)
        pe.wait_ge(s_const, 16 * 11)
        pe.wait_ge(s_setup, 4)
        pe.sem_inc(s_mf[2], FIRST[2])
        groups(nc.tensor.Fori, group)
        routing_tensor(pe)
        experts_tensor(pe)


def kernel(**inputs):
    import concourse.bacc as bacc
    from concourse.bass_utils import run_bass_kernel_spmd

    a = {n: np.asarray(v) for n, v in inputs.items()}
    halves = lambda w: np.ascontiguousarray(w.T.reshape(2, 128, -1).transpose(1, 0, 2))
    up = a["L0_ffn_w_up"].transpose(0, 2, 1).reshape(NE, 2, 128, 2 * INTER).transpose(0, 2, 1, 3).reshape(NE, 128, -1)
    down = a["L0_ffn_w_down"].transpose(0, 2, 1).reshape(NE, KE, 128, C).transpose(0, 2, 1, 3).reshape(NE, 128, -1)
    aup = a["L0_ffn_a_up"].transpose(0, 2, 1).reshape(NGRP, 2, 128, 2 * AINTER).transpose(0, 2, 1, 3)
    adown = a["L0_ffn_a_down"].transpose(0, 2, 1)
    r1 = a["L0_ffn_r1_w"]
    ctx_t = a["ctx_1024"][:, :T].transpose(2, 0, 1).reshape(2, 128, NG, NT).transpose(2, 1, 0, 3)
    arrays = {
        "x": a["x"].reshape(TOKENS, C),
        "ctx": ctx_t,
        "table": table(),
        "digits": digits(),
        "wq": halves(a["L0_xattn_Wq"]), "wk": halves(a["L0_xattn_Wk"]),
        "wv": halves(a["L0_xattn_Wv"]), "wo": halves(a["L0_xattn_Wo"]),
        "bqk": np.concatenate([a["L0_xattn_bk"].reshape(2, 128), a["L0_xattn_bq"].reshape(2, 128)]).T,
        "bv": a["L0_xattn_bv"], "bo": a["L0_xattn_bo"],
        "gates": np.concatenate([a["g_xattn"], a["g_ffn"]]),
        "r1t": halves(r1[:, :C]), "r1s": r1[:, C:].T, "r1b": a["L0_ffn_r1_b"].reshape(HID, 1),
        "r2t": a["L0_ffn_r2_w"].T,
        "w_experts": np.concatenate([up, down], axis=2),
        "w_adapters": np.concatenate([aup.reshape(NGRP, 128, -1), adown], axis=2),
    }
    arrays = {f"{n}_in": np.ascontiguousarray(v) for n, v in arrays.items()}
    nc = bacc.Bacc("TRN2", target_bir_lowering=False, num_devices=1)
    d = {n[:-3]: nc.dram_tensor(n, v.shape, mybir.dt.from_np(v.dtype), kind="ExternalInput").ap()
         for n, v in arrays.items()}
    d["out"] = nc.dram_tensor("rows_out", (TOKENS + CAP, C), F32, kind="ExternalOutput").ap()
    slots = nc.dram_tensor("slots", (NE * CAP, ROW), F32).ap()
    d["slots_flat"] = slots
    d["slots"] = slots.rearrange("(e s p) c -> e p s c", e=NE, s=2)
    build(nc, d)
    r = run_bass_kernel_spmd(nc, [arrays], core_ids=[0])
    return r.results[0]["rows_out"][:TOKENS].reshape(NB, T, C)
```

```python
from contextlib import ExitStack

import numpy as np
import concourse.bass as bass
from concourse import mybir

F32 = mybir.dt.float32
BF16 = mybir.dt.bfloat16
I32 = mybir.dt.int32
ALU = mybir.AluOpType
ACT = mybir.ActivationFunctionType
X = mybir.AxisListType.X

NB, T, C = 32, 112, 256
NH, DH = 16, 16
WINDOW = 128
assert T <= WINDOW
GB = 4
NG = NB // GB
NT = GB * T
HU = 4
NU = NH // HU
GU = GB * NU
VE = DH + 1
NE, NGRP, INTER, AINTER = 32, 16, 512, 128
HID = 128
NST = 6
TOKENS = NB * T
CAP = int(1.25 * TOKENS / NE)
HC = CAP // 2
ROW = C + NE + 1
BIG = float(1 << 20)
NCH, CHB = 4, NB // 4
DIGITS, DBITS, ROUNDS, CANDS = 3, 10, 5, 3
WARM = 12
IDLE = {7: 12, 12: 18, 14: 2}
ABOVE = float(2 << DBITS)
KE = INTER // 128
KD = KE + 1
WE_COLS = 2 * 2 * INTER + KE * C
WA_COLS = 2 * 2 * AINTER + C
SCALE = 0.05

TAB = {}
_at = 0
for _name, _n in (("ident", 128), ("cos", T), ("sin", T), ("causal", T), ("lower", T), ("rev", NE),
                  ("slot0", NE), ("parity", 2), ("chunk", 128)):
    TAB[_name] = slice(_at, _at + _n)
    _at += _n
TAB_COLS = _at


def table():
    t = np.zeros((128, TAB_COLS), np.float32)
    t[:, TAB["ident"]] = np.eye(128)
    half = DH // 2
    freq = (1.0 / 10000.0 ** (np.arange(half, dtype=np.float32) / half)).astype(np.float32)
    ang = np.arange(T, dtype=np.float32)[None, :] * freq[:, None]
    row = np.arange(128)
    t[:, TAB["cos"]] = np.cos(ang)[row % half]
    t[:, TAB["sin"]] = np.sin(ang)[row % half] * np.where(row % DH < half, -1.0, 1.0)[:, None]
    q = np.arange(T)
    t[:T, TAB["causal"]] = np.where(q[None, :] > q[:, None], -1e30, 0.0)
    t[:T, TAB["lower"]] = q[:, None] < q[None, :]
    t[:, TAB["rev"]] = NE - np.arange(NE)
    t[:, TAB["slot0"]] = CAP * np.arange(NE) + BIG
    t[:, TAB["parity"]] = (row[:, None] // DH) % 2 == np.arange(2)[None, :]
    t[:, TAB["chunk"]] = (row[:, None] % NE) == (row[None, :] % NE)
    return t


def search_table():
    cols = 1 + CANDS
    sign = np.array([1, 1, 1, -1], np.float32)
    steps = [4 ** (ROUNDS - 1 - r) for r in range(ROUNDS)] + [0]
    above = [sign * np.array([0] + [j * s - 0.5 for j in range(1, cols)]) for s in steps]
    t = np.zeros((128, (2 * ROUNDS + 3) * cols), np.float32)
    for r in range(ROUNDS):
        t[:, r * 2 * cols:(r * 2 + 1) * cols] = sign * steps[r]
        t[:, (r * 2 + 1) * cols:(r * 2 + 2) * cols] = above[r + 1]
    t[:, -3 * cols:-2 * cols] = sign + above[0]
    t[:, -2 * cols:-cols] = sign
    t[:, -cols:] = [0, CAP, CAP, 2 * CAP - TOKENS]
    return t


def wait(eng, sem, value):
    if not (isinstance(value, int) and value <= 0):
        eng.wait_ge(sem, value)


class Plain:

    def __init__(self, sem):
        self.sem = sem

    def __call__(self, eng):
        eng.sem_inc(self.sem, 1)


class Chain:

    def __init__(self, eng, sem):
        self.eng, self.sem, self.base, self.n = eng, sem, 0, 0

    def __call__(self, ins, then=None):
        self.n += 1
        ins.then_inc(self.sem, 1)
        self.eng.wait_ge(self.sem, self.base + self.n)
        if then:
            then(self.eng)

    def enter(self, trip, per_trip):
        self.outer = self.base + self.n
        self.base, self.n, self.per_trip = self.outer + trip * per_trip, 0, per_trip

    def leave(self, trips):
        assert self.n == self.per_trip, (self.sem, self.n, self.per_trip)
        self.base, self.n = self.outer + trips * self.per_trip, 0


FRONT = [(0, "K", 0), (2, "K", 1), (3, "V", 0), (5, "X", 0), (6, "X", 1), (7, "Q", 0), (9, "Q", 1), (14, "V", 1)]
OUT = sorted([(NU * b + 8, "A", b) for b in range(GB)] + [(NU * b + 9, "O", b) for b in range(GB)])
ROUTE = [(GU + 10, "T", 0), (GU + 11, "T", 1), (GU + 14, "S", 0), (GU + 15, "H", 0)]
KINDS = (FRONT, OUT, ROUTE)
FIRST = (0, 0, 1)
STEPS = GU
TURN, WEIGH, ATT = 2, 3, 3
ROTATE = (1, 5, 8, 11)
LN1_STATS, LN1_APPLY = 0, 3
LN2_APPLY = 7
XF_STATS = {9: ("mean",), 11: ("zeros0",), 12: ("zeros1",), 13: ("min", "max")}
GELU, GELU_TAIL, SHIFTED = 0, 5, (5, 7)
LOGITS = {1: (0, 1), 2: (2, 3), 6: (4, 5)}
CHOOSE = {9: (0, 1), 10: (2,), 11: (3,), 12: (4, 5), 13: (6,), 14: (7,), 15: (8, 9)}


def at_step(s, lag, front, own, prev):
    found = []
    for kind, items in enumerate(KINDS):
        for n, (when, what, j) in enumerate(items):
            when += lag
            if kind == 0:
                assert when < STEPS
                hit, back = front and when == s, -1
            else:
                hit, back = (own and when == s, 0) if when < STEPS else (prev and when - STEPS == s, 1)
            if hit:
                found.append((kind, back, what, j, n))
    return found


def unit_at(s, lag, own, prev):
    u = s - lag
    return [(0, u)] if u >= 0 and own and u < GU else [(1, u + GU)] if u < 0 and prev else []


BS, BT, BO, BM = (0, 1), (2, 3), 4, (5, 6, 7)
POOL_LINKS, DVE_LINKS = 22, 38


def signal(eng, ins, sem, value):
    ins.then_inc(sem, 1)
    eng.wait_ge(sem, value)


def build(nc, d):
    ctx = ExitStack()
    with ctx:
        program(nc, d, ctx)


def program(nc, d, ctx):
    def sb(name, shape, dt=F32):
        return ctx.enter_context(nc.sbuf_tensor(name, shape, dt))

    def sem(name):
        return ctx.enter_context(nc.semaphore(name))

    tab = sb("tab", [128, TAB_COLS])
    ident = tab[:, TAB["ident"]]
    xf_all = sb("xf_all", [T, NB, ROW])
    hpre = sb("hpre", [HID, TOKENS])
    we = [[sb(f"we{s}{j}", [128, WE_COLS]) for j in range(2)] for s in range(2)]
    wa = [sb(f"wa{s}", [128, WA_COLS]) for s in range(2)]
    gates = sb("gates", [128, 4])
    r2t = sb("r2t", [HID, NE])
    banks = [ctx.enter_context(nc.psum_tensor(f"bank{i}", [128, 512], F32)) for i in range(8)]

    ARENA = 25440
    arena = sb("arena", [128, ARENA])
    used = [0]

    def take(parts, shape, dt=F32):
        n = int(np.prod(shape))
        words = n if dt in (F32, I32) else (n + 1) // 2
        a = arena[:, used[0]:used[0] + words]
        used[0] += words
        assert used[0] <= ARENA, used[0]
        a = a if dt == F32 else a.bitcast(dt)
        names = "abcd"[:len(shape)]
        if len(shape) > 1:
            a = a.rearrange(f"p ({' '.join(names)}) -> p {' '.join(names)}", **dict(zip(names, shape)))
        return a[0:parts]

    wq, wk, wv = (take(128, [2, C]) for _ in range(3))
    ctxt = [take(128, [2, NT]) for _ in range(2)]
    xin = take(T, [GB, C])
    xn = take(T, [GB, C])
    xnt = take(128, [2, NT])
    proj = [take(128, [NT]) for _ in range(2)]
    prot = [take(128, [NT]) for _ in range(2)]
    assert NG % 2 == 0
    qt = [take(128, [2, NT])]
    kt = [take(128, [2, NT])]
    free_early = used[0]
    qt.append(take(128, [2, NT]))
    kt.append(take(128, [2, NT]))
    wo = take(128, [2, C])
    bqk = take(128, [4])
    bvb, gbo = take(T, [C]), take(T, [C])
    r1t, r1s = take(128, [2, HID]), take(NST, [HID])
    r1b = take(128, [1])
    identb, causalb = take(T, [T], BF16), take(T, [T], BF16)
    half_pow = take(T, [8])
    mv1, mv2, mv3 = (take(T, [GB, 2]) for _ in range(3))
    rs1, rs2, tmp4 = (take(T, [GB]) for _ in range(3))
    bns = take(T, [GB, 6])
    kz = [take(128, [2, 8, T]) for _ in range(2)]
    vx = [take(T, [GB, NH, VE]) for _ in range(2)]
    nmx = [take(T, [HU]) for _ in range(2)]
    pr = [take(T, [HU, T]) for _ in range(2)]
    prt = [take(T, [HU, T]) for _ in range(2)]
    rden = take(T, [NH])
    att = take(T, [C])
    attt = take(128, [2, T])
    x1 = [take(T, [GB, C]) for _ in range(2)]
    xf = take(T, [GB, C])
    st = take(T, [GB, NST])
    xft = we[1][0][:, 0:2 * NT].rearrange("p (c t) -> p c t", c=2)
    stt = we[1][0][0:NST, 2 * NT:3 * NT]
    pcos = [we[1][1][:, i * NT:(i + 1) * NT] for i in range(2)]
    spj = [we[1][0][0:T, 3 * NT + i * C:3 * NT + (i + 1) * C] for i in range(2)]


    used[0] = 0
    prb, w0, w1, h1, h2 = (take(T, [NB, NE]) for _ in range(5))
    sc = take(T, [CHB, NCH, NE])
    sc_flat = sc.rearrange("p j c e -> p (j c e)")
    col = [take(T, [NB]) for _ in range(8)]
    assert used[0] <= free_early
    w2, w3 = (take(T, [NB, NE]) for _ in range(2))
    se = take(128, [CHB * T])
    F16 = mybir.dt.float16
    digit_bits = [take(128, [CHB * T], I32) for _ in range(DIGITS)]
    digit = [take(128, [CHB * T], F16) for _ in range(DIGITS)]
    live = [digit[0]] + [take(128, [CHB * T], F16) for _ in range(DIGITS - 1)]
    over = take(128, [CHB * T], F16)
    junk = [take(128, [CHB * T], F16) for _ in range(CANDS)]
    srt = take(128, [(2 * ROUNDS + 3) * (1 + CANDS)])
    cand, base, passed = take(128, [1 + CANDS]), take(128, [1 + CANDS]), take(128, [1])
    reached = take(128, [CANDS])
    cnt = take(128, [CANDS])
    found, found_i = take(128, [DIGITS]), take(128, [DIGITS], I32)
    vb = take(128, [1])
    thd, thr = take(NE, [NE]), take(T, [NE])
    ge = take(T, [2, NE, NB], BF16)
    inc = take(T, [2, NE, NB], BF16)
    fresh = take(T, [2, NE, NB], BF16)
    lowb, onesb = take(T, [T], BF16), take(T, [T], BF16)
    ones = take(128, [T])
    dest = take(T, [2, NB], I32)


    used[0] = 0
    xr = [take(HC, [2, ROW]) for _ in range(4)]
    xet = [take(128, [2, CAP]) for _ in range(2)]
    th = [take(128, [CAP]) for _ in range(2)]
    gs = [take(128, [CAP]) for _ in range(2)]
    hh = [take(128, [KD, CAP]) for _ in range(2)]
    yt = [take(128, [2, CAP]) for _ in range(2)]
    yr = [take(HC, [2, C]) for _ in range(2)]
    fill = hpre[0:HC, 0:2 * ROW].rearrange("p (s c) -> p s c", s=2)
    zero = hpre[0:HC, 2 * ROW:2 * ROW + 2 * C].rearrange("p (s c) -> p s c", s=2)

    s_tab, s_first, s_const = sem("tables_in"), sem("first_weights_in"), sem("weights_in")
    s_filled, s_gl = sem("filling_made"), sem("gates_in")
    s_fo = sem("filling_out")
    s_setup, s_gate = sem("vector_setup"), sem("gates_ready")
    s_xin = sem("x_in")
    s_ctx = [sem("ctx_in0"), sem("ctx_in1")]
    s_mv1, s_rs1, s_xn, s_xnt = sem("mean1"), sem("rstd1"), sem("xn_ready"), sem("xnt_ready")
    s_xb = sem("bias_added")
    s_m = [sem("front_written"), sem("out_written"), sem("route_written")]
    s_mf = [sem("front_read"), sem("out_read"), sem("route_read")]
    s_proj, s_rot, s_rope, s_kz, s_v = (sem(n) for n in ("proj_ready", "rotated", "roped", "kz_ready", "v_ready"))
    s_s, s_mx, s_exp, s_ptr = sem("scores_ready"), sem("max_ready"), sem("exp_ready"), sem("probs_turned")
    s_pte = [sem("prt_even"), sem("prt_odd")]
    s_pv, s_att, s_attt, s_x1 = (sem(n) for n in ("pv_done", "att_ready", "attt_ready", "x1_ready"))
    s_ln2, s_rs2, s_mv3, s_st, s_xout, s_xfc = (sem(n) for n in (
        "ln2_stats", "rstd2", "xf_stats", "stats_ready", "x1_stored", "xf_kept"))
    s_mean = sem("xf_mean")
    s_xft, s_ln2a = sem("xft_ready"), sem("xf_ready")
    s_zeros = sem("zeros_ready")
    s_dve, s_pool = sem("vector_chain"), sem("pool_chain")

    x_rows = d["x"].rearrange("(n p) c -> p n c", p=T)
    o_rows = d["out"][0:TOKENS, :].rearrange("(n p) c -> p n c", p=T)
    block = ctx.enter_context(nc.Block())

    plain = Plain(sem("waits_carried"))
    GV = {}
    for s, per in ((s_mv1, 1), (s_rs1, 1), (s_xn, 1), (s_xb, 1), (s_xnt, 2), (s_proj, 4), (s_rot, 4),
                   (s_rope, 4), (s_kz, 4 * GB), (s_v, 2), (s_s, GU), (s_mx, GU), (s_exp, GU), (s_ptr, GU),
                   (s_pte[0], GU // 2), (s_pte[1], GU // 2), (s_pv, GU), (s_att, GB),
                   (s_attt, GB), (s_x1, GB), (s_ln2, 1), (s_ln2a, 1), (s_mean, 1), (s_rs2, 1), (s_mv3, 1), (s_st, 1),
                   (s_xft, 3), (s_xout, 16), (s_xfc, 16)):
        GV[s] = per * NG
    GV[s_xfc] += 1
    for kind in range(3):
        GV[s_m[kind]] = NG * len(KINDS[kind])
        GV[s_mf[kind]] = FIRST[kind] + NG * len(KINDS[kind])

    def attention_done(eng):
        for s, v in GV.items():
            eng.wait_ge(s, v)

    def groups(eng_fori, body, chain=None, per_trip=0):
        body(-1, 1, True, False, False)
        body(0, 0, True, True, False)
        with eng_fori(0, (NG - 2) // 2) as i:
            if chain:
                chain.enter(i, per_trip)
            body(2 * i + 1, 1, True, True, True, i + 2)
            body(2 * i + 2, 0, True, True, True, i + 2)
            if chain:
                chain.leave((NG - 2) // 2)
        body(NG - 1, 1, False, True, True)
        body(NG, 0, False, False, True)

    def keep_warm(times, weights, data):
        for _ in range(times):
            nc.tensor.matmul(banks[BS[0]][0:T, 0:NT], weights, data, start=True, stop=True)

    w_sem = [sem("experts_in0"), sem("experts_in1")]
    s_xs, s_xr = sem("rows_dispatched"), [sem(f"xr_in{i}") for i in range(4)]
    s_added = sem("rows_added")

    def load_pair(p, slot):
        for j in range(2):
            nc.sync.dma_start(we[slot][j][:], d["w_experts"][2 * p + j]).then_inc(w_sem[slot], 16)
        nc.sync.dma_start(wa[slot][:], d["w_adapters"][p]).then_inc(w_sem[slot], 16)

    s_h, s_lg, s_sub, s_e = sem("gelu_ready"), sem("logits_ready"), sem("logits_shifted"), sem("exp_of_logits")
    s_dig, s_ones, s_scr, s_set = sem("digits_in"), sem("ones_ready"), sem("scores_by_token"), sem("scores_turned")
    s_cnt, s_tot, s_thd, s_thr = sem("chunk_counts"), sem("totals"), sem("thresholds"), sem("thresholds_spread")
    s_ge, s_inc, s_slot, s_dest = sem("compared"), sem("prefix_ready"), sem("slots_counted"), sem("destinations")
    s_cand, s_cmp = sem("candidates"), sem("scores_to_compare")
    s_share = sem("shares_ready")

    EARLY = (NG - 2) * GB
    LATE = slice(EARLY, NB)

    def gelu(g):
        h = hpre[:, g * NT:(g + 1) * NT]
        nc.scalar.activation(h, h, ACT.Gelu).then_inc(s_h, 1)

    def routing_scalar(act):
        def shifted_exp(rows, count):
            act.wait_ge(s_sub, count)
            nc.scalar.activation(w0[:, rows, :], w0[:, rows, :], ACT.Exp).then_inc(s_e, 1)

        attention_done(act)
        gelu(NG - 1)
        shifted_exp(LATE, 3)
        act.wait_ge(s_set, 1)
        nc.scalar.copy(se[:, 0:GB * T], banks[2][:, 0:GB * T])
        nc.scalar.copy(se[:, GB * T:], banks[3][:, 0:GB * T]).then_inc(s_set, 1)
        for k in range(DIGITS):
            with nc.scalar.Fori(0, ROUNDS) as r:
                act.wait_ge(s_cand, (ROUNDS + 1) * k + r + 1)
                nc.scalar.activation(junk[2], live[k], ACT.Sign, bias=cand[:, 3:4],
                                     accum_out=cnt[:, 2:3]).then_inc(s_cnt, 1)

    def logits(pe, rows, bank, start=0):
        for b in range(rows.start, rows.stop):
            pe.wait_ge(s_h, b // GB + 1)
            at = start + (b - rows.start) * NE
            last = nc.tensor.matmul(banks[bank][0:T, at:at + NE], hpre[:, b * T:(b + 1) * T], r2t[:],
                                    start=True, stop=True)
        last.then_inc(s_lg, 1)

    def routing_tensor(pe):
        attention_done(pe)
        logits(pe, LATE, BS[0])
        pe.wait_ge(s_scr, 1)
        for j in range(CHB):
            last = nc.tensor.transpose(banks[2 + j // GB][:, (j % GB) * T:(j % GB + 1) * T],
                                       sc_flat[:, j * 128:(j + 1) * 128], ident[0:T, 0:T])
        last.then_inc(s_set, 1)
        with nc.tensor.Fori(0, DIGITS * ROUNDS) as r:
            pe.wait_ge(s_cnt, 2 * r + 2)
            nc.tensor.matmul(banks[4][:, 0:CANDS], tab[:, TAB["chunk"]], cnt, start=True, stop=True).then_inc(s_tot, 1)
        pe.wait_ge(s_thd, 1)
        pe.wait_ge(s_ones, 3)
        nc.tensor.matmul(banks[5][0:T, 0:NE], ones[0:NE], thd, start=True, stop=True).then_inc(s_thr, 1)
        part_of = lambda a, w, q: a[:, w, :, q * 16:(q + 1) * 16].rearrange("p e b -> p b e")
        pe.wait_ge(s_ge, 1)
        for w in range(2):
            for q in range(2):
                nc.tensor.matmul(banks[2 * w + q][0:T, :], lowb, part_of(ge, w, q), start=True, stop=False)
        pe.wait_ge(s_inc, 1)
        for q in range(2):
            for w in range(2):
                nc.tensor.matmul(banks[2 * w + q][0:T, :], onesb, part_of(inc, w, q),
                                 start=False, stop=(w == 0))
            nc.tensor.matmul(banks[2 + q][0:T, :], onesb,
                             inc[:, 0, :, NB - 1].unsqueeze(1).to_broadcast([T, 16, NE]),
                             start=False, stop=True).then_inc(s_slot, 1)

    over_b = lambda a, n: a.unsqueeze(1).to_broadcast([T, n, NE])
    over_e = lambda a: a.unsqueeze(2).to_broadcast([T, a.shape[1], NE])

    def shift_logits(dve, link, rows, bank, count):
        n = rows.stop - rows.start
        dve.wait_ge(s_lg, count)
        lg = banks[bank][0:T, 0:n * NE].rearrange("p (b e) -> p b e", e=NE)
        link(nc.vector.tensor_reduce(col[0][:, rows], lg, X, ALU.max))
        link(nc.vector.tensor_tensor(w0[:, rows, :], lg, over_e(col[0][:, rows]), ALU.subtract))
        dve.sem_inc(s_sub, 1)

    def choose(dve, link, rows, part, count):
        n = rows.stop - rows.start
        c = [a[:, rows] for a in col]
        p, u, v = (a[:, rows, :] for a in (prb, w0, w1))
        rev = over_b(tab[0:T, TAB["rev"]], n)
        values, top, hit = (p, c[4], h1[:, rows, :]) if part < 5 else (u, c[5], h2[:, rows, :])
        if part == 0:
            dve.wait_ge(s_e, count)
            link(nc.vector.tensor_reduce(c[1], u, X, ALU.add))
            link(nc.vector.reciprocal(c[2], c[1]))
        elif part == 1:
            link(nc.vector.tensor_tensor(p, u, over_e(c[2]), ALU.mult))
        elif part in (2, 6):
            link(nc.vector.tensor_reduce(top, values, X, ALU.max))
            link(nc.vector.tensor_tensor(v, values, over_e(top), ALU.is_equal))
        elif part in (3, 7):
            link(nc.vector.tensor_tensor(v, v, rev, ALU.mult))
            link(nc.vector.tensor_reduce(c[3], v, X, ALU.max))
        elif part in (4, 8):
            link(nc.vector.tensor_tensor(hit, v, over_e(c[3]), ALU.is_equal))
        elif part == 5:
            link(nc.vector.scalar_tensor_tensor(u, h1[:, rows, :], -2.0, p, ALU.mult, ALU.add))
        elif part == 9:
            link(nc.vector.tensor_tensor(v, h1[:, rows, :], h2[:, rows, :], ALU.add))
            for chunk in range(rows.start // CHB, rows.stop // CHB):
                at = slice(chunk * CHB, (chunk + 1) * CHB)
                last = nc.vector.tensor_tensor(sc[:, :, chunk, :], prb[:, at, :], w1[:, at, :], ALU.mult)
            link(last)

    def shares(link, part):
        if part == 0:
            link(nc.vector.tensor_tensor(col[6], col[4], col[5], ALU.add))
        elif part == 1:
            link(nc.vector.reciprocal(col[7], col[6]))
        elif part == 2:
            link(nc.vector.tensor_scalar(col[7], col[7], gates[0:T, 2:3], None, ALU.mult))
        else:
            choice = col[1 + part]
            link(nc.vector.tensor_tensor(choice, choice, col[7], ALU.mult))

    def routing_vector(dve, link):
        attention_done(dve)
        nc.vector.memset(ones, 1.0).then_inc(s_ones, 1)
        nc.vector.memset(onesb, 1.0).then_inc(s_ones, 1)
        nc.vector.tensor_scalar(lowb, tab[0:T, TAB["lower"]], -1.0, None, ALU.add).then_inc(s_ones, 1)
        shift_logits(dve, link, LATE, BS[0], EARLY // GB + 1)
        for part in range(10):
            choose(dve, link, LATE, part, 2)
        dve.sem_inc(s_scr, 1)
        dve.wait_ge(s_dig, 16)
        dve.wait_ge(s_set, 2)
        cols = 1 + CANDS
        def take_digit(k):
            shift = DBITS * (DIGITS - 1 - k)
            link(nc.vector.tensor_scalar(digit_bits[k], se.bitcast(I32), shift, (1 << DBITS) - 1,
                                         ALU.logical_shift_right, ALU.bitwise_and))

        def to_float(k):
            link(nc.vector.tensor_scalar(digit[k], digit_bits[k], 1.0, None, ALU.add))

        take_digit(0)
        to_float(0)
        for k in range(DIGITS):
            if k:
                top = found[:, k - 1:k]
                nc.vector.tensor_scalar(over, live[k - 1], top, ABOVE, ALU.is_gt, ALU.mult)
                link(nc.vector.scalar_tensor_tensor(live[k], live[k - 1], top, digit[k], ALU.is_equal, ALU.mult))
                link(nc.vector.tensor_tensor(live[k], live[k], over, ALU.add))
            link(nc.vector.tensor_copy(cand, srt[:, 2 * ROUNDS * cols:(2 * ROUNDS + 1) * cols]))
            dve.sem_inc(s_cand, 1)
            for r in range(ROUNDS):
                for j in range(CANDS - 1):
                    last = nc.vector.tensor_scalar(junk[j], live[k], cand[:, 1 + j:2 + j], None, ALU.is_ge, ALU.add,
                                                   accum_out=cnt[:, j:j + 1])
                link(last)
                dve.sem_inc(s_cnt, 1)
                link(nc.vector.scalar_tensor_tensor(base, srt[:, (2 * ROUNDS + 1) * cols:(2 * ROUNDS + 2) * cols],
                                                    cand[:, 0:1], srt[:, (2 * r + 1) * cols:(2 * r + 2) * cols],
                                                    ALU.mult, ALU.add))
                if k == 0 and r in (0, 1):
                    take_digit(r + 1)
                elif k == 0 and r in (2, 3):
                    to_float(r - 1)
                elif k == 1:
                    shares(link, r)
                    if r == ROUNDS - 1:
                        dve.sem_inc(s_share, 1)
                dve.wait_ge(s_tot, ROUNDS * k + r + 1)
                link(nc.vector.scalar_tensor_tensor(reached, banks[4][:, 0:CANDS], 0.0,
                                                    srt[:, (2 * ROUNDS + 2) * cols + 1:(2 * ROUNDS + 3) * cols],
                                                    ALU.add, ALU.is_ge, accum_out=passed))
                link(nc.vector.scalar_tensor_tensor(cand, srt[:, 2 * r * cols:(2 * r + 1) * cols], passed, base,
                                                    ALU.mult, ALU.add))
                dve.sem_inc(s_cand, 1)
            link(nc.vector.tensor_copy(found[:, k:k + 1], cand[:, 0:1]))
        link(nc.vector.tensor_scalar(found_i, found, -1.0, None, ALU.add))
        for k in range(DIGITS - 1):
            last = nc.vector.tensor_scalar(found_i[:, k:k + 1], found_i[:, k:k + 1], DBITS * (DIGITS - 1 - k), None,
                                           ALU.logical_shift_left)
        link(last)
        link(nc.vector.tensor_tensor(vb.bitcast(I32), found_i[:, 0:1], found_i[:, 1:2], ALU.bitwise_or))
        link(nc.vector.tensor_tensor(vb.bitcast(I32), vb.bitcast(I32), found_i[:, 2:3], ALU.bitwise_or))
        link(nc.vector.tensor_scalar(thd, ident[0:NE, 0:NE], vb[0:NE, 0:1], None, ALU.mult))
        dve.sem_inc(s_thd, 1)
        dve.wait_ge(s_thr, 1)
        link(nc.vector.tensor_copy(thr, banks[5][0:T, 0:NE]))
        tb = thr.unsqueeze(1).unsqueeze(1).to_broadcast([T, NCH, CHB, NE])
        dve.wait_ge(s_cmp, 1)
        for w, op in ((0, ALU.is_gt), (1, ALU.is_equal)):
            last = nc.vector.tensor_tensor(ge[:, w].rearrange("p e (c j) -> p c j e", j=CHB),
                                           sc.rearrange("p j c e -> p c j e"), tb, op)
        link(last)
        dve.sem_inc(s_ge, 1)
        flat = lambda a: a.rearrange("p w e b -> p (w e b)")
        link(nc.vector.tensor_tensor_scan(flat(inc), flat(fresh), flat(ge), 0.0, ALU.mult, ALU.add))
        dve.sem_inc(s_inc, 1)
        for c in range(NCH):
            rows = slice(c * CHB, (c + 1) * CHB)
            at = slice((c % 2) * CHB * NE, (c % 2 + 1) * CHB * NE)
            pg = banks[c // 2][0:T, at].rearrange("p (b e) -> p b e", e=NE)
            pq = banks[2 + c // 2][0:T, at].rearrange("p (b e) -> p b e", e=NE)
            if c % 2 == 0:
                dve.wait_ge(s_slot, c // 2 + 1)
            gec = [ge[:, w, :, rows].rearrange("p e b -> p b e") for w in range(2)]
            every = lambda a: a.unsqueeze(1).to_broadcast([T, CHB, NE])
            w0c, w1c, w2c = w0[:, rows, :], w1[:, rows, :], w2[:, rows, :]
            nc.vector.tensor_tensor(w0c, gec[0], pg, ALU.mult)
            nc.vector.tensor_tensor(w2c, gec[0], gec[1], ALU.add)
            link(nc.vector.tensor_tensor(w1c, gec[1], pq, ALU.mult))
            link(nc.vector.tensor_tensor(w0c, w0c, w1c, ALU.add))
            link(nc.vector.scalar_tensor_tensor(w1c, w2c, -BIG, w0c, ALU.mult, ALU.add))
            link(nc.vector.tensor_scalar(w2c, w0c, float(CAP), BIG, ALU.is_ge, ALU.mult))
            link(nc.vector.tensor_tensor(w1c, w1c, w2c, ALU.add))
            link(nc.vector.tensor_tensor(w1c, w1c, every(tab[0:T, TAB["slot0"]]), ALU.add))
            nc.vector.tensor_tensor(w0c, w1c, h1[:, rows, :], ALU.mult)
            link(nc.vector.tensor_tensor(w2c, w1c, h2[:, rows, :], ALU.mult))
            nc.vector.tensor_reduce(col[0][:, rows], w0c, X, ALU.add)
            link(nc.vector.tensor_reduce(col[1][:, rows], w2c, X, ALU.add))
            for k in range(2):
                last = nc.vector.tensor_copy(dest[:, k, rows], col[k][:, rows])
            link(last)
            dve.sem_inc(s_dest, 1)

    s_xet, s_xrt, s_up, s_th, s_hh, s_yt, s_yts, s_yw, s_yr = (sem(n) for n in (
        "xet_ready", "rows_turned", "up_done", "tanh_ready", "hidden_ready", "down_done", "yt_ready",
        "y_turned", "y_ready"))
    s_gs = sem("gated")
    LAST = NE - 4

    def experts_sync(sp):
        with nc.sync.Fori(0, NE // 4 - 1) as i:
            for s in range(2):
                sp.wait_ge(s_yt, 4 * i + 2 * s + 2)
                load_pair(2 * i + s + 2, s)

    def experts_pool(pool, link):
        attention_done(pool)
        link(nc.gpsimd.memset(fresh, 1.0))
        link(nc.gpsimd.memset(fresh[:, :, :, 0], 0.0))
        pool.wait_ge(s_set, 1)
        link(nc.gpsimd.tensor_tensor(w2, h1, h2, ALU.add))
        link(nc.gpsimd.tensor_scalar(w2, w2, -1.0, None, ALU.add))
        for chunk in range(NCH):
            link(nc.gpsimd.tensor_tensor(sc[:, :, chunk, :], sc[:, :, chunk, :],
                                         w2[:, chunk * CHB:(chunk + 1) * CHB, :], ALU.add))
        pool.sem_inc(s_cmp, 1)
        pool.wait_ge(s_share, 1)
        link(nc.gpsimd.tensor_tensor(prb, h1, over_e(col[4]), ALU.mult))
        link(nc.gpsimd.tensor_tensor(w3, h2, over_e(col[5]), ALU.mult))
        link(nc.gpsimd.tensor_tensor(xf_all[:, :, C:C + NE], prb, w3, ALU.add))
        pool.wait_ge(s_fo, 16 * (NE + 1))
        slots = d["slots_flat"]
        for b in range(NB):
            if b % CHB == 0:
                pool.wait_ge(s_dest, b // CHB + 1)
            for k in range(2):
                nc.gpsimd.indirect_dma_start(slots, bass.IndirectOffsetOnAxis(ap=dest[:, k, b:b + 1], axis=0),
                                             xf_all[:, b, :], None, bounds_check=NE * CAP - 1,
                                             oob_is_err=False).then_inc(s_xs, 16)

        pool.wait_ge(s_xs, 16 * 2 * NB)
        for e in range(4):
            nc.gpsimd.dma_start(xr[e], d["slots"][e]).then_inc(s_xr[e], 16)

        def expert(e, j, load=True):
            wait(pool, s_added, 32 * e)
            if load:
                plain(pool)
                slot = (j - 1) % 4
                nc.gpsimd.dma_start(xr[slot], d["slots"][e + 3]).then_inc(s_xr[slot], 16)
            pool.wait_ge(s_yr, e + 1)
            plain(pool)
            for h in range(2):
                nc.gpsimd.indirect_dma_start(d["out"], bass.IndirectOffsetOnAxis(
                    ap=xr[j][:, h, ROW - 1:ROW].bitcast(I32), axis=0), yr[j % 2][:, h, :], None,
                    compute_op=ALU.add).then_inc(s_added, 16)

        for j in range(4):
            expert(j, j, j > 0)
        with nc.gpsimd.Fori(1, NE // 4 - 1) as i:
            for j in range(4):
                expert(4 * i + j, j)
        for j in range(4):
            expert(NE - 4 + j, j, j == 0)
        pool.wait_ge(s_added, 32 * NE)

    def experts_scalar(act):
        def rows_turned(e, j):
            act.wait_ge(s_xrt, e + 1)
            nc.scalar.copy(xet[j % 2].rearrange("p c t -> p (c t)"), banks[4][:, 0:2 * CAP]).then_inc(s_xet, 1)

        def expert(e, j, last):
            for k in range(KD):
                n, m = KD * e + k, KD * j + k
                act.wait_ge(s_up, n + 1)
                wait(act, s_gs, n - 1)
                nc.scalar.activation(th[m % 2], banks[m % 4][:, 0:CAP], ACT.Tanh, scale=0.5).then_inc(s_th, 1)
            if not last:
                rows_turned(e + 1, (j + 1) % 4)
            act.wait_ge(s_yt, e + 1)
            wait(act, s_yw, e - 1)
            nc.scalar.copy(yt[j % 2][:, 0, :], banks[5][:, 0:CAP])
            nc.scalar.copy(yt[j % 2][:, 1, :], banks[6][:, 0:CAP]).then_inc(s_yts, 1)

        rows_turned(0, 0)
        for j in range(4):
            expert(j, j, False)
        with nc.scalar.Fori(1, NE // 4 - 1) as i:
            for j in range(4):
                expert(4 * i + j, j, False)
        for j in range(4):
            expert(NE - 4 + j, j, j == 3)

    def experts_vector(dve, link):
        def turned(e, j):
            dve.wait_ge(s_yw, e + 1)
            wait(dve, s_added, 32 * (e - 1))
            for h in range(2):
                last = nc.vector.tensor_scalar(yr[j % 2][:, h, :], banks[7][0:HC, h * C:(h + 1) * C],
                                               xr[j][:, h, bass.ds(C + e, 1)], None, ALU.mult)
            last.then_inc(s_yr, 1)

        def expert(e, j, first):
            for k in range(KD):
                if k == 1 and not first:
                    turned(e - 1, (j - 1) % 4)
                n, m = KD * e + k, KD * j + k
                dve.wait_ge(s_th, n + 1)
                signal(dve, nc.vector.scalar_tensor_tensor(gs[m % 2], th[m % 2], 1.0, banks[m % 4][:, 0:CAP],
                                                           ALU.add, ALU.mult), s_gs, n + 1)
                if k == 0:
                    wait(dve, s_yt, e - 1)
                if k < KE:
                    nc.vector.tensor_tensor(hh[j % 2][:, k, :], gs[m % 2], banks[m % 4][:, CAP:2 * CAP],
                                            ALU.mult).then_inc(s_hh, 1)
                else:
                    nc.vector.scalar_tensor_tensor(hh[j % 2][:, k, :], gs[m % 2], SCALE,
                                                   banks[m % 4][:, CAP:2 * CAP], ALU.mult,
                                                   ALU.mult).then_inc(s_hh, 1)

        for j in range(4):
            expert(j, j, j == 0)
        with nc.vector.Fori(1, NE // 4) as i:
            for j in range(4):
                expert(4 * i + j, j, False)
        turned(NE - 1, 3)

    def experts_tensor(pe):
        def turn_rows(e, j, loads):
            pe.wait_ge(s_xr[j], 16 * loads)
            wait(pe, s_xet, e)
            for c in range(2):
                for h in range(2):
                    last = nc.tensor.transpose(banks[4][:, c * CAP + h * HC:c * CAP + (h + 1) * HC],
                                               xr[j][:, h, c * 128:(c + 1) * 128], ident[0:HC, 0:HC])
            last.then_inc(s_xrt, 1)

        def up(e, j, k):
            n, m = KD * e + k, KD * j + k
            wait(pe, s_hh, n - 3)
            w, width, at = (we[j // 2][j % 2], INTER, k * 128) if k < KE else (wa[j // 2], AINTER, 0)
            for part in range(2):
                for c in range(2):
                    col0 = c * 2 * width + part * width + at
                    last = nc.tensor.matmul(banks[m % 4][:, part * CAP:(part + 1) * CAP], w[:, col0:col0 + 128],
                                            xet[j % 2][:, c, :], start=(c == 0), stop=(c == 1))
            last.then_inc(s_up, 1)

        def down(e, j, k):
            pe.wait_ge(s_hh, KD * e + k + 1)
            if k == 0:
                wait(pe, s_yts, e)
            w, col0 = (we[j // 2][j % 2], 4 * INTER + k * C) if k < KE else (wa[j // 2], 4 * AINTER)
            for o in range(2):
                last = nc.tensor.matmul(banks[5 + o][:, 0:CAP], w[:, col0 + o * 128:col0 + (o + 1) * 128],
                                        hh[j % 2][:, k, :], start=(k == 0), stop=(k == KD - 1))
            if k == KD - 1:
                last.then_inc(s_yt, 1)

        def turn_back(e, j):
            pe.wait_ge(s_yts, e + 1)
            wait(pe, s_yr, e)
            for h in range(2):
                for o in range(2):
                    last = nc.tensor.transpose(banks[7][0:HC, h * C + o * 128:h * C + (o + 1) * 128],
                                               yt[j % 2][:, o, h * HC:(h + 1) * HC], ident)
            last.then_inc(s_yw, 1)

        def four(i, loads, first, last_four):
            for j in range(4):
                e = 4 * i + j
                if j % 2 == 0:
                    pe.wait_ge(w_sem[j // 2], 48 * loads)
                pe.wait_ge(s_xet, e + 1)
                for k in range(KD):
                    up(e, j, k)
                    if k == 0 and not (first and j == 0):
                        turn_back(e - 1, (j - 1) % 4)
                    if k >= 2:
                        down(e, j, k - 2)
                if j < 3:
                    turn_rows(e + 1, j + 1, loads)
                elif not last_four:
                    turn_rows(e + 1, 0, loads + 1)
                down(e, j, KD - 2)
                down(e, j, KD - 1)

        pe.wait_ge(s_xs, 16 * 2 * NB)
        keep_warm(WARM // 4, ident[0:T, 0:T], tab[0:T, 0:NT])
        turn_rows(0, 0, 1)
        four(0, 1, True, False)
        with nc.tensor.Fori(1, NE // 4 - 1) as i:
            four(i, i + 1, False, False)
        four(NE // 4 - 1, NE // 4, False, True)
        turn_back(NE - 1, 3)

    @block.sync
    def _(sp):
        nc.sync.dma_start(ctxt[0], d["ctx"][0]).then_inc(s_ctx[0], 16)
        nc.sync.dma_start(wk, d["wk"]).then_inc(s_first, 16)
        nc.sync.dma_start(gates[:, 0:2], d["gates"].partition_broadcast(128)).then_inc(s_gl, 16)
        nc.sync.dma_start(bqk, d["bqk"]).then_inc(s_first, 16)
        nc.sync.dma_start(xin, x_rows[:, 0:GB, :]).then_inc(s_xin, 16)
        nc.sync.dma_start(tab[:], d["table"]).then_inc(s_tab, 16)
        nc.sync.dma_start(gbo, d["bo"].partition_broadcast(T)).then_inc(s_first, 16)
        nc.sync.dma_start(bvb, d["bv"].partition_broadcast(T)).then_inc(s_const, 16)
        for dst, name in ((wv, "wv"), (wq, "wq"), (wo, "wo"), (r1t, "r1t"), (r1s, "r1s"), (r1b, "r1b"),
                          (r2t[:], "r2t")):
            nc.sync.dma_start(dst, d[name]).then_inc(s_const, 16)

        def fill_slots():
            sp.wait_ge(s_filled, 2)
            with nc.sync.Fori(0, NE) as e:
                nc.sync.dma_start(d["slots"][e], fill).then_inc(s_fo, 16)
            nc.sync.dma_start(d["out"][TOKENS:TOKENS + CAP, :].rearrange("(s p) c -> p s c", p=HC),
                              zero).then_inc(s_fo, 16)

        def group(g, par, front, own, prev, _=1):
            if front and own:
                wait(sp, s_v, 2 * g)
                plain(sp)
                wait(sp, s_proj, 4 * g)
                plain(sp)
                nc.sync.dma_start(ctxt[1 - par], d["ctx"][g + 1]).then_inc(s_ctx[1 - par], 16)
                wait(sp, s_xn, g + 1)
                plain(sp)
                wait(sp, s_xb, g + 1)
                plain(sp)
                nc.sync.dma_start(xin, x_rows[:, bass.ds(GB * (g + 1), GB), :]).then_inc(s_xin, 16)
                if not prev:
                    fill_slots()
                    load_pair(0, 0)
            if prev:
                wait(sp, s_x1, GB * g)
                plain(sp)
                nc.sync.dma_start(o_rows[:, bass.ds(GB * (g - 1), GB), :], x1[1 - par]).then_inc(s_xout, 16)
            if prev:
                wait(sp, s_ln2a, g)
                plain(sp)
                nc.sync.dma_start(xf_all[:, bass.ds(GB * (g - 1), GB), 0:C], xf).then_inc(s_xfc, 16)

        sp.sem_inc(s_xfc, 1)
        groups(nc.sync.Fori, group)
        attention_done(sp)
        load_pair(1, 1)
        nc.sync.dma_start(srt, d["search"]).then_inc(s_dig, 16)
        experts_sync(sp)

    @block.gpsimd
    def _(pool):
        link = Chain(pool, s_pool)
        link(nc.gpsimd.memset(hpre[0:HC, 0:2 * ROW + 2 * C], 0.0))
        nc.gpsimd.iota(fill[:, :, ROW - 1].bitcast(I32), pattern=[[HC, 2]], base=TOKENS,
                       channel_multiplier=1).then_inc(s_filled, 1)
        nc.gpsimd.iota(xf_all[:, :, ROW - 1].bitcast(I32), pattern=[[T, NB]], base=0,
                       channel_multiplier=1).then_inc(s_filled, 1)
        nc.gpsimd.memset(half_pow[:, 0:4], -0.5)
        link(nc.gpsimd.memset(half_pow[:, 4:8], 0.5))

        def ln1_rstd(n):
            wait(pool, s_mv1, n + 1)
            plain(pool)
            link(nc.gpsimd.tensor_scalar(tmp4, mv1[:, :, 1], 1e-5, None, ALU.add))
            signal(pool, nc.gpsimd.tensor_tensor(rs1, tmp4, half_pow[:, 0:4], ALU.pow), s_rs1, n + 1)

        def add_bias(n, par):
            wait(pool, s_xin, 16 * (n + 1))
            pool.wait_ge(s_gate, 2)
            wait(pool, s_ln2a, n - 1)
            wait(pool, s_xout, 16 * (n - 1))
            signal(pool, nc.gpsimd.tensor_tensor(x1[par], xin, gbo.unsqueeze(1).to_broadcast([T, GB, C]),
                                                 ALU.add), s_xb, n + 1)

        def rope(n, par, z):
            wait(pool, s_rot, 4 * n + z + 1)
            link(nc.gpsimd.tensor_tensor(prot[z % 2].rearrange("p (b t) -> p b t", b=GB),
                                         prot[z % 2].rearrange("p (b t) -> p b t", b=GB),
                                         tab[:, TAB["sin"]].unsqueeze(1).to_broadcast([128, GB, T]), ALU.mult))
            if z < 2:
                wait(pool, s_kz, 4 * GB * (n - 1))
                dst = kt[par][:, z, :]
            else:
                wait(pool, s_s, GU * (n - 1))
                dst = qt[par][:, z - 2, :]
            signal(pool, nc.gpsimd.tensor_tensor(dst, pcos[z % 2], prot[z % 2], ALU.add), s_rope, 4 * n + z + 1)

        def spread(n, par, b):
            if b == 0:
                wait(pool, s_rope, 4 * n + 2)
            wait(pool, s_s, GU * n + NU * (b - 1))
            for r in range(4):
                rows = slice(32 * r, 32 * r + 32)
                signal(pool, nc.gpsimd.tensor_tensor(
                    kz[b % 2][rows, :, 2 * r:2 * r + 2, :],
                    kt[par][rows, :, b * T:(b + 1) * T].unsqueeze(2).to_broadcast([32, 2, 2, T]),
                    tab[rows, TAB["parity"]].unsqueeze(1).unsqueeze(3).to_broadcast([32, 2, 2, T]),
                    ALU.mult), s_kz, 4 * (GB * n + b) + r + 1)

        def ln2_rstd(r):
            wait(pool, s_ln2, r + 1)
            plain(pool)
            link(nc.gpsimd.tensor_scalar(tmp4, mv2[:, :, 1], 1e-5, None, ALU.add))
            signal(pool, nc.gpsimd.tensor_tensor(rs2, tmp4, half_pow[:, 0:4], ALU.pow), s_rs2, r + 1)

        def router_stats(r):
            wait(pool, s_mean, r + 1)
            plain(pool)
            link(nc.gpsimd.tensor_scalar(tmp4, mv3[:, :, 1], float(C) / (C - 1), None, ALU.mult))
            link(nc.gpsimd.tensor_tensor(st[:, :, 1], tmp4, half_pow[:, 4:8], ALU.pow))
            link(nc.gpsimd.tensor_tensor(tmp4, mv3[:, :, 0], mv3[:, :, 0], ALU.mult))
            link(nc.gpsimd.tensor_tensor(tmp4, tmp4, mv3[:, :, 1], ALU.add), plain)
            link(nc.gpsimd.tensor_scalar(tmp4, tmp4, float(C), None, ALU.mult))
            signal(pool, nc.gpsimd.tensor_tensor(st[:, :, 4], tmp4, half_pow[:, 4:8], ALU.pow), s_st, r + 1)

        def group(g, par, front, own, prev, _=1):
            if own:
                spread(g, par, 1)
            if front:
                ln1_rstd(g + 1)
                rope(g + 1, 1 - par, 0)
            if own:
                spread(g, par, 2)
            if front:
                rope(g + 1, 1 - par, 1)
                if not own:
                    spread(g + 1, 1 - par, 0)
            if prev:
                ln2_rstd(g - 1)
            if front:
                rope(g + 1, 1 - par, 2)
            if own:
                spread(g, par, 3)
            if prev:
                router_stats(g - 1)
            if front:
                rope(g + 1, 1 - par, 3)
                add_bias(g + 1, 1 - par)
                if own:
                    spread(g + 1, 1 - par, 0)

        for i in range(2):
            nc.gpsimd.memset(kz[i], 0.0).then_inc(s_zeros, 1)
        pool.wait_ge(s_zeros, 2)
        pool.wait_ge(s_tab, 16)
        groups(nc.gpsimd.Fori, group, link, POOL_LINKS)
        experts_pool(pool, link)

    @block.scalar
    def _(act):
        act.wait_ge(s_gl, 16)
        nc.scalar.activation(gates[:, 0:2], gates[:, 0:2], ACT.Tanh).then_inc(s_gate, 1)
        act.wait_ge(s_gate, 3)

        def item(q, par, kind, what, j, n):
            src = banks[BM[kind]]
            wait(act, s_m[kind], len(KINDS[kind]) * q + n + 1)
            if what == "X":
                if j == 0:
                    wait(act, s_proj, 4 * q)
                nc.scalar.copy(xnt[:, :, 2 * j * T:2 * (j + 1) * T],
                               src[:, 0:4 * T].rearrange("p (c t) -> p c t", c=2)).then_inc(s_xnt, 1)
                act.wait_ge(s_xnt, 2 * q + j + 1)
                act.sem_inc(s_mf[kind], 1)
            elif what in "KQ":
                z = j + (2 if what == "Q" else 0)
                wait(act, s_rot, 4 * q + z - 1)
                nc.scalar.activation(proj[z % 2], src[:, 0:NT], ACT.Identity, bias=bqk[:, z:z + 1],
                                     scale=1.0 if z < 2 else DH ** -0.5).then_inc(s_proj, 1)
                act.wait_ge(s_proj, 4 * q + z + 1)
                act.sem_inc(s_mf[kind], 1)
            elif what == "T":
                nc.scalar.copy(xft[:, :, 2 * j * T:2 * (j + 1) * T],
                               src[:, 0:4 * T].rearrange("p (c t) -> p c t", c=2)).then_inc(s_xft, 1)
                act.wait_ge(s_xft, 3 * q + j + 1)
                act.sem_inc(s_mf[kind], 1)
            elif what == "S":
                nc.scalar.copy(stt, src[0:NST, 0:NT]).then_inc(s_xft, 1)
                act.wait_ge(s_xft, 3 * q + 3)
                act.sem_inc(s_mf[kind], 1)
            elif what == "A":
                wait(act, s_x1, GB * q + j)
                nc.scalar.copy(attt, src[:, 0:2 * T].rearrange("p (c t) -> p c t", c=2)).then_inc(s_attt, 1)
                act.wait_ge(s_attt, GB * q + j + 1)
                act.sem_inc(s_mf[kind], 1)
            elif what == "H":
                act.wait_ge(s_fo, 16 * (NE + 1))
                nc.scalar.activation(hpre[:, bass.ds(q * NT, NT)], src[:, 0:NT], ACT.Identity,
                                     bias=r1b[:, 0:1]).then_inc(s_mf[kind], 1)

        def group(g, par, front, own, prev, _=1):
            for s in range(STEPS):
                for back, u in unit_at(s, TURN, own, prev):
                    if u % 2 == 1:
                        wait(act, s_ptr, GU * (g - back) + u + 1)
                        wait(act, s_pv, GU * (g - back) + u - 1)
                        nc.scalar.copy(prt[1].rearrange("p a b -> p (a b)"),
                                       banks[BT[1]][0:T, 0:HU * T]).then_inc(s_pte[1], 1)
                if own:
                    wait(act, s_mx, GU * g + s + 1)
                    wait(act, s_ptr, GU * g + s - 1)
                    for j in range(HU):
                        last = nc.scalar.activation(pr[s % 2][:, j, :], banks[BS[s % 2]][0:T, j * T:(j + 1) * T],
                                                    ACT.Exp, bias=nmx[s % 2][:, j:j + 1])
                    last.then_inc(s_exp, 1)
                for kind, back, what, j, n in at_step(s, 0, front, own, prev):
                    if what not in "VO":
                        item(g - back, (par + back) % 2, kind, what, j, n)
                if own and not front and s == GELU:
                    act.wait_ge(s_mf[2], FIRST[2] + len(ROUTE) * EARLY // GB)
                    for early in range(EARLY // GB):
                        gelu(early)
                if own and not front and s == SHIFTED[-1] + 1:
                    act.wait_ge(s_sub, 2)
                    nc.scalar.activation(w0[:, 0:EARLY, :], w0[:, 0:EARLY, :], ACT.Exp).then_inc(s_e, 1)
                if not own and not front and s == GELU_TAIL:
                    act.wait_ge(s_mf[2], FIRST[2] + len(ROUTE) * (NG - 1))
                    gelu(NG - 2)

        groups(nc.scalar.Fori, group)
        routing_scalar(act)
        experts_scalar(act)

    @block.vector
    def _(dve):
        link = Chain(dve, s_dve)
        for par in range(2):
            nc.vector.memset(vx[par], 1.0).then_inc(s_setup, 1)
        dve.wait_ge(s_tab, 16)
        nc.vector.tensor_copy(identb, tab[0:T, TAB["ident"]][:, 0:T]).then_inc(s_setup, 1)
        nc.vector.tensor_copy(causalb, tab[0:T, TAB["causal"]]).then_inc(s_setup, 1)
        dve.wait_ge(s_setup, 4)
        dve.wait_ge(s_gate, 1)
        dve.wait_ge(s_first, 16 * 3)
        nc.vector.tensor_scalar(gates[:, 2:3], gates[:, 1:2], 0.5, None, ALU.mult).then_inc(s_setup, 1)
        nc.vector.tensor_scalar(gbo, gbo, gates[0:T, 0:1], None, ALU.mult).then_inc(s_gate, 1)
        nc.vector.tensor_scalar(bqk[:, 2:4], bqk[:, 2:4], DH ** -0.5, None, ALU.mult).then_inc(s_gate, 1)

        def ln1_stats(n):
            wait(dve, s_xin, 16 * (n + 1))
            wait(dve, s_xn, n)
            for b in range(GB):
                last = nc.vector.bn_stats(bns[:, b, :], xin[:, b, :])
            link(last, plain)
            for b in range(GB):
                last = nc.vector.bn_aggr(mv1[:, b, :], bns[:, b, :])
            link(last)
            dve.sem_inc(s_mv1, 1)

        def ln1_apply(n):
            wait(dve, s_rs1, n + 1)
            wait(dve, s_xnt, 2 * n)
            for b in range(GB):
                last = nc.vector.tensor_scalar(xn[:, b, :], xin[:, b, :], mv1[:, b, 0:1], rs1[:, b:b + 1],
                                               ALU.subtract, ALU.mult)
            signal(dve, last, s_xn, n + 1)

        def rotate(n, z):
            wait(dve, s_proj, 4 * n + z + 1)
            wait(dve, s_rope, 4 * n + z - 1)
            plain(dve)
            nc.vector.stream_shuffle(prot[z % 2], proj[z % 2],
                                     mask=[i + DH // 2 if i % DH < DH // 2 else i - DH // 2 for i in range(32)])
            nc.vector.tensor_tensor(pcos[z % 2].rearrange("p (b t) -> p b t", b=GB),
                                    proj[z % 2].rearrange("p (b t) -> p b t", b=GB),
                                    tab[:, TAB["cos"]].unsqueeze(1).to_broadcast([128, GB, T]),
                                    ALU.mult).then_inc(s_rot, 1)

        def values(q, par, j, kind, n):
            wait(dve, s_m[kind], len(KINDS[kind]) * q + n + 1)
            wait(dve, s_pv, GU * (q - 1))
            nc.vector.tensor_tensor(
                vx[par][:, 2 * j:2 * j + 2, :, 0:DH],
                banks[BM[kind]][0:T, 0:2 * C].rearrange("p (b h d) -> p b h d", b=2, h=NH),
                bvb.rearrange("p (h d) -> p h d", h=NH).unsqueeze(1).to_broadcast([T, 2, NH, DH]),
                ALU.add).then_inc(s_v, 1)
            dve.wait_ge(s_v, 2 * q + j + 1)
            dve.sem_inc(s_mf[kind], 1)

        def residual(q, par, b, kind, n):
            wait(dve, s_m[kind], len(KINDS[kind]) * q + n + 1)
            wait(dve, s_xb, q + 1)
            signal(dve, nc.vector.scalar_tensor_tensor(x1[par][:, b, :], banks[BM[kind]][0:T, 0:C], gates[0:T, 0:1],
                                                       x1[par][:, b, :], ALU.mult, ALU.add),
                   s_x1, GB * q + b + 1)
            dve.sem_inc(s_mf[kind], 1)
            if b == GB - 2:
                for i in range(GB - 1):
                    last = nc.vector.bn_stats(bns[:, i, :], x1[par][:, i, :])
                link(last, plain)
                for i in range(GB - 1):
                    last = nc.vector.bn_aggr(mv2[:, i, :], bns[:, i, :])
                link(last)
            if b == GB - 1:
                link(nc.vector.bn_stats(bns[:, b, :], x1[par][:, b, :]), plain)
                link(nc.vector.bn_aggr(mv2[:, b, :], bns[:, b, :]))
                dve.sem_inc(s_ln2, 1)

        def ln2_apply(r, par):
            wait(dve, s_rs2, r + 1)
            wait(dve, s_xfc, 1 + 16 * r)
            for b in range(GB):
                last = nc.vector.tensor_scalar(xf[:, b, :], x1[par][:, b, :], mv2[:, b, 0:1], rs2[:, b:b + 1],
                                               ALU.subtract, ALU.mult)
            signal(dve, last, s_ln2a, r + 1)

        def xf_stats(r, part):
            if part == "mean":
                for b in range(GB):
                    last = nc.vector.bn_stats(bns[:, b, :], xf[:, b, :])
                link(last, plain)
                for b in range(GB):
                    last = nc.vector.bn_aggr(mv3[:, b, :], bns[:, b, :])
                link(last)
                dve.sem_inc(s_mean, 1)
                nc.vector.tensor_copy(st[:, :, 0], mv3[:, :, 0])
            elif part == "min":
                link(nc.vector.tensor_reduce(st[:, :, 2], xf, X, ALU.min))
            elif part == "max":
                link(nc.vector.tensor_reduce(st[:, :, 3], xf, X, ALU.max))
                dve.sem_inc(s_mv3, 1)
            else:
                two = (0, 1) if part == "zeros0" else (2, 3)
                for b in two:
                    last = nc.vector.tensor_scalar(spj[b % 2], xf[:, b, :], 1e-6, None, ALU.is_lt)
                link(last)
                for b in two:
                    last = nc.vector.scalar_tensor_tensor(spj[b % 2], xf[:, b, :], -1e-6, spj[b % 2], ALU.is_gt,
                                                          ALU.mult, accum_out=st[:, b, 5:6])
                link(last)
                if part == "zeros1":
                    link(nc.vector.tensor_scalar(st[:, :, 5], st[:, :, 5], 1.0 / C, None, ALU.mult))

        def group(g, par, front, own, prev, _=1):
            for s in range(STEPS):
                for back, u in unit_at(s, WEIGH + ATT + 1, own, prev):
                    if u % NU == 0:
                        wait(dve, s_pv, GU * (g - back) + u + NU)
                        ov = banks[BO][0:T, 0:NH * VE].rearrange("p (h e) -> p h e", h=NH)
                        link(nc.vector.reciprocal(rden, ov[:, :, DH]))
                        nc.vector.tensor_tensor(att.rearrange("p (h e) -> p h e", h=NH), ov[:, :, 0:DH],
                                                rden.unsqueeze(2).to_broadcast([T, NH, DH]),
                                                ALU.mult).then_inc(s_att, 1)
                if own:
                    wait(dve, s_s, GU * g + s + 1)
                    nc.vector.tensor_reduce(nmx[s % 2], banks[BS[s % 2]][0:T, 0:HU * T].rearrange(
                        "p (h k) -> p h k", h=HU), X, ALU.max, negate=True).then_inc(s_mx, 1)
                for back, u in unit_at(s, TURN, own, prev):
                    if u % 2 == 0:
                        wait(dve, s_ptr, GU * (g - back) + u + 1)
                        wait(dve, s_pv, GU * (g - back) + u - 1)
                        nc.vector.tensor_copy(prt[0].rearrange("p a b -> p (a b)"),
                                              banks[BT[0]][0:T, 0:HU * T]).then_inc(s_pte[0], 1)
                for kind, back, what, j, n in at_step(s, 1, front, own, prev):
                    if what == "V":
                        values(g - back, (par + back) % 2, j, kind, n)
                    elif what == "O":
                        residual(g - back, (par + back) % 2, j, kind, n)
                if front and s == LN1_STATS:
                    ln1_stats(g + 1)
                if prev and s == LN2_APPLY:
                    ln2_apply(g - 1, 1 - par)
                if front and s == LN1_APPLY:
                    ln1_apply(g + 1)
                for part in XF_STATS.get(s, ()) if prev else ():
                    xf_stats(g - 1, part)
                if front and s in ROTATE:
                    rotate(g + 1, ROTATE.index(s))
                if own and not front:
                    if s == SHIFTED[0]:
                        for done, value in ((s_v, 2 * NG), (s_proj, 4 * NG), (s_rope, 4 * NG), (s_xb, NG),
                                            (s_xnt, 2 * NG), (s_kz, 4 * (GB * g + 1)), (s_s, GU * g)):
                            dve.wait_ge(done, value)
                    for h, rows in enumerate((slice(0, 16), slice(16, EARLY))):
                        if s == SHIFTED[h]:
                            shift_logits(dve, link, rows, BM[0], rows.stop // GB)
                    for part in CHOOSE.get(s, ()):
                        choose(dve, link, slice(0, EARLY), part, 1)

        groups(nc.vector.Fori, group, link, DVE_LINKS)
        routing_vector(dve, link)
        experts_vector(dve, link)

    @block.tensor
    def _(pe):
        def item(q, par, loads, kind, what, j, n):
            out = banks[BM[kind]]
            wait(pe, s_mf[kind], FIRST[kind] + len(KINDS[kind]) * q + n)
            if what in "XT":
                rows = xn if what == "X" else xf
                if what == "X":
                    wait(pe, s_xn, q + 1)
                else:
                    wait(pe, s_ln2a, q + 1)
                for c in range(2):
                    for h in range(2):
                        last = nc.tensor.transpose(out[:, (2 * c + h) * T:(2 * c + h + 1) * T],
                                                   rows[:, 2 * j + h, c * 128:(c + 1) * 128], ident[0:T, 0:T])
            elif what in "KQ":
                if what == "K":
                    pe.wait_ge(s_ctx[par], 16 * loads)
                else:
                    wait(pe, s_xnt, 2 * (q + 1))
                w, src = (wk, ctxt[par]) if what == "K" else (wq, xnt)
                for c in range(2):
                    last = nc.tensor.matmul(out[:, 0:NT], w[:, c, j * 128:(j + 1) * 128], src[:, c, :],
                                            start=(c == 0), stop=(c == 1))
            elif what == "A":
                wait(pe, s_att, GB * q + j + 1)
                for c in range(2):
                    last = nc.tensor.transpose(out[:, c * T:(c + 1) * T], att[:, c * 128:(c + 1) * 128],
                                               ident[0:T, 0:T])
            elif what == "O":
                wait(pe, s_attt, GB * q + j + 1)
                for c in range(2):
                    last = nc.tensor.matmul(out[0:T, 0:C], attt[:, c, :], wo[:, c, :],
                                            start=(c == 0), stop=(c == 1))
            elif what == "V":
                pe.wait_ge(s_ctx[par], 16 * loads)
                for h in range(2):
                    for c in range(2):
                        last = nc.tensor.matmul(out[0:T, h * C:(h + 1) * C],
                                                ctxt[par][:, c, (2 * j + h) * T:(2 * j + h + 1) * T], wv[:, c, :],
                                                start=(c == 0), stop=(c == 1))
            elif what == "S":
                wait(pe, s_st, q + 1)
                wait(pe, s_mv3, q + 1)
                for b in range(GB):
                    last = nc.tensor.transpose(out[0:NST, b * T:(b + 1) * T], st[:, b, :], ident[0:T, 0:T])
            elif what == "H":
                wait(pe, s_xft, 3 * (q + 1))
                for c in range(2):
                    nc.tensor.matmul(out[:, 0:NT], r1t[:, c, :], xft[:, c, :], start=(c == 0), stop=False)
                last = nc.tensor.matmul(out[:, 0:NT], r1s, stt, start=False, stop=True)
            last.then_inc(s_m[kind], 1)

        def scores(g, par, s):
            b, k = s // NU, s % NU
            out = banks[BS[s % 2]][0:T, 0:HU * T]
            if s == 0:
                wait(pe, s_rope, 4 * (g + 1))
            if k == 0:
                wait(pe, s_kz, 4 * (GB * g + b + 1))
            nc.tensor.matmul(out, identb, causalb.unsqueeze(1).to_broadcast([T, HU, T]), start=True, stop=False)
            t, h = divmod(HU * k, 8)
            nc.tensor.matmul(out, qt[par][:, t, b * T:(b + 1) * T], kz[b % 2][:, t, h:h + HU, :],
                             start=False, stop=True).then_inc(s_s, 1)

        def turn(q, u):
            wait(pe, s_exp, GU * q + u + 1)
            wait(pe, s_pte[u % 2], GU // 2 * q + u // 2)
            for j in range(HU):
                last = nc.tensor.transpose(banks[BT[u % 2]][0:T, j * T:(j + 1) * T], pr[u % 2][:, j, :],
                                           ident[0:T, 0:T])
            last.then_inc(s_ptr, 1)

        def weigh(q, par, u):
            b, k = u // NU, u % NU
            if u == 0:
                wait(pe, s_v, 2 * (q + 1))
            if k == 0:
                wait(pe, s_att, GB * q + b)
            wait(pe, s_pte[u % 2], GU // 2 * q + u // 2 + 1)
            for j in range(HU):
                h = HU * k + j
                last = nc.tensor.matmul(banks[BO][0:T, h * VE:(h + 1) * VE], prt[u % 2][:, j, :],
                                        vx[par][:, b, h, :], start=True, stop=True)
            last.then_inc(s_pv, 1)

        def group(g, par, front, own, prev, loads=1):
            for s in range(STEPS):
                for back, u in unit_at(s, TURN, own, prev):
                    turn(g - back, u)
                if own:
                    scores(g, par, s)
                for kind, back, what, j, n in at_step(s, 0, front, own, prev):
                    if what == "V" and j == 0 and not own:
                        pe.wait_ge(s_const, 16 * 8)
                        pe.wait_ge(s_tab, 16)
                        pe.wait_ge(s_setup, 4)
                    item(g - back, (par + back) % 2, loads, kind, what, j, n)
                    if not own and not prev:
                        keep_warm(3, ones_like[:, 0:T], ones_like)
                for back, u in unit_at(s, WEIGH, own, prev):
                    weigh(g - back, (par + back) % 2, u)
                if not own and prev and s in IDLE:
                    keep_warm(IDLE[s], identb, causalb.unsqueeze(1).to_broadcast([T, HU, T]))
                for early in LOGITS.get(s, ()) if own and not front else ():
                    if early == 0:
                        pe.wait_ge(s_mf[0], len(FRONT) * NG)
                    if early == GB:
                        pe.wait_ge(s_sub, 1)
                    logits(pe, slice(early * GB, (early + 1) * GB), BM[0], early % GB * GB * NE)

        pe.wait_ge(s_setup, 2)
        ones_like = vx[1].rearrange("p b h e -> p (b h e)")[:, 0:NT // 2].bitcast(BF16)
        keep_warm(WARM, ones_like[:, 0:T], ones_like)
        pe.wait_ge(s_first, 16 * 3)
        pe.sem_inc(s_mf[2], FIRST[2])
        groups(nc.tensor.Fori, group)
        routing_tensor(pe)
        experts_tensor(pe)


def kernel(**inputs):
    import concourse.bacc as bacc
    from concourse.bass_utils import run_bass_kernel_spmd

    a = {n: np.asarray(v) for n, v in inputs.items()}
    halves = lambda w: np.ascontiguousarray(w.T.reshape(2, 128, -1).transpose(1, 0, 2))
    up = a["L0_ffn_w_up"].transpose(0, 2, 1).reshape(NE, 2, 128, 2 * INTER).transpose(0, 2, 1, 3).reshape(NE, 128, -1)
    down = a["L0_ffn_w_down"].transpose(0, 2, 1).reshape(NE, KE, 128, C).transpose(0, 2, 1, 3).reshape(NE, 128, -1)
    aup = a["L0_ffn_a_up"].transpose(0, 2, 1).reshape(NGRP, 2, 128, 2 * AINTER).transpose(0, 2, 1, 3)
    adown = a["L0_ffn_a_down"].transpose(0, 2, 1)
    r1 = a["L0_ffn_r1_w"]
    ctx_t = a["ctx_1024"][:, :T].transpose(2, 0, 1).reshape(2, 128, NG, NT).transpose(2, 1, 0, 3)
    arrays = {
        "x": a["x"].reshape(TOKENS, C),
        "ctx": ctx_t,
        "table": table(),
        "search": search_table(),
        "wq": halves(a["L0_xattn_Wq"]), "wk": halves(a["L0_xattn_Wk"]),
        "wv": halves(a["L0_xattn_Wv"]), "wo": halves(a["L0_xattn_Wo"]),
        "bqk": np.concatenate([a["L0_xattn_bk"].reshape(2, 128), a["L0_xattn_bq"].reshape(2, 128)]).T,
        "bv": a["L0_xattn_bv"], "bo": a["L0_xattn_bo"],
        "gates": np.concatenate([a["g_xattn"], a["g_ffn"]]),
        "r1t": halves(r1[:, :C]), "r1s": r1[:, C:].T, "r1b": a["L0_ffn_r1_b"].reshape(HID, 1),
        "r2t": a["L0_ffn_r2_w"].T,
        "w_experts": np.concatenate([up, down], axis=2),
        "w_adapters": np.concatenate([aup.reshape(NGRP, 128, -1), adown], axis=2),
    }
    arrays = {f"{n}_in": np.ascontiguousarray(v) for n, v in arrays.items()}
    nc = bacc.Bacc("TRN2", target_bir_lowering=False, num_devices=1)
    d = {n[:-3]: nc.dram_tensor(n, v.shape, mybir.dt.from_np(v.dtype), kind="ExternalInput").ap()
         for n, v in arrays.items()}
    d["out"] = nc.dram_tensor("rows_out", (TOKENS + CAP, C), F32, kind="ExternalOutput").ap()
    slots = nc.dram_tensor("slots", (NE * CAP, ROW), F32).ap()
    d["slots_flat"] = slots
    d["slots"] = slots.rearrange("(e s p) c -> e p s c", e=NE, s=2)
    build(nc, d)
    r = run_bass_kernel_spmd(nc, [arrays], core_ids=[0])
    return r.results[0]["rows_out"][:TOKENS].reshape(NB, T, C)
```
